# Optimizing a Trainium2 kernel written in Bass

```python
import numpy as np
import jax
import jax.numpy as jnp

def _softmax(x, axis=-1):
    return jax.nn.softmax(x, axis=axis)

def _gelu(x):
    return jax.nn.gelu(x, approximate=True)

def _silu(x):
    return jax.nn.silu(x)

def _sigmoid(x):
    return jax.nn.sigmoid(x)

def _layernorm(x, axis=-1, eps=1e-05):
    m = jnp.mean(x, axis=axis, keepdims=True)
    v = jnp.var(x, axis=axis, keepdims=True)
    return (x - m) / jnp.sqrt(v + eps)

def _scatter_add(tgt, idx, src, axis=0):
    return tgt.at[idx].add(src)

def _segment_sum(src, seg, n):
    return jax.ops.segment_sum(src, seg, n)
kernel_name = 'mk_decoder_preln_d2_seqx_r4_724344'

def setup_inputs(seed: int=0):
    np.random.seed(seed)
    _w = jnp.asarray

    def _rec_inputs():
        import jax
        import jax.numpy as jnp
        _rk = jax.random.key(seed)
        x = 6.313e-05 + 0.9998 * jax.random.normal(jax.random.fold_in(_rk, 1), (8, 112, 256), jnp.float32)
        _lenS = 112 - jax.random.randint(jax.random.fold_in(_rk, 7), (8,), 0, max(1, 112 // 4) + 1, jnp.int32)
        _lenS2 = 375 - jax.random.randint(jax.random.fold_in(_rk, 8), (8,), 0, max(1, 375 // 4) + 1, jnp.int32)
        _ctx_1024P = jax.random.normal(jax.random.fold_in(_rk, 11), (8, 16, 256), jnp.float32)
        _ctx_1024c = jax.random.dirichlet(jax.random.fold_in(_rk, 511), 0.3 * jnp.ones((16,), jnp.float32), (8, 375))
        _ctx_1024t = jnp.einsum('bsk,bkd->bsd', _ctx_1024c, _ctx_1024P)
        _ctx_1024t = _ctx_1024t * jax.lax.rsqrt(jnp.mean(jnp.square(_ctx_1024t)) + 1e-12) * 0.953939
        ctx_1024 = -0.000214406 + 1.00034 * (_ctx_1024t + 0.3 * jax.random.normal(jax.random.fold_in(_rk, 611), (8, 375, 256), jnp.float32))
        return (x, ctx_1024)
    x, ctx_1024 = _rec_inputs()

    def _L0_attn_setup():
        import jax, jax.numpy as jnp
        import numpy as np
        D = 256
        key = jax.random.key(seed)
        k0, k1, k2, k3 = jax.random.split(key, 4)
        x = jax.random.normal(k0, (4, 512, D), dtype=jnp.float32)
        Wk = jax.random.normal(k1, (D, D), dtype=jnp.float32) * 0.02
        Wq = jax.random.normal(k2, (D, D), dtype=jnp.float32) * 0.02
        Wv = jax.random.normal(k3, (D, D), dtype=jnp.float32) * 0.02
        return {'x': x, 'Wk': Wk, 'Wq': Wq, 'Wv': Wv}
    _L0_attn_all = _L0_attn_setup()
    _L0_attn_in = {k: v for k, v in _L0_attn_all.items() if k in ('Wk', 'Wq', 'Wv')}
    del _L0_attn_all

    def _L0_xattn_setup():
        import jax, jax.numpy as jnp
        import numpy as np
        from jax import lax
        BIG = jnp.float32(1e+30)

        def _pairwise_euclidean(a, b):
            aa = jnp.sum(a * a, axis=-1)[:, None]
            bb = jnp.sum(b * b, axis=-1)[None, :]
            ab = a @ b.T
            return jnp.sqrt(jnp.maximum(aa + bb - 2.0 * ab, 0.0))

        def _dtw_cost(D):
            row0 = jnp.cumsum(D[0])

            def row_step(prev_row, d_row):
                first = d_row[0] + prev_row[0]

                def col_step(left, inp):
                    d_ij, up, diag = inp
                    r = d_ij + jnp.minimum(jnp.minimum(up, left), diag)
                    return (r, r)
                _, rest = lax.scan(col_step, first, (d_row[1:], prev_row[1:], prev_row[:-1]))
                row = jnp.concatenate([first[None], rest])
                return (row, row)
            _, rows = lax.scan(row_step, row0, D[1:])
            return jnp.concatenate([row0[None], rows], axis=0)

        def _backtrack(R, T1, T2):
            L = T1 + T2 - 1

            def step(carry, _):
                i, j, done = carry
                valid = jnp.logical_not(done)
                cd = jnp.where((i > 0) & (j > 0), R[jnp.maximum(i - 1, 0), jnp.maximum(j - 1, 0)], BIG)
                cu = jnp.where(i > 0, R[jnp.maximum(i - 1, 0), j], BIG)
                cl = jnp.where(j > 0, R[i, jnp.maximum(j - 1, 0)], BIG)
                choice = jnp.argmin(jnp.stack([cd, cu, cl]))
                ni = jnp.where(choice <= 1, i - 1, i)
                nj = jnp.where((choice == 0) | (choice == 2), j - 1, j)
                at_origin = (i == 0) & (j == 0)
                ni = jnp.where(at_origin, 0, ni)
                nj = jnp.where(at_origin, 0, nj)
                return ((ni, nj, done | at_origin), (i, j, valid))
            init = (jnp.int32(T1 - 1), jnp.int32(T2 - 1), jnp.bool_(False))
            _, (i_idx, j_idx, valid) = lax.scan(step, init, None, length=L)
            return (i_idx, j_idx, valid)

        def _align_one(small, large):
            T_small, d = small.shape
            T_large = large.shape[0]
            D = _pairwise_euclidean(small, large)
            R = _dtw_cost(D)
            i_idx, j_idx, valid = _backtrack(R, T_small, T_large)
            contrib = small[i_idx] * valid[:, None].astype(small.dtype)
            expanded = jnp.zeros((T_large, d), dtype=small.dtype).at[j_idx].add(contrib)
            return expanded
        key = jax.random.key(seed)
        k1, k2 = jax.random.split(key)
        teacher = jax.random.normal(k1, (16, 100, 256), dtype=jnp.float32)
        student = jax.random.normal(k2, (16, 150, 256), dtype=jnp.float32)
        return {'teacher_features': teacher, 'student_features': student}
    _L0_xattn_all = _L0_xattn_setup()
    _L0_xattn_in = {k: v for k, v in _L0_xattn_all.items() if k in ()}
    del _L0_xattn_all

    def _L0_ffn_setup():
        import jax, jax.numpy as jnp
        import numpy as np
        B, S, H, E, K = (2, 256, 256, 8, 2)
        D = 2 * H
        key = jax.random.key(seed)
        ks = jax.random.split(key, 7)
        x = jax.random.normal(ks[0], (B, S, H), dtype=jnp.float32)
        Wr = jax.random.normal(ks[1], (H, E), dtype=jnp.float32) / np.sqrt(H)
        br = jnp.zeros((E,), dtype=jnp.float32)
        W1 = jax.random.normal(ks[2], (E, H, D), dtype=jnp.float32) / np.sqrt(H)
        b1 = jnp.zeros((E, D), dtype=jnp.float32)
        W2 = jax.random.normal(ks[3], (E, D, H), dtype=jnp.float32) / np.sqrt(D)
        b2 = jnp.zeros((E, H), dtype=jnp.float32)
        return {'x': x, 'Wr': Wr, 'br': br, 'W1': W1, 'b1': b1, 'W2': W2, 'b2': b2}
    _L0_ffn_all = _L0_ffn_setup()
    _L0_ffn_in = {k: v for k, v in _L0_ffn_all.items() if k in ('Wr', 'br', 'W1', 'b1', 'W2', 'b2')}
    del _L0_ffn_all

    def _L1_attn_setup():
        import jax, jax.numpy as jnp
        import numpy as np
        MODEL_DIM = 256
        NUM_HEADS = 16
        D_K = MODEL_DIM // NUM_HEADS
        MAX_SEQ_LEN = 800
        B, T = (2, 512)
        THETA_BASE = 10000.0
        key = jax.random.key(seed)
        ks = jax.random.split(key, 5)
        scale = 1.0 / np.sqrt(MODEL_DIM)
        x = jax.random.normal(ks[0], (B, T, MODEL_DIM), dtype=jnp.float32)
        wq = jax.random.normal(ks[1], (MODEL_DIM, MODEL_DIM), dtype=jnp.float32) * scale
        wk = jax.random.normal(ks[2], (MODEL_DIM, MODEL_DIM), dtype=jnp.float32) * scale
        wv = jax.random.normal(ks[3], (MODEL_DIM, MODEL_DIM), dtype=jnp.float32) * scale
        wo = jax.random.normal(ks[4], (MODEL_DIM, MODEL_DIM), dtype=jnp.float32) * scale
        bq = jnp.zeros((MODEL_DIM,), jnp.float32)
        bk = jnp.zeros((MODEL_DIM,), jnp.float32)
        bv = jnp.zeros((MODEL_DIM,), jnp.float32)
        bo = jnp.zeros((MODEL_DIM,), jnp.float32)
        theta = THETA_BASE ** (jnp.arange(D_K // 2, dtype=jnp.float32) * (-2.0 / D_K))
        ang = jnp.outer(jnp.arange(MAX_SEQ_LEN, dtype=jnp.float32), theta)
        ang = jnp.repeat(ang, 2, axis=-1)
        return {'x': x, 'wq': wq, 'bq': bq, 'wk': wk, 'bk': bk, 'wv': wv, 'bv': bv, 'wo': wo, 'bo': bo, 'cos': jnp.cos(ang), 'sin': jnp.sin(ang)}
    _L1_attn_all = _L1_attn_setup()
    _L1_attn_in = {k: v for k, v in _L1_attn_all.items() if k in ('wq', 'bq', 'wk', 'bk', 'wv', 'bv', 'wo', 'bo', 'cos', 'sin')}
    del _L1_attn_all

    def _L1_xattn_setup():
        import jax, jax.numpy as jnp
        import numpy as np
        B, LQ, LK = (4, 512, 512)
        DQ, DK, DO = (256, 256, 256)
        key = jax.random.key(seed)
        ks = jax.random.split(key, 9)
        s = 0.02
        return {'query_input': jax.random.normal(ks[0], (B, LQ, DQ), jnp.float32), 'key_input': jax.random.normal(ks[1], (B, LK, DK), jnp.float32), 'value_input': jax.random.normal(ks[2], (B, LK, DK), jnp.float32), 'Wq': jax.random.normal(ks[3], (DQ, DO), jnp.float32) * s, 'bq': jax.random.normal(ks[4], (DO,), jnp.float32) * s, 'Wk': jax.random.normal(ks[5], (DK, DO), jnp.float32) * s, 'bk': jax.random.normal(ks[6], (DO,), jnp.float32) * s, 'Wv': jax.random.normal(ks[7], (DK, DO), jnp.float32) * s, 'bv': jax.random.normal(ks[8], (DO,), jnp.float32) * s}
    _L1_xattn_all = _L1_xattn_setup()
    _L1_xattn_in = {k: v for k, v in _L1_xattn_all.items() if k in ('Wq', 'bq', 'Wk', 'bk', 'Wv', 'bv')}
    del _L1_xattn_all

    def _L1_ffn_setup():
        import jax, jax.numpy as jnp
        import numpy as np
        B, S, D = (2, 512, 256)
        E, K, F = (16, 2, 128)
        FS = 256
        key = jax.random.key(seed)
        ks = jax.random.split(key, 8)

        def w(k, shape, fan_in):
            return jax.random.normal(k, shape, jnp.float32) / np.sqrt(fan_in).astype(np.float32)
        return {'x': jax.random.normal(ks[0], (B, S, D), jnp.float32), 'Wr': w(ks[1], (D, E), D), 'Wg': w(ks[2], (E, D, F), D), 'Wu': w(ks[3], (E, D, F), D), 'Wd': w(ks[4], (E, F, D), F), 'Sg': w(ks[5], (D, FS), D), 'Su': w(ks[6], (D, FS), D), 'Sd': w(ks[7], (FS, D), FS)}
    _L1_ffn_all = _L1_ffn_setup()
    _L1_ffn_in = {k: v for k, v in _L1_ffn_all.items() if k in ('Wr', 'Wg', 'Wu', 'Wd', 'Sg', 'Su', 'Sd')}
    del _L1_ffn_all
    return {'x': x, 'ctx_1024': ctx_1024, 'L0_attn_Wk': _L0_attn_in['Wk'], 'L0_attn_Wq': _L0_attn_in['Wq'], 'L0_attn_Wv': _L0_attn_in['Wv'], 'L0_ffn_Wr': _L0_ffn_in['Wr'], 'L0_ffn_br': _L0_ffn_in['br'], 'L0_ffn_W1': _L0_ffn_in['W1'], 'L0_ffn_b1': _L0_ffn_in['b1'], 'L0_ffn_W2': _L0_ffn_in['W2'], 'L0_ffn_b2': _L0_ffn_in['b2'], 'L1_attn_wq': _L1_attn_in['wq'], 'L1_attn_bq': _L1_attn_in['bq'], 'L1_attn_wk': _L1_attn_in['wk'], 'L1_attn_bk': _L1_attn_in['bk'], 'L1_attn_wv': _L1_attn_in['wv'], 'L1_attn_bv': _L1_attn_in['bv'], 'L1_attn_wo': _L1_attn_in['wo'], 'L1_attn_bo': _L1_attn_in['bo'], 'L1_attn_cos': _L1_attn_in['cos'], 'L1_attn_sin': _L1_attn_in['sin'], 'L1_xattn_Wq': _L1_xattn_in['Wq'], 'L1_xattn_bq': _L1_xattn_in['bq'], 'L1_xattn_Wk': _L1_xattn_in['Wk'], 'L1_xattn_bk': _L1_xattn_in['bk'], 'L1_xattn_Wv': _L1_xattn_in['Wv'], 'L1_xattn_bv': _L1_xattn_in['bv'], 'L1_ffn_Wr': _L1_ffn_in['Wr'], 'L1_ffn_Wg': _L1_ffn_in['Wg'], 'L1_ffn_Wu': _L1_ffn_in['Wu'], 'L1_ffn_Wd': _L1_ffn_in['Wd'], 'L1_ffn_Sg': _L1_ffn_in['Sg'], 'L1_ffn_Su': _L1_ffn_in['Su'], 'L1_ffn_Sd': _L1_ffn_in['Sd']}

def reference(x, ctx_1024, L0_attn_Wk, L0_attn_Wq, L0_attn_Wv, L0_ffn_Wr, L0_ffn_br, L0_ffn_W1, L0_ffn_b1, L0_ffn_W2, L0_ffn_b2, L1_attn_wq, L1_attn_bq, L1_attn_wk, L1_attn_bk, L1_attn_wv, L1_attn_bv, L1_attn_wo, L1_attn_bo, L1_attn_cos, L1_attn_sin, L1_xattn_Wq, L1_xattn_bq, L1_xattn_Wk, L1_xattn_bk, L1_xattn_Wv, L1_xattn_bv, L1_ffn_Wr, L1_ffn_Wg, L1_ffn_Wu, L1_ffn_Wd, L1_ffn_Sg, L1_ffn_Su, L1_ffn_Sd):
    import jax
    import jax.numpy as jnp

    def _L0_attn_ref(x, Wk, Wq, Wv):
        import jax, jax.numpy as jnp
        import numpy as np
        D = 256
        K = x @ Wk
        Q = x @ Wq
        V = x @ Wv
        N = Q.shape[-2]
        d = K.shape[-1]
        scores = jnp.einsum('bnd,bmd->bnm', Q, K) / jnp.sqrt(jnp.float32(d))
        causal = jnp.tril(jnp.ones((N, N), dtype=bool))
        scores = jnp.where(causal[None, :, :], scores, -jnp.inf)
        attn = jax.nn.softmax(scores, axis=-1)
        return attn @ V

    def _L0_xattn_ref(teacher_features, student_features):
        import jax, jax.numpy as jnp
        import numpy as np
        from jax import lax
        BIG = jnp.float32(1e+30)

        def _pairwise_euclidean(a, b):
            aa = jnp.sum(a * a, axis=-1)[:, None]
            bb = jnp.sum(b * b, axis=-1)[None, :]
            ab = a @ b.T
            return jnp.sqrt(jnp.maximum(aa + bb - 2.0 * ab, 0.0))

        def _dtw_cost(D):
            row0 = jnp.cumsum(D[0])

            def row_step(prev_row, d_row):
                first = d_row[0] + prev_row[0]

                def col_step(left, inp):
                    d_ij, up, diag = inp
                    r = d_ij + jnp.minimum(jnp.minimum(up, left), diag)
                    return (r, r)
                _, rest = lax.scan(col_step, first, (d_row[1:], prev_row[1:], prev_row[:-1]))
                row = jnp.concatenate([first[None], rest])
                return (row, row)
            _, rows = lax.scan(row_step, row0, D[1:])
            return jnp.concatenate([row0[None], rows], axis=0)

        def _backtrack(R, T1, T2):
            L = T1 + T2 - 1

            def step(carry, _):
                i, j, done = carry
                valid = jnp.logical_not(done)
                cd = jnp.where((i > 0) & (j > 0), R[jnp.maximum(i - 1, 0), jnp.maximum(j - 1, 0)], BIG)
                cu = jnp.where(i > 0, R[jnp.maximum(i - 1, 0), j], BIG)
                cl = jnp.where(j > 0, R[i, jnp.maximum(j - 1, 0)], BIG)
                choice = jnp.argmin(jnp.stack([cd, cu, cl]))
                ni = jnp.where(choice <= 1, i - 1, i)
                nj = jnp.where((choice == 0) | (choice == 2), j - 1, j)
                at_origin = (i == 0) & (j == 0)
                ni = jnp.where(at_origin, 0, ni)
                nj = jnp.where(at_origin, 0, nj)
                return ((ni, nj, done | at_origin), (i, j, valid))
            init = (jnp.int32(T1 - 1), jnp.int32(T2 - 1), jnp.bool_(False))
            _, (i_idx, j_idx, valid) = lax.scan(step, init, None, length=L)
            return (i_idx, j_idx, valid)

        def _align_one(small, large):
            T_small, d = small.shape
            T_large = large.shape[0]
            D = _pairwise_euclidean(small, large)
            R = _dtw_cost(D)
            i_idx, j_idx, valid = _backtrack(R, T_small, T_large)
            contrib = small[i_idx] * valid[:, None].astype(small.dtype)
            expanded = jnp.zeros((T_large, d), dtype=small.dtype).at[j_idx].add(contrib)
            return expanded
        return jax.vmap(_align_one)(teacher_features, student_features)

    def _L0_ffn_ref(x, Wr, br, W1, b1, W2, b2):
        import jax, jax.numpy as jnp
        import numpy as np
        B, S, H, E, K = (2, 256, 256, 8, 2)
        D = 2 * H
        logits = jnp.einsum('bsh,he->bse', x, Wr) + br
        probs = jax.nn.softmax(logits, axis=-1)
        top_p, top_i = jax.lax.top_k(probs, K)
        cw = jnp.sum(jax.nn.one_hot(top_i, E, dtype=x.dtype) * top_p[..., None], axis=-2)
        h = jax.nn.relu(jnp.einsum('bsh,ehd->bsed', x, W1) + b1)
        y = jnp.einsum('bsed,edh->bseh', h, W2) + b2
        out = jnp.einsum('bseh,bse->bsh', y, cw)
        return out

    def _L1_attn_ref(x, wq, bq, wk, bk, wv, bv, wo, bo, cos, sin):
        import jax, jax.numpy as jnp
        import numpy as np
        MODEL_DIM = 256
        NUM_HEADS = 16
        D_K = MODEL_DIM // NUM_HEADS
        MAX_SEQ_LEN = 800
        B, T = (2, 512)
        THETA_BASE = 10000.0
        b, t, dm = x.shape
        h, d = (NUM_HEADS, dm // NUM_HEADS)
        xq = (x @ wq.T + bq).reshape(b, h, t, d)
        xk = (x @ wk.T + bk).reshape(b, h, t, d)
        xv = (x @ wv.T + bv).reshape(b, h, t, d)

        def rot_half(q):
            q2 = q.reshape(b, h, t, d // 2, 2)
            return jnp.stack([-q2[..., 1], q2[..., 0]], axis=-1).reshape(b, h, t, d)
        c = cos[t]
        s = sin[t]
        xq = xq * c + rot_half(xq) * s
        xk = xk * c + rot_half(xk) * s
        scores = jnp.einsum('bhqd,bhkd->bhqk', xq, xk) / np.sqrt(d)
        p = jax.nn.softmax(scores, axis=-1)
        o = jnp.einsum('bhqk,bhkd->bhqd', p, xv)
        o = o.transpose(0, 2, 1, 3).reshape(b, t, dm)
        return o @ wo.T + bo

    def _L1_xattn_ref(query_input, key_input, value_input, Wq, bq, Wk, bk, Wv, bv):
        import jax, jax.numpy as jnp
        import numpy as np
        B, LQ, LK = (4, 512, 512)
        DQ, DK, DO = (256, 256, 256)
        scale = jnp.asarray(DO, query_input.dtype) ** 0.5
        q = query_input @ Wq + bq
        k = key_input @ Wk + bk
        v = value_input @ Wv + bv
        attn = jnp.einsum('bqd,bkd->bqk', q, k) / scale
        attn = jax.nn.softmax(attn, axis=-1)
        return jnp.einsum('bqk,bkd->bqd', attn, v)

    def _L1_ffn_ref(x, Wr, Wg, Wu, Wd, Sg, Su, Sd):
        import jax, jax.numpy as jnp
        import numpy as np
        B, S, D = (2, 512, 256)
        E, K, F = (16, 2, 128)
        FS = 256
        b, s, d = x.shape
        T = b * s
        xf = x.reshape(T, d)
        shared = jax.nn.silu(xf @ Sg) * (xf @ Su) @ Sd
        probs = jax.nn.softmax(xf @ Wr, axis=-1)
        topk_p, topk_i = jax.lax.top_k(probs, K)
        n_exp = Wr.shape[1]
        cw = jnp.zeros((T, n_exp), x.dtype).at[jnp.arange(T)[:, None], topk_i].add(topk_p)

        def step(acc, ew):
            wg, wu, wd, c = ew
            y = jax.nn.silu(xf @ wg) * (xf @ wu) @ wd
            return (acc + y * c[:, None], None)
        routed, _ = jax.lax.scan(step, jnp.zeros_like(xf), (Wg, Wu, Wd, cw.T))
        return (routed + shared).reshape(b, s, d)
    x = x + _L0_attn_ref(_layernorm(x, axis=-1), L0_attn_Wk, L0_attn_Wq, L0_attn_Wv)
    x = x + _L0_xattn_ref(ctx_1024, _layernorm(x, axis=-1))
    x = x + _L0_ffn_ref(_layernorm(x, axis=-1), L0_ffn_Wr, L0_ffn_br, L0_ffn_W1, L0_ffn_b1, L0_ffn_W2, L0_ffn_b2)
    x = x + _L1_attn_ref(_layernorm(x, axis=-1), L1_attn_wq, L1_attn_bq, L1_attn_wk, L1_attn_bk, L1_attn_wv, L1_attn_bv, L1_attn_wo, L1_attn_bo, L1_attn_cos, L1_attn_sin)
    x = x + _L1_xattn_ref(_layernorm(x, axis=-1), ctx_1024, ctx_1024, L1_xattn_Wq, L1_xattn_bq, L1_xattn_Wk, L1_xattn_bk, L1_xattn_Wv, L1_xattn_bv)
    x = x + _L1_ffn_ref(_layernorm(x, axis=-1), L1_ffn_Wr, L1_ffn_Wg, L1_ffn_Wu, L1_ffn_Wd, L1_ffn_Sg, L1_ffn_Su, L1_ffn_Sd)
    return x

_drawn_inputs = setup_inputs


def setup_inputs(seed=0):
    import zlib

    import numpy as np

    out = dict(_drawn_inputs(seed))
    spreads = {'L0_ffn_br': (0.0, 0.561),
     'L0_ffn_b1': (0.0, 0.8),
     'L0_ffn_b2': (0.0, 0.8),
     'L1_attn_bq': (0.0, 0.8),
     'L1_attn_bk': (0.0, 0.8),
     'L1_attn_bv': (0.0, 0.8),
     'L1_attn_bo': (0.0, 0.513)}
    factors = {'L1_attn_cos': 3.298,
     'L1_attn_sin': 2.992,
     'L1_xattn_Wq': 8.0,
     'L1_xattn_bq': 64.0,
     'L1_xattn_Wk': 8.0,
     'L1_xattn_bk': 64.0,
     'L1_xattn_bv': 8.0}
    for name, (base, spread) in spreads.items():
        noise = np.random.default_rng([zlib.crc32(name.encode()), seed]).standard_normal(out[name].shape)
        drawn = base * np.exp(spread * noise) if base else spread * noise
        out[name] = jnp.asarray(drawn.astype(out[name].dtype))
    for name, factor in factors.items():
        out[name] = (out[name] * factor).astype(out[name].dtype)
    return out
```

```python
from contextlib import ExitStack

import concourse.bass as bass
from concourse import mybir

F32 = mybir.dt.float32
ALU = mybir.AluOpType
ACT = mybir.ActivationFunctionType
AX_X = mybir.AxisListType.X

BIG = 1e30
BANKS = 8
EPS = 1e-5
TINY = 1e-14


class Slot:

    def __init__(self, n, reader, count, before):
        self.n, self.bank, self.reader, self.count, self.before = n, n % BANKS, reader, count, before


class BankRing:

    def __init__(self):
        self.slots = []
        self.counts = {}

    def take(self, *readers):
        out = []
        for reader in readers:
            n = len(self.slots)
            self.counts[reader] = self.counts.get(reader, 0) + 1
            before = self.slots[n - BANKS] if n >= BANKS else None
            self.slots.append(Slot(n, reader, self.counts[reader], before))
            out.append(self.slots[-1])
        return out


def view(t, offset, dims, parts=None):
    x = t[:] if parts is None else t[parts[0]:parts[1]]
    return bass.AP(x.tensor, x.offset + offset, [x.ap[0]] + dims)


def rows_of(a, parts):
    n = a.shape[-1]
    return bass.AP(a.tensor, a.offset, [[0, parts], [1, n]])


def decoder_kernel(nc, A, out):
    B, T, D = A["x"].shape
    S = A["ctx_1024"].shape[1]
    KD = D // 128
    CH = 3
    CR = S // CH
    HB = B // 2
    HT = HB * T
    E0, F0 = A["L0_ffn_b1"].shape
    M0 = F0 // 128
    E1, _, F1 = A["L1_ffn_Wg"].shape
    NX = E1 + A["L1_ffn_Sg"].shape[1] // F1
    G = 4
    RC = -(-S // G)
    KC = 4
    STEPS = T // KC + G - 1
    NSLOT = STEPS * KC + 1
    SC = 8
    SEG = T // SC
    NH, HD = 16, D // 16
    HV = HD + 1
    TC = 4 * CR
    NQ = B * CH // 4
    assert S == CH * CR and SEG * B == T and T * HD == NH * T and 2 * HB == B

    with ExitStack() as ctx:
        def sb(name, shape):
            return ctx.enter_context(nc.sbuf_tensor(name, shape, F32))

        def sem(name):
            return ctx.enter_context(nc.semaphore(name))

        ps = ctx.enter_context(nc.psum_tensor("ps", [128, BANKS, 512], F32))

        X = sb("X", [T, B, D])
        N_r = sb("N_r", [128, B * D])
        NT = sb("NT", [128, KD, B * T])
        ctxT_r = sb("ctxT_r", [128, 3 * 2048])
        KcT = sb("KcT", [128, KD, B * S])
        Vc_r = sb("Vc_r", [128, B * CH * D])
        BIGN = 26930
        big = sb("big", [128, BIGN])
        ident = sb("ident", [128, 128])
        iota = sb("iota", [128, S + 1])
        ones = sb("ones", [128, T])
        stats = sb("stats", [T, B, 6])
        mv = sb("mv", [T, B, 2])
        veps = sb("veps", [T, B])
        mhalf = sb("mhalf", [T, B])
        rstd = sb("rstd", [T, B])
        mx = sb("mx", [T, 2, B])
        rs = sb("rs", [T, 2, B])
        bb = sb("bb", [T, B])
        NB = E0 * M0 + 2 * KD
        brow = KcT[0:NB, 0, 0:128]
        bcol = sb("bcol", [128, NB])
        b1c = bcol[:, 0:E0 * M0].rearrange("p (e m) -> p e m", e=E0)
        bqk = bcol[:, E0 * M0:NB].rearrange("p (w k) -> p w k", w=2)
        brb = sb("brb", [T, E0])
        cw = sb("cw", [T, B, E1])
        einb = sb("einb", [B, SEG])
        esel = sb("esel", [B, T])
        ecol = sb("ecol", [T, SC])

        ctxT = ctxT_r[:, 0:KD * B * S].rearrange("p (k n) -> p k n", k=KD)
        N = N_r[0:T, :].rearrange("p (b d) -> p b d", b=B)
        Vc = Vc_r[0:CR, :].rearrange("p (b c d) -> p b c d", b=B, c=CH)

        def place(start, *sizes):
            offs, o = [], start
            for n in sizes:
                offs.append(o)
                o += n
            assert o <= BIGN, (start, sizes, o)
            return offs

        NS = SC * S
        RB = S + 2
        o_dsk, o_rs, o_rb = place(0, STEPS * KC * RC, NSLOT * (RC + 1), (SC + 1) * RB)
        ctxN0 = big[0:CR, 0:B * CH * D].rearrange("p (j d) -> p j d", d=D)
        o_w0, o_qk0, o_v0, o_p0, o_pt0, o_cm, o_sq = place(
            o_rs, 3 * KD * D, 2 * KD * B * T, B * D, B * T, B * T, T, 2 * KD * TC)
        w0 = big[:, o_w0:o_qk0].rearrange("p (w k n) -> p w k n", w=3, k=KD)
        qkT0 = big[:, o_qk0:o_v0].rearrange("p (w k n) -> p w k n", w=2, k=KD)
        V0 = big[0:T, o_v0:o_p0].rearrange("p (b d) -> p b d", b=B)
        P0 = big[0:T, o_p0:o_pt0].rearrange("p (b n) -> p b n", b=B)
        PT0 = big[0:T, o_pt0:o_cm].rearrange("p (b n) -> p b n", b=B)
        cmask = big[0:T, o_cm:o_cm + T]
        csq = big[:, o_sq:o_sq + 2 * KD * TC].rearrange("p (a k n) -> p a k n", a=2, k=KD)
        assert o_sq + 2 * KD * TC <= o_rb
        Dd = Vc_r[0:T, 0:B * S].rearrange("p (b n) -> p b n", b=B)
        aaB = Vc_r[0:T, B * S:2 * B * S].rearrange("p (b n) -> p b n", b=B)
        inv = big[0:T, o_rb:o_rb + B * S].rearrange("p (b n) -> p b n", b=B)
        Dsk = big[0:G * B, o_dsk:o_rs]
        RS = big[0:G * B, o_rs:o_rb].rearrange("p (q i) -> p q i", i=RC + 1)
        mtmp = sb("mtmp", [G * B, RC])
        Rb = big[0:T, o_rb:o_rb + (SC + 1) * RB].rearrange("p (c i) -> p c i", c=SC + 1)
        ctxN = big[0:CR, 0:B * CH * D].rearrange("p (b c d) -> p b c d", b=B, c=CH)
        o_m1, o_cc, o_tt = place(B * CH * D, NS, 2 * (S + 1), 2 * S)
        assert o_tt + 2 * S <= o_rs
        o_dl, o_u, o_pts = place(o_rs, 2 * NS, NS + 1, CH * B * T)
        assert o_pts + CH * B * T <= o_rb
        m1 = big[0:T, o_m1:o_m1 + NS]
        dl = big[0:T, o_dl:o_dl + 2 * NS].rearrange("p (a n) -> p a n", a=2)
        U = big[0:T, o_u:o_u + NS + 1]
        Ex = m1
        Cc = big[0:T, o_cc:o_cc + 2 * (S + 1)].rearrange("p (a i) -> p a i", a=2)
        Tt = big[0:T, o_tt:o_tt + 2 * S].rearrange("p (a i) -> p a i", a=2)
        Cw = big[0:B, o_dl:o_dl + SEG * S].rearrange("p (s i) -> p s i", s=SEG)
        OH = big[0:T, o_rb:o_rb + NS]
        Pm = big[0:T, o_dl:o_dl + NS]
        PTs = big[0:CR, o_pts:o_pts + CH * B * T].rearrange("p (h b s c) -> p h b s c", h=CH, b=B, s=SEG)
        junk = sb("junk", [T, S])
        junk2 = junk[:, 0:D]
        wkv = N_r[:, 0:2 * KD * D].rearrange("p (w k n) -> p w k n", w=2, k=KD)
        NW0 = 3
        QW = 3 * D + HD
        W1s = ctxT_r[:, 0:NW0 * 1024].rearrange("p (r k f) -> p r k f", r=NW0, k=KD)
        W2s = ctxT_r[:, NW0 * 1024:NW0 * 2048].rearrange("p (r m d) -> p r m d", r=NW0, m=M0)
        (o_h0, o_qkv, o_vt, o_vh, o_wn, o_wt, o_bq, o_cs, o_b2, o_ps, o_pp, o_pq) = place(
            0, 2 * M0 * B * T, B * QW, 2 * NH * T, B * NH * HV, 2 * KD * D, 4 * KD * D,
            4 * D, 2 * HD, D, 2 * HT, 2 * HT, 2 * HT)
        hT = big[:, o_h0:o_qkv].rearrange("p (r m n) -> p r m n", r=2, m=M0)
        QKT = big[:, o_h0:o_h0 + 2 * 2 * NH * T].rearrange("p (w g n) -> p w g n", w=2, g=2)
        QKV = big[0:T, o_qkv:o_qkv + 3 * B * D].rearrange("p (w g c b d) -> p w g c b d", w=3, g=2, c=NH // 2, b=HB)
        VT = big[:, o_vt:o_vh].rearrange("p (g n) -> p g n", g=2)
        Vh = big[0:T, o_vh:o_wn].rearrange("p (b h d) -> p b h d", b=B, h=NH)
        wn = big[:, o_wn:o_wt].rearrange("p (w r n) -> p w r n", w=2, r=KD)
        wT = big[:, o_wt:o_bq].rearrange("p (k w n) -> p k w n", k=KD, w=4)
        bqkv = big[:, o_bq:o_cs].rearrange("p (w n) -> p w n", w=4)
        cs = big[:, o_cs:o_b2].rearrange("p (w n) -> p w n", w=2)
        b2s = big[0:E0, o_b2:o_ps]
        cwT = big[0:E0, o_pq:o_pq + B * T]
        wr0 = sb("wr0", [128, KD, E0])
        wr1 = sb("wr1", [128, KD, E1])
        Sx = big[0:T, o_ps:o_pp].rearrange("p (r n) -> p r n", r=2)
        Px = big[0:T, o_pp:o_pq].rearrange("p (r n) -> p r n", r=2)
        PxT = big[0:T, o_pq:o_pq + 2 * HT].rearrange("p (r n) -> p r n", r=2)
        rope = big[:, o_ps:o_ps + 4 * D].rearrange("p (a n) -> p a n", a=2)
        rk = sb("rk", [T, B * E1])
        gl = sb("gl", [T, B, E1])
        gp = sb("gp", [T, B, E1])
        hm = sb("hm", [T, 3, 8])
        o_ra, o_re = place(o_qkv, B * E1 * E1, B * E1 * E1)
        tri = junk[:, 0:E1 * E1].rearrange("p (e o) -> p e o", e=E1)
        boB = bqkv[0:T, 3, :]
        bvB = big[0:T, o_b2:o_b2 + D]
        o_qx, o_sx, o_px, o_ptx, o_wq = place(o_qkv, KD * B * T, 2 * S, 2 * S, 2 * CH * T, KD * D)
        assert o_wq + KD * D <= o_vt
        qxT = big[:, o_qx:o_sx].rearrange("p (k n) -> p k n", k=KD)
        Pc = big[0:T, o_px:o_px + 2 * S].rearrange("p (r n) -> p r n", r=2)
        PcT = big[0:CR, o_ptx:o_ptx + 2 * CH * T].rearrange("p (r h n) -> p r h n", r=2, h=CH)
        wq1 = big[:, o_wq:o_wq + KD * D].rearrange("p (k n) -> p k n", k=KD)
        NF = 8
        WXA = ctxT_r[:, :].rearrange("p (e n) -> p e n", e=NF)
        o_wx, o_sg, o_hx = place(o_vt, (NX - NF) * 768, 2 * B * T, 2 * B * T)
        WXB = big[:, o_wx:o_sg].rearrange("p (e n) -> p e n", e=NX - NF)
        sg = big[:, o_sg:o_hx].rearrange("p (r n) -> p r n", r=2)
        hx = big[:, o_hx:o_hx + 2 * B * T].rearrange("p (r n) -> p r n", r=2)

        def wx(e):
            w = WXA[:, e, :] if e < NF else WXB[:, e - NF, :]
            return (w[:, 0:256].rearrange("p (k f) -> p k f", k=KD),
                    w[:, 256:512].rearrange("p (k f) -> p k f", k=KD), w[:, 512:768])

        ring = BankRing()
        act, dve = "act", "dve"
        r_ctx = ring.take(*[act] * (KD * NQ))
        (r_bias,) = ring.take(act)
        ln_slots = {}
        ln_slots[0] = ring.take(*[act] * 4)
        r_qk0 = ring.take(*[act] * 8)
        r_v0 = ring.take(*[act] * 4)
        r_s0 = ring.take(dve, dve)
        r_aa = ring.take(*[act] * NQ)
        r_pt0 = ring.take(dve, dve)
        r_pv0 = ring.take(*[dve] * 4)
        ln_slots[1] = ring.take(*[act] * 4)
        r_dist = ring.take(*[dve] * B)
        r_kc = ring.take(*[act] * (KD * NQ))
        r_vc = ring.take(*[act] * (B * CH // 2))
        r_e = ring.take(dve)
        r_ptm = ring.take(*[act, dve] * 3)
        r_exp = ring.take(*[dve] * 4)
        ln_slots[2] = ring.take(*[act] * 4)
        r_g0 = ring.take(dve)
        r_up0 = {}
        r_dn0 = {}
        r_up0[0] = ring.take(*[act] * (2 * M0))
        r_cwt = ring.take(act, act)
        r_b2 = ring.take(*[dve] * 4)
        r_wt = ring.take(*[act] * 4)
        for e in range(1, E0 + 1):
            if e < E0:
                r_up0[e] = ring.take(*[act] * (2 * M0))
            r_dn0[e - 1] = ring.take(*[dve] * 4)
        ln_slots[3] = ring.take(*[act] * 4)
        r_qkv = ring.take(*[dve] * (2 * B))
        r_hT = ring.take(*[act, dve] * 12)
        r_vh = ring.take(*[act] * 8)
        NG = 2 * 4 * 4
        r_s1, r_pt1, r_o1 = {}, {}, {}
        for n in range(NG + 2):
            if n < NG:
                (r_s1[n],) = ring.take(dve)
            if 1 <= n <= NG:
                (r_pt1[n - 1],) = ring.take(act)
            if n >= 2:
                (r_o1[n - 2],) = ring.take(dve)
        r_oT = ring.take(*[act] * 4)
        r_wo = ring.take(*[dve] * 4)
        ln_slots[4] = ring.take(*[act] * 4)
        r_qx = ring.take(*[act] * 4)
        r_sc, r_ptc, r_oc = {}, {}, {}
        for n in range(B + 2):
            if n < B:
                (r_sc[n],) = ring.take(act)
            if 1 <= n <= B:
                (r_ptc[n - 1],) = ring.take(act)
            if n >= 2:
                (r_oc[n - 2],) = ring.take(dve)
        ln_slots[5] = ring.take(*[act] * 4)
        r_g1 = ring.take(dve)
        r_up1, r_dn1 = {}, {}
        for e in range(NX + 1):
            if e < NX:
                r_up1[e] = ring.take(act, dve, act, dve)
            if e:
                r_dn1[e - 1] = ring.take(*[dve] * 4)

        full = sem("banks_filled")
        free = {act: sem("banks_emptied_by_act"), dve: sem("banks_emptied_by_dve")}
        names = ("ident_ready", "consts_ready", "x_loaded0", "x_loaded1", "w0_loaded", "aux_loaded",
                 "stats_ready", "rstd_ready", "norm_ready", "p0_exp", "s0_ready",
                 "bb_ready", "csq_ready", "dsk_clear", "costs_clear", "ln_arg", "inv_ready", "dist_ready",
                 "dist_moved0", "dist_moved1", "dist_moved2", "dist_moved3", "wkv_loaded", "wkv_b_loaded",
                 "dtw_step", "costs_moved", "ctx_reloaded", "choices_ready", "exits_ready",
                 "compose_done", "cw_moved", "esel_ready", "path_ready", "logits_exp", "logits_ready",
                 "gates_ready", "attn_w_loaded", "wn_loaded0", "wn_loaded1", "wn_used", "heads_exp",
                 "heads_shifted", "wo_loaded", "ffn_aux_loaded", "rope_ready", "tri_ready", "bias_loaded", "bias_added", "router_loaded", "out_stored1",
                 "vh_ones", "wq1_loaded", "pc_shift", "pc_exp", "silu_ready", "hx_ready",
                 "wxa_loaded", "wxb_loaded", "attn1_done", "out_stored", "x_final", "mask_ready",
                 "edge_ready", "fw", "dve_link", "act_link", "pool_link", "ucol_ready", "shared_one")
        s = {name: sem(name) for name in names}
        ctx_loaded = [sem(f"ctx_loaded{i}") for i in range(4)]
        w0x_loaded = [sem(f"expert_w_loaded{i}") for i in range(NW0)]

        block = ctx.enter_context(nc.Block())

        def halves():
            for h in range(2):
                yield h, range(h * HB, h * HB + HB)

        def x_cols(h):
            return slice(h * HT, (h + 1) * HT)

        def tok(b):
            return slice(b * T, (b + 1) * T)

        def step_of(seg, g):
            return 2 * seg + 1 + g

        def turned(i):
            w, g, cq = i // 8, (i // 4) % 2, i % 4
            tile = VT[:, g] if w == 2 else QKT[:, w, g]
            return tile.rearrange("p (t c) -> p c t", c=NH)[:, 4 * cq:4 * cq + 4, :]

        @block.sync
        def _(sp):
            x_d = A["x"].rearrange("b t d -> t b d")
            sp.dma_start(X[:, 0:HB, :], x_d[:, 0:HB, :]).then_inc(s["x_loaded0"], 16)
            sp.dma_start(X[:, HB:B, :], x_d[:, HB:B, :]).then_inc(s["x_loaded1"], 16)
            c_d = A["ctx_1024"].rearrange("b (c p) d -> p b c d", c=CH)
            for i in range(4):
                sp.dma_start(ctxN0[:, 6 * i:6 * i + 6, :].rearrange("p (b c) d -> p b c d", c=CH),
                             c_d[:, 2 * i:2 * i + 2]).then_inc(ctx_loaded[i], 16)
            sp.wait_ge(s["dsk_clear"], 1)
            for h, bs in halves():
                sp.wait_ge(s["dist_ready"], h + 1)
                for b in bs:
                    for g in range(G):
                        n = min(RC, S - g * RC)
                        dst = view(Dsk, g * KC * RC, [[RC, T], [1, n]], (g * B + b, g * B + b + 1))
                        src = Dd[:, b, g * RC:g * RC + n]
                        src = bass.AP(src.tensor, src.offset, [src.ap[0], [1, n]])
                        sp.dma_start(dst, src).then_inc(s[f"dist_moved{h * 2}"], 16)
            sp.wait_ge(s["edge_ready"], 1)
            for seg in range(SEG):
                for g in range(G):
                    n = min(RC, S - g * RC)
                    sp.wait_ge(s["dtw_step"], min(step_of(seg, g) + 1, STEPS))
                    q = seg * SC + g * KC
                    sp.dma_start(Rb[seg * B:(seg + 1) * B, :, 1 + g * RC:1 + g * RC + n],
                                 RS[g * B:(g + 1) * B, q:q + SC + 1, 1:1 + n]).then_inc(s["costs_moved"], 16)
            sp.wait_ge(s["dtw_step"], STEPS)
            sp.dma_start(ctxN, c_d).then_inc(s["ctx_reloaded"], 16)
            sp.wait_ge(s["compose_done"], 1)
            sp.wait_ge(s["exits_ready"], 1)
            for seg in range(SEG - 1, 0, -1):
                sp.dma_start(Cw[:, seg, :], Cc[seg * B:(seg + 1) * B, (SC - 1) % 2, 1:S + 1])\
                    .then_inc(s["cw_moved"], 16)
            sp.wait_ge(free[dve], r_exp[-1].count)
            sp.dma_start(b2s, A["L0_ffn_b2"]).then_inc(s["ffn_aux_loaded"], 16)
            sp.dma_start(cs[:, 0, :], rows_of(A["L1_attn_cos"][T:T + 1, :], 128)).then_inc(s["attn_w_loaded"], 16)
            sp.dma_start(cs[:, 1, :], rows_of(A["L1_attn_sin"][T:T + 1, :], 128)).then_inc(s["attn_w_loaded"], 16)
            for w, name in enumerate(("bq", "bk", "bv", "bo")):
                sp.dma_start(bqkv[:, w, :], rows_of(A["L1_attn_" + name], 128)).then_inc(s["attn_w_loaded"], 16)
            for i, pair in enumerate((("wq", "wk"), ("wv", "wo"))):
                if i:
                    sp.wait_ge(s["wn_used"], 1)
                for w, name in enumerate(pair):
                    sp.dma_start(wn[:, w], A["L1_attn_" + name].rearrange("(r p) n -> p r n", p=128))\
                        .then_inc(s[f"wn_loaded{i}"], 16)
            sp.wait_ge(full, r_b2[-1].n + 1)
            sp.dma_start(bvB, rows_of(A["L1_xattn_bv"], T)).then_inc(s["bias_loaded"], 16)
            def load_expert(e, name):
                g, u, d = wx(e)
                if e < E1:
                    srcs = (A["L1_ffn_Wg"][e], A["L1_ffn_Wu"][e], A["L1_ffn_Wd"][e])
                else:
                    f = slice((e - E1) * F1, (e - E1 + 1) * F1)
                    srcs = (A["L1_ffn_Sg"][:, f], A["L1_ffn_Su"][:, f], A["L1_ffn_Sd"][f, :])
                sp.dma_start(g, srcs[0].rearrange("(k p) f -> p k f", p=128)).then_inc(s[name], 16)
                sp.dma_start(u, srcs[1].rearrange("(k p) f -> p k f", p=128)).then_inc(s[name], 16)
                sp.dma_start(d, srcs[2]).then_inc(s[name], 16)
            sp.wait_ge(full, r_dn0[E0 - 1][-1].n + 1)
            for e in range(NF):
                load_expert(e, "wxa_loaded")
            sp.wait_ge(full, r_vh[-1].n + 1)
            sp.dma_start(wq1, A["L1_xattn_Wq"].rearrange("(k p) n -> p k n", p=128)).then_inc(s["wq1_loaded"], 16)
            sp.wait_ge(free[dve], r_wo[-1].count)
            for e in range(NF, NX):
                load_expert(e, "wxb_loaded")
            for b in range(B):
                if b % 2 == 0:
                    sp.wait_ge(free[dve], r_dn1[NX - 1][b // 2].count)
                sp.dma_start(out[b], X[:, b, :]).then_inc(s["out_stored"], 16)
            sp.wait_ge(s["out_stored"], 16 * B)

        @block.gpsimd
        def _(pool):
            link_n = [0]

            def link(ins):
                link_n[0] += 1
                ins.then_inc(s["pool_link"], 1)
                pool.wait_ge(s["pool_link"], link_n[0])

            link(nc.gpsimd.memset(ident[:], 0.0))
            nc.gpsimd.affine_select(out=ident[:], in_=ident[:], compare_op=ALU.not_equal, fill=1.0, base=0,
                                    pattern=[[-1, 128]], channel_multiplier=1).then_inc(s["ident_ready"], 1)
            nc.gpsimd.memset(ones[:], 1.0).then_inc(s["consts_ready"], 1)
            nc.gpsimd.memset(mhalf[:], -0.5).then_inc(s["consts_ready"], 1)
            link(nc.gpsimd.memset(cmask, 0.0))
            nc.gpsimd.affine_select(out=cmask, in_=cmask, compare_op=ALU.is_ge, fill=-BIG, base=0,
                                    pattern=[[-1, T]], channel_multiplier=1).then_inc(s["mask_ready"], 1)
            nc.gpsimd.iota(iota[:], pattern=[[1, S + 1]], base=-1, channel_multiplier=0,
                           allow_small_or_imprecise_dtypes=True).then_inc(s["consts_ready"], 1)
            link(nc.gpsimd.memset(esel[:], 1.0))
            nc.gpsimd.affine_select(out=esel[:].rearrange("p (s b) -> p s b", b=B),
                                    in_=esel[:].rearrange("p (s b) -> p s b", b=B),
                                    compare_op=ALU.is_equal, fill=0.0, base=0,
                                    pattern=[[0, SEG], [-1, B]], channel_multiplier=1).then_inc(s["consts_ready"], 1)
            for w, name in enumerate(("Wq", "Wk", "Wv")):
                pool.dma_start(w0[:, w], A["L0_attn_" + name].rearrange("(k p) n -> p k n", p=128))\
                    .then_inc(s["w0_loaded"], 16)
            pool.dma_start(brow[0:E0 * M0, :], A["L0_ffn_b1"].rearrange("e (m p) -> (e m) p", p=128))\
                .then_inc(s["aux_loaded"], 16)
            for w, name in enumerate(("bq", "bk")):
                lo = E0 * M0 + w * KD
                pool.dma_start(brow[lo:lo + KD, :], A["L1_xattn_" + name].rearrange("(k p) -> k p", p=128))\
                    .then_inc(s["aux_loaded"], 16)
            pool.dma_start(brb[:], rows_of(A["L0_ffn_br"], T)).then_inc(s["aux_loaded"], 16)
            pool.dma_start(wr0[:], A["L0_ffn_Wr"].rearrange("(k p) e -> p k e", p=128)).then_inc(s["router_loaded"], 16)
            pool.dma_start(wr1[:], A["L1_ffn_Wr"].rearrange("(k p) e -> p k e", p=128)).then_inc(s["router_loaded"], 16)

            def ln_root(n):
                for h in range(2):
                    cols = slice(h * HB, h * HB + HB)
                    pool.wait_ge(s["stats_ready"], 2 * n + h + 1)
                    link(nc.gpsimd.tensor_scalar(veps[:, cols], mv[:, cols, 1], EPS, None, ALU.add))
                    nc.gpsimd.tensor_tensor(rstd[:, cols], veps[:, cols], mhalf[:, cols], ALU.pow)\
                        .then_inc(s["rstd_ready"], 1)

            ln_root(0)
            pool.wait_ge(full, r_ctx[-1].n + 1)
            nc.gpsimd.memset(Dsk, BIG).then_inc(s["dsk_clear"], 1)
            ln_root(1)
            pool.wait_ge(full, ln_slots[1][-1].n + 1)
            pool.wait_ge(s["bb_ready"], 1)
            for w, name in enumerate(("Wk", "Wv")):
                pool.dma_start(wkv[:, w], A["L1_xattn_" + name].rearrange("(k p) n -> p k n", p=128))\
                    .then_inc(s["wkv_loaded"], 16)
            pool.wait_ge(free[dve], r_pv0[-1].count)
            pool.wait_ge(full, r_aa[-1].n + 1)
            link(nc.gpsimd.memset(big[0:G * B, o_rs:o_rb], BIG))
            nc.gpsimd.memset(RS[0:B, 0, 0:1], 0.0).then_inc(s["costs_clear"], 1)
            pool.wait_ge(s["dist_ready"], 2)
            nc.gpsimd.memset(Rb[:, :, 0:1], BIG).then_inc(s["edge_ready"], 1)
            def load_w0(e):
                r = e % NW0
                if e == 0:
                    pool.wait_ge(full, r_vc[-1].n + 1)
                if e >= NW0:
                    pool.wait_ge(full, r_dn0[e - NW0][-1].n + 1)
                pool.dma_start(W1s[:, r], A["L0_ffn_W1"][e].rearrange("(k p) f -> p k f", p=128))\
                    .then_inc(w0x_loaded[r], 16)
                pool.dma_start(W2s[:, r], A["L0_ffn_W2"][e].rearrange("(m p) d -> p m d", p=128))\
                    .then_inc(w0x_loaded[r], 16)
            for e in range(NW0):
                load_w0(e)
            pool.wait_ge(s["choices_ready"], 2)
            link(nc.gpsimd.tensor_tensor(Ex, dl[:, 0, :], dl[:, 1, :], ALU.add))
            link(nc.gpsimd.tensor_scalar(U[:, 0:NS], Ex, -1.0, 1.0, ALU.mult, ALU.add))
            link(nc.gpsimd.memset(U[:, NS:NS + 1], 0.0))
            link(nc.gpsimd.tensor_tensor(Ex.rearrange("p (c i) -> p c i", c=SC), Ex.rearrange("p (c i) -> p c i", c=SC),
                                         view(iota, 1, [[0, SC], [1, S]], (0, T)), ALU.mult))
            nc.gpsimd.tensor_tensor(Ex, Ex, dl[:, 0, :], ALU.subtract).then_inc(s["exits_ready"], 1)
            pool.wait_ge(s["path_ready"], 1)
            link(nc.gpsimd.memset(tri, 1.0))
            nc.gpsimd.affine_select(out=tri, in_=tri, compare_op=ALU.is_gt, fill=0.0, base=0,
                                    pattern=[[1, E1], [-1, E1]], channel_multiplier=0).then_inc(s["tri_ready"], 1)
            ln_root(2)
            for e in range(NW0, E0):
                load_w0(e)
            pool.wait_ge(free[dve], r_exp[-1].count)
            nc.gpsimd.memset(Vh[:, :, :, HD:HV], 1.0).then_inc(s["vh_ones"], 1)
            nc.gpsimd.memset(big[0:T, o_qkv + 3 * B * D:o_vt], 0.0).then_inc(s["vh_ones"], 1)

            def add_bias(n, tile, offset):
                pool.wait_ge(s["norm_ready"], (n + 1) * B)
                nc.gpsimd.tensor_tensor(X[:, :, :], X[:, :, :], view(tile, offset, [[0, B], [1, D]], (0, T)), ALU.add)\
                    .then_inc(s["bias_added"], 1)

            ln_root(3)
            pool.wait_ge(s["attn_w_loaded"], 96)
            add_bias(3, big, o_bq + 3 * D)
            ln_root(4)
            pool.wait_ge(s["bias_loaded"], 16)
            add_bias(4, big, o_b2)
            ln_root(5)

        @block.scalar
        def _(sc):
            link_n = [0]

            def link(ins):
                link_n[0] += 1
                ins.then_inc(s["act_link"], 1)
                sc.wait_ge(s["act_link"], link_n[0])

            def copy(slot, dst, src, func=ACT.Copy, **kw):
                sc.wait_ge(full, slot.n + 1)
                return nc.scalar.activation(dst, src, func, **kw).then_inc(free[act], 1)

            def bank(slot):
                return ps[:, slot.bank, :]

            def ln_turned(n):
                for i, slot in enumerate(ln_slots[n]):
                    h, k = i // KD, i % KD
                    copy(slot, NT[:, k, x_cols(h)], bank(slot)[:, 0:HT])

            for i, slot in enumerate(r_ctx):
                q, k = i // KD, i % KD
                copy(slot, ctxT[:, k, q * TC:(q + 1) * TC], bank(slot)[:, 0:TC])
            copy(r_bias, bcol[:, :], bank(r_bias)[:, 0:NB])
            ln_turned(0)
            i = 0
            for w in range(2):
                for m in range(KD):
                    for h in range(2):
                        copy(r_qk0[i], qkT0[:, w, m, x_cols(h)], bank(r_qk0[i])[:, 0:HT])
                        i += 1
            for i, slot in enumerate(r_v0):
                copy(slot, V0[:, 2 * i:2 * i + 2, :], bank(slot)[0:T, :].rearrange("p (b d) -> p b d", b=2))

            def squares(q):
                if q >= 2:
                    sc.wait_ge(full, r_aa[q - 2].n + 1)
                if q == 0:
                    sc.wait_ge(free[act], r_ctx[-1].count)
                nc.scalar.activation(csq[:, q % 2], ctxT[:, :, q * TC:(q + 1) * TC], ACT.Square)\
                    .then_inc(s["csq_ready"], 1)

            def norms(q):
                lo = q * TC
                copy(r_aa[q], Vc_r[0:T, B * S + lo:B * S + lo + TC], bank(r_aa[q])[0:T, 0:TC])
            squares(0)
            squares(1)
            for b in range(B):
                if b % HB == 0:
                    sc.wait_ge(s["s0_ready"], b // HB + 1)
                nc.scalar.activation(P0[:, b, :], P0[:, b, :], ACT.Exp, bias=mx[:, 1, b:b + 1],
                                     accum_out=rs[:, 0, b:b + 1]).then_inc(s["p0_exp"], 1)
            for q in range(NQ):
                norms(q)
                if q + 2 < NQ:
                    squares(q + 2)
            for b in range(B):
                sc.wait_ge(s["norm_ready"], B + b + 1)
                link(nc.scalar.activation(junk2[:, :], N[:, b, :], ACT.Square, accum_out=bb[:, b:b + 1]))
            sc.sem_inc(s["bb_ready"], 1)
            ln_turned(1)
            for h, bs in halves():
                sl = slice(h * HB, h * HB + HB)
                sc.wait_ge(s["ln_arg"], h + 1)
                link(nc.scalar.activation(inv[:, sl, :], inv[:, sl, :], ACT.Ln))
                nc.scalar.activation(inv[:, sl, :], inv[:, sl, :], ACT.Exp, scale=-0.5).then_inc(s["inv_ready"], 1)
            sc.wait_ge(free[act], r_bias.count)
            i = 0
            for m in range(KD):
                for q in range(NQ):
                    copy(r_kc[i], KcT[:, m, q * TC:(q + 1) * TC], bank(r_kc[i])[:, 0:TC], ACT.Identity,
                         bias=bqk[:, 1, m:m + 1])
                    i += 1
            sc.wait_ge(s["dist_moved0"], 16 * HB * G)
            sc.wait_ge(s["dist_moved2"], 16 * HB * G)
            for i, slot in enumerate(r_vc):
                copy(slot, Vc_r[0:CR, 2 * i * D:(2 * i + 2) * D], bank(slot)[0:CR, :])
            for i, slot in enumerate(r_ptm):
                if slot.reader == act:
                    h, c4 = i // 2, i % 2
                    copy(slot, PTs[:, h, :, :, 4 * c4:4 * c4 + 4].rearrange("p b s c -> p c s b"),
                         bank(slot)[0:CR, 0:4 * T].rearrange("p (c s b) -> p c s b", c=4, s=SEG))
            ln_turned(2)

            def up0(e):
                r = e % 2
                if e >= 2:
                    sc.wait_ge(full, r_dn0[e - 2][-1].n + 1)
                for i, slot in enumerate(r_up0[e]):
                    m, h = i // 2, i % 2
                    copy(slot, hT[:, r, m, x_cols(h)], bank(slot)[:, 0:HT], ACT.Relu, bias=b1c[:, e, m:m + 1])

            def gate_exp(n):
                E = (E0, E1)[n]
                sc.wait_ge(s["logits_ready"], n + 1)
                nc.scalar.activation(gp[:, :, 0:E], gl[:, :, 0:E], ACT.Exp).then_inc(s["logits_exp"], 1)
            gate_exp(0)
            up0(0)
            for i, slot in enumerate(r_cwt):
                copy(slot, cwT[:, x_cols(i)], bank(slot)[0:E0, 0:HT])
            for w, slot in enumerate(r_wt):
                copy(slot, wT[:, :, w, :], bank(slot).rearrange("p (k n) -> p k n", k=KD))
            for e in range(1, E0):
                up0(e)
            ln_turned(3)
            for i, slot in enumerate(r_hT):
                if slot.reader == act:
                    copy(slot, turned(i), bank(slot)[:, 0:4 * T].rearrange("p (c t) -> p c t", c=4))
            for i, slot in enumerate(r_vh):
                g, h4 = i // 4, i % 4
                src = bank(slot)[0:T, :].rearrange("p (h b d) -> p h b d", h=4, b=HB)[:, :, :, 0:HD]
                copy(slot, Vh[:, g * HB:(g + 1) * HB, 4 * h4:4 * h4 + 4, 0:HD],
                     src.rearrange("p h b d -> p b h d"))
            for n in range(NG + 1):
                if n < NG:
                    sc.wait_ge(free[dve], r_s1[n].count)
                    if n >= 2:
                        sc.wait_ge(full, r_pt1[n - 2].n + 1)
                    nc.scalar.activation(Px[:, n % 2], Sx[:, n % 2], ACT.Exp, scale=HD ** -0.5)\
                        .then_inc(s["heads_exp"], 1)
                if n >= 1:
                    if n >= 3:
                        sc.wait_ge(full, r_o1[n - 3].n + 1)
                    copy(r_pt1[n - 1], PxT[:, (n - 1) % 2], bank(r_pt1[n - 1])[0:T, 0:HT])
            for i, slot in enumerate(r_oT):
                h, k = i // KD, i % KD
                copy(slot, NT[:, k, x_cols(h)], bank(slot)[:, 0:HT])
            ln_turned(4)
            i = 0
            for m in range(KD):
                for h in range(2):
                    copy(r_qx[i], qxT[:, m, x_cols(h)], bank(r_qx[i])[:, 0:HT], ACT.Identity, bias=bqk[:, 0, m:m + 1])
                    i += 1
            for b in range(B + 1):
                if b < B:
                    sc.wait_ge(s["pc_shift"], b + 1)
                    if b >= 2:
                        sc.wait_ge(full, r_ptc[b - 2].n + 1)
                    copy(r_sc[b], Pc[:, b % 2], bank(r_sc[b])[0:T, 0:S], ACT.Exp,
                         bias=mx[:, 1, b:b + 1], scale=D ** -0.5, accum_out=rs[:, 0, b:b + 1])
                if b >= 1:
                    if b >= 3:
                        sc.wait_ge(full, r_oc[b - 3].n + 1)
                    copy(r_ptc[b - 1], PcT[:, (b - 1) % 2],
                         bank(r_ptc[b - 1])[0:CR, 0:CH * T].rearrange("p (h n) -> p h n", h=CH))
            ln_turned(5)
            gate_exp(1)
            for e in range(NX):
                for h in range(2):
                    if e >= 2:
                        sc.wait_ge(free[dve], r_up1[e - 2][2 * h + 1].count)
                    copy(r_up1[e][2 * h], sg[:, e % 2, x_cols(h)], bank(r_up1[e][2 * h])[:, 0:HT], ACT.Silu)

        @block.tensor
        def _(pe):
            def bank(slot):
                if slot.before is not None:
                    pe.wait_ge(free[slot.before.reader], slot.before.count)
                return ps[:, slot.bank, :]

            def mm(dst, lhsT, rhs, first=True, last=True):
                return nc.tensor.matmul(dst, lhsT, rhs, start=first, stop=last)

            def turn(dst, src, n):
                return nc.tensor.transpose(dst, src, ident[0:n, 0:n])

            def filled(ins):
                ins.then_inc(full, 1)

            def ln_turn(n):
                for i, slot in enumerate(ln_slots[n]):
                    h, k = i // KD, i % KD
                    pe.wait_ge(s["norm_ready"], n * B + (h + 1) * HB)
                    dst = bank(slot)
                    for j in range(HB):
                        m = turn(dst[:, j * T:(j + 1) * T], N[:, h * HB + j, k * 128:(k + 1) * 128], T)
                    filled(m)

            def wait_act(slot):
                pe.wait_ge(free[act], slot.count)

            def wait_dve(slot):
                pe.wait_ge(free[dve], slot.count)

            pe.wait_ge(s["ident_ready"], 1)
            for i, slot in enumerate(r_ctx):
                q, k = i // KD, i % KD
                for l in range(2 * q // 3, (4 * q + 3) // 6 + 1):
                    pe.wait_ge(ctx_loaded[l], 16)
                dst = bank(slot)
                for j in range(4):
                    m = turn(dst[:, j * CR:(j + 1) * CR], ctxN0[:, 4 * q + j, k * 128:(k + 1) * 128], CR)
                filled(m)
            pe.wait_ge(s["aux_loaded"], 64)
            filled(turn(bank(r_bias)[:, 0:NB], brow, NB))
            ln_turn(0)
            pe.wait_ge(s["w0_loaded"], 48)
            wait_act(ln_slots[0][-1])
            i = 0
            for w in range(2):
                for m in range(KD):
                    for h in range(2):
                        dst = bank(r_qk0[i])[:, 0:HT]
                        for k in range(KD):
                            last = mm(dst, w0[:, w, k, m * 128:(m + 1) * 128], NT[:, k, x_cols(h)], k == 0, k == KD - 1)
                        filled(last)
                        i += 1
            for i, slot in enumerate(r_v0):
                dst = bank(slot)
                for j in range(2):
                    for k in range(KD):
                        last = mm(dst[0:T, j * D:(j + 1) * D], NT[:, k, tok(2 * i + j)], w0[:, 2, k, :],
                                  k == 0, k == KD - 1)
                filled(last)
            wait_act(r_qk0[-1])
            for i, slot in enumerate(r_s0):
                dst = bank(slot)
                for j in range(HB):
                    b = i * HB + j
                    for k in range(KD):
                        last = mm(dst[0:T, j * T:(j + 1) * T], qkT0[:, 0, k, tok(b)], qkT0[:, 1, k, tok(b)],
                                  k == 0, k == KD - 1)
                filled(last)
            pe.wait_ge(s["consts_ready"], 1)
            for q, slot in enumerate(r_aa):
                pe.wait_ge(s["csq_ready"], q + 1)
                dst = bank(slot)
                for k in range(KD):
                    last = mm(dst[0:T, 0:TC], ones[:, :], csq[:, q % 2, k, :], k == 0, k == KD - 1)
                filled(last)
            for i, slot in enumerate(r_pt0):
                pe.wait_ge(s["p0_exp"], (i + 1) * HB)
                dst = bank(slot)
                for j in range(HB):
                    last = turn(dst[0:T, j * T:(j + 1) * T], P0[:, i * HB + j, :], T)
                filled(last)
            wait_act(r_v0[-1])
            for i, slot in enumerate(r_pv0):
                wait_dve(r_pt0[i // 2])
                dst = bank(slot)
                for j in range(2):
                    b = 2 * i + j
                    last = mm(dst[0:T, j * D:(j + 1) * D], PT0[:, b, :], V0[:, b, :])
                filled(last)
            ln_turn(1)
            wait_act(ln_slots[1][-1])
            for b, slot in enumerate(r_dist):
                dst = bank(slot)[0:T, 0:S]
                for k in range(KD):
                    last = mm(dst, NT[:, k, tok(b)], ctxT[:, k, b * S:(b + 1) * S], k == 0, k == KD - 1)
                filled(last)
            pe.wait_ge(s["wkv_loaded"], 32)
            i = 0
            for m in range(KD):
                for q in range(NQ):
                    dst = bank(r_kc[i])[:, 0:TC]
                    for k in range(KD):
                        last = mm(dst, wkv[:, 0, k, m * 128:(m + 1) * 128], ctxT[:, k, q * TC:(q + 1) * TC],
                                  k == 0, k == KD - 1)
                    filled(last)
                    i += 1
            for i, slot in enumerate(r_vc):
                dst = bank(slot)
                for j in range(2):
                    lo = (2 * i + j) * CR
                    for k in range(KD):
                        last = mm(dst[0:CR, j * D:(j + 1) * D], ctxT[:, k, lo:lo + CR], wkv[:, 1, k, :],
                                  k == 0, k == KD - 1)
                filled(last)
            pe.wait_ge(s["esel_ready"], 1)
            filled(mm(bank(r_e[0])[0:T, 0:1], esel[:, :], ones[0:B, 0:1]))
            pe.wait_ge(s["path_ready"], 1)
            for i, slot in enumerate(r_ptm):
                h, c4 = i // 2, i % 2
                dst = bank(slot)
                for j in range(4):
                    c = 4 * c4 + j
                    last = turn(dst[0:CR, j * T:(j + 1) * T], Pm[:, c * S + h * CR:c * S + (h + 1) * CR], T)
                filled(last)
            pe.wait_ge(s["ctx_reloaded"], 16)
            wait_act(r_ptm[4])
            wait_dve(r_ptm[5])
            for i, slot in enumerate(r_exp):
                dst = bank(slot)
                for j in range(2):
                    b = 2 * i + j
                    for h in range(CH):
                        last = mm(dst[0:T, j * D:(j + 1) * D], PTs[:, h, b].rearrange("p s c -> p (s c)"),
                                  ctxN[:, b, h, :], h == 0, h == CH - 1)
                filled(last)
            ln_turn(2)

            def gate_logits(slot, wr, E):
                dst = bank(slot)
                for b in range(B):
                    for k in range(KD):
                        last = mm(dst[0:T, b * E:(b + 1) * E], NT[:, k, tok(b)], wr[:, k, :], k == 0, k == KD - 1)
                filled(last)

            def up0(e):
                r = e % NW0
                pe.wait_ge(w0x_loaded[r], 32 * (e // NW0 + 1))
                for i, slot in enumerate(r_up0[e]):
                    m, h = i // 2, i % 2
                    dst = bank(slot)[:, 0:HT]
                    for k in range(KD):
                        last = mm(dst, W1s[:, r, k, m * 128:(m + 1) * 128], NT[:, k, x_cols(h)], k == 0, k == KD - 1)
                    filled(last)

            def down0(e):
                r, rh = e % NW0, e % 2
                wait_act(r_up0[e][-1])
                for i, slot in enumerate(r_dn0[e]):
                    dst = bank(slot)
                    for j in range(2):
                        for m in range(M0):
                            last = mm(dst[0:T, j * D:(j + 1) * D], hT[:, rh, m, tok(2 * i + j)], W2s[:, r, m, :],
                                      m == 0, m == M0 - 1)
                    filled(last)

            wait_act(ln_slots[2][-1])
            pe.wait_ge(s["router_loaded"], 32)
            gate_logits(r_g0[0], wr0, E0)
            up0(0)
            pe.wait_ge(s["gates_ready"], 1)
            for i, slot in enumerate(r_cwt):
                dst = bank(slot)
                for j in range(HB):
                    last = turn(dst[0:E0, j * T:(j + 1) * T], cw[:, i * HB + j, 0:E0], T)
                filled(last)
            wait_act(r_cwt[-1])
            pe.wait_ge(s["ffn_aux_loaded"], 16)
            for i, slot in enumerate(r_b2):
                dst = bank(slot)
                for j in range(2):
                    last = mm(dst[0:T, j * D:(j + 1) * D], cwT[:, tok(2 * i + j)], b2s[:, :])
                filled(last)
            for w, slot in enumerate(r_wt):
                if w % 2 == 0:
                    pe.wait_ge(s[f"wn_loaded{w // 2}"], 32)
                dst = bank(slot).rearrange("p (k n) -> p k n", k=KD)
                for k in range(KD):
                    for r in range(KD):
                        last = turn(dst[:, k, r * 128:(r + 1) * 128], wn[:, w % 2, r, k * 128:(k + 1) * 128], 128)
                filled(last)
                if w == 1:
                    pe.wait_ge(full, slot.n + 1)
                    pe.sem_inc(s["wn_used"], 1)
            for e in range(1, E0 + 1):
                if e < E0:
                    up0(e)
                down0(e - 1)
            ln_turn(3)
            wait_act(ln_slots[3][-1])
            pe.wait_ge(s["rope_ready"], 1)
            for i, slot in enumerate(r_qkv):
                b = i // 2
                cols = slice(0, 2 * D) if i % 2 == 0 else slice(2 * D, 3 * D)
                dst = bank(slot)[0:T, 0:cols.stop - cols.start]
                for k in range(KD):
                    last = mm(dst, NT[:, k, tok(b)], wT[:, k].rearrange("p w n -> p (w n)")[:, cols],
                              k == 0, k == KD - 1)
                filled(last)
            pe.wait_ge(s["vh_ones"], 2)
            wait_dve(r_qkv[-1])
            for i, slot in enumerate(r_hT):
                w, g, cq = i // 8, (i // 4) % 2, i % 4
                dst = bank(slot)
                for j in range(4):
                    lo = o_qkv + (2 * w + g) * HB * D + (2 * cq + j // 2) * 128 + j % 2 * HD
                    last = turn(dst[:, j * T:(j + 1) * T], big[0:T, lo:lo + 128], T)
                filled(last)
            wait_act(r_hT[-2])
            wait_dve(r_hT[-1])
            for i, slot in enumerate(r_vh):
                g, h4 = i // 4, i % 4
                dst = bank(slot)
                for j in range(4):
                    h = 4 * h4 + j
                    last = turn(dst[0:T, j * 128:(j + 1) * 128], VT[:, g, h * T:(h + 1) * T], 128)
                filled(last)
            for n in range(NG + 2):
                if n < NG:
                    g, hq, b4 = n // 16, (n // 4) % 4, n % 4
                    lo = 32 * b4
                    dst = bank(r_s1[n])
                    for j in range(4):
                        cols = slice((4 * hq + j) * T, (4 * hq + j + 1) * T)
                        last = mm(dst[0:T, j * T:(j + 1) * T], QKT[lo:lo + HD, 0, g, cols], QKT[lo:lo + HD, 1, g, cols])
                    filled(last)
                if 1 <= n <= NG:
                    pe.wait_ge(s["heads_exp"], n)
                    dst = bank(r_pt1[n - 1])
                    for j in range(4):
                        last = turn(dst[0:T, j * T:(j + 1) * T], Px[:, (n - 1) % 2, j * T:(j + 1) * T], T)
                    filled(last)
                if n >= 2:
                    g, hq, b4 = (n - 2) // 16, ((n - 2) // 4) % 4, (n - 2) % 4
                    if n == 2:
                        wait_act(r_vh[-1])
                    wait_act(r_pt1[n - 2])
                    dst = bank(r_o1[n - 2])
                    for j in range(4):
                        last = mm(dst[0:T, j * HV:(j + 1) * HV], PxT[:, n % 2, j * T:(j + 1) * T],
                                  Vh[:, g * HB + b4, 4 * hq + j, :])
                    filled(last)
            wait_dve(r_o1[NG - 1])
            for i, slot in enumerate(r_oT):
                h, k = i // KD, i % KD
                dst = bank(slot)
                for j in range(HB):
                    last = turn(dst[:, j * T:(j + 1) * T], N[:, h * HB + j, k * 128:(k + 1) * 128], T)
                filled(last)
            wait_act(r_oT[-1])
            for i, slot in enumerate(r_wo):
                dst = bank(slot)
                for j in range(2):
                    for k in range(KD):
                        last = mm(dst[0:T, j * D:(j + 1) * D], NT[:, k, tok(2 * i + j)], wT[:, k, 3, :],
                                  k == 0, k == KD - 1)
                filled(last)
            ln_turn(4)
            wait_act(ln_slots[4][-1])
            pe.wait_ge(s["wq1_loaded"], 16)
            i = 0
            for m in range(KD):
                for h in range(2):
                    dst = bank(r_qx[i])[:, 0:HT]
                    for k in range(KD):
                        last = mm(dst, wq1[:, k, m * 128:(m + 1) * 128], NT[:, k, x_cols(h)], k == 0, k == KD - 1)
                    filled(last)
                    i += 1
            wait_act(r_qx[-1])
            for n in range(B + 2):
                if n < B:
                    dst = bank(r_sc[n])[0:T, 0:S]
                    for k in range(KD):
                        last = mm(dst, qxT[:, k, tok(n)], KcT[:, k, n * S:(n + 1) * S], k == 0, k == KD - 1)
                    filled(last)
                if 1 <= n <= B:
                    wait_act(r_sc[n - 1])
                    dst = bank(r_ptc[n - 1])
                    for h in range(CH):
                        last = turn(dst[0:CR, h * T:(h + 1) * T], Pc[:, (n - 1) % 2, h * CR:(h + 1) * CR], T)
                    filled(last)
                if n >= 2:
                    wait_act(r_ptc[n - 2])
                    dst = bank(r_oc[n - 2])[0:T, 0:D]
                    for h in range(CH):
                        last = mm(dst, PcT[:, n % 2, h, :], Vc[:, n - 2, h, :], h == 0, h == CH - 1)
                    filled(last)
            ln_turn(5)
            wait_act(ln_slots[5][-1])
            gate_logits(r_g1[0], wr1, E1)
            for e in range(NX + 1):
                if e < NX:
                    if e == 0:
                        pe.wait_ge(s["wxa_loaded"], 48 * NF)
                    if e == NF:
                        pe.wait_ge(s["wxb_loaded"], 48 * (NX - NF))
                    for i, slot in enumerate(r_up1[e]):
                        h, w = i // 2, wx(e)[i % 2]
                        dst = bank(slot)[:, 0:HT]
                        for k in range(KD):
                            last = mm(dst, w[:, k, :], NT[:, k, x_cols(h)], k == 0, k == KD - 1)
                        filled(last)
                if e:
                    wait_dve(r_up1[e - 1][3])
                    for i, slot in enumerate(r_dn1[e - 1]):
                        dst = bank(slot)
                        for j in range(2):
                            last = mm(dst[0:T, j * D:(j + 1) * D], hx[:, (e - 1) % 2, tok(2 * i + j)], wx(e - 1)[2])
                        filled(last)

        @block.vector
        def _(ve):
            link_n = [0]

            def link(ins):
                link_n[0] += 1
                ins.then_inc(s["dve_link"], 1)
                ve.wait_ge(s["dve_link"], link_n[0])

            v = nc.vector

            def bank(slot):
                ve.wait_ge(full, slot.n + 1)
                return ps[:, slot.bank, :]

            def empty(slot, ins):
                ins.then_inc(free[dve], 1)

            def layer_norm(n, x_ready):
                for h, bs in halves():
                    for b in bs:
                        x_ready(b)
                        ins = v.bn_stats(stats[:, b, :], X[:, b, :])
                    link(ins)
                    for b in bs:
                        ins = v.bn_aggr(mv[:, b, :], stats[:, b, :])
                    ins.then_inc(s["stats_ready"], 1)
                for h, bs in halves():
                    ve.wait_ge(s["rstd_ready"], 2 * n + h + 1)
                    for b in bs:
                        v.tensor_scalar(N[:, b, :], X[:, b, :], mv[:, b, 0:1], rstd[:, b:b + 1],
                                        ALU.subtract, ALU.mult).then_inc(s["norm_ready"], 1)

            layer_norm(0, lambda b: ve.wait_ge(s[f"x_loaded{b // HB}"], 16))
            ve.wait_ge(s["mask_ready"], 1)
            for i, slot in enumerate(r_s0):
                bs = slice(i * HB, (i + 1) * HB)
                src = bank(slot)[0:T, 0:HT].rearrange("p (b n) -> p b n", b=HB)
                ins = v.scalar_tensor_tensor(P0[:, bs, :], src, D ** -0.5, view(cmask, 0, [[0, HB], [1, T]]),
                                             ALU.mult, ALU.add)
                empty(slot, ins)
                ve.wait_ge(free[dve], slot.count)
                link(v.tensor_reduce(mx[:, 0, bs], P0[:, bs, :], AX_X, ALU.max))
                v.tensor_scalar(mx[:, 1, bs], mx[:, 0, bs], -1.0, None, ALU.mult).then_inc(s["s0_ready"], 1)
            for i, slot in enumerate(r_pt0):
                bs = slice(i * HB, (i + 1) * HB)
                empty(slot, v.tensor_copy(PT0[:, bs, :], bank(slot)[0:T, 0:HT].rearrange("p (b n) -> p b n", b=HB)))
            ve.wait_ge(s["p0_exp"], B)
            link(v.reciprocal(rs[:, 1, :], rs[:, 0, :]))
            for i, slot in enumerate(r_pv0):
                src = bank(slot)
                for j in range(2):
                    b = 2 * i + j
                    ins = v.scalar_tensor_tensor(X[:, b, :], src[0:T, j * D:(j + 1) * D], rs[:, 1, b:b + 1],
                                                 X[:, b, :], ALU.mult, ALU.add)
                empty(slot, ins)
            ve.wait_ge(full, ln_slots[0][-1].n + 1)
            layer_norm(1, lambda b: ve.wait_ge(free[dve], r_pv0[b // 2].count))
            ve.wait_ge(s["bb_ready"], 1)
            ve.wait_ge(free[act], r_aa[-1].count)
            for b in range(B):
                ins = v.tensor_scalar(aaB[:, b, :], aaB[:, b, :], bb[:, b:b + 1], None, ALU.add)
            link(ins)
            for h, bs in halves():
                for b in bs:
                    slot = r_dist[b]
                    empty(slot, v.scalar_tensor_tensor(Dd[:, b, :], bank(slot)[0:T, 0:S], -2.0, aaB[:, b, :],
                                                       ALU.mult, ALU.add))
                ve.wait_ge(free[dve], slot.count)
                hb = slice(bs[0], bs[-1] + 1)
                v.tensor_scalar(inv[:, hb, :], Dd[:, hb, :], TINY, None, ALU.max).then_inc(s["ln_arg"], 1)
            for h, bs in halves():
                hb = slice(bs[0], bs[-1] + 1)
                d, r, z = Dd[:, hb, :], inv[:, hb, :], aaB[:, hb, :]
                ve.wait_ge(s["inv_ready"], h + 1)
                link(v.scalar_tensor_tensor(d, d, 0.0, r, ALU.max, ALU.mult))
                link(v.tensor_tensor(z, d, r, ALU.mult))
                link(v.scalar_tensor_tensor(z, z, -0.5, d, ALU.mult, ALU.mult))
                v.scalar_tensor_tensor(d, d, 1.5, z, ALU.mult, ALU.add).then_inc(s["dist_ready"], 1)
            ve.wait_ge(s["costs_clear"], 1)
            ve.wait_ge(s["dist_moved0"], 16 * HB * G)
            ve.wait_ge(s["dist_moved2"], 16 * HB * G)
            for t in range(STEPS):
                for k in range(KC):
                    q = t * KC + k + 1
                    link(v.tensor_tensor(mtmp[:, :], RS[:, q - 1, 0:RC], RS[:, q - 1, 1:RC + 1], ALU.min))
                    ins = v.tensor_tensor_scan(RS[:, q, 1:RC + 1], mtmp[:, :], Dsk[:, (q - 1) * RC:q * RC],
                                               RS[:, q, 0:1], ALU.min, ALU.add)
                    if k < KC - 1:
                        link(ins)
                ins.then_inc(s["dtw_step"], 1)
                ve.wait_ge(s["dtw_step"], t + 1)
                if t < STEPS - 1:
                    link(v.stream_shuffle(RS[:, q + 1:q + KC + 1, 0], RS[:, q - KC + 1:q + 1, RC],
                                          [(p - B) % 32 for p in range(32)]))
            link(v.memset(Cc[:, :, 0:1], 0.0))
            link(v.memset(einb[:, SEG - 1:SEG], float(S - 1)))
            ve.wait_ge(s["costs_moved"], 16 * SEG * G)
            cd, cu, cl = Rb[:, 0:SC, 0:S], Rb[:, 1:SC + 1, 0:S], Rb[:, 0:SC, 1:S + 1]
            m1v = m1.rearrange("p (c i) -> p c i", c=SC)
            diag, left = (dl[:, a, :].rearrange("p (c i) -> p c i", c=SC) for a in range(2))
            link(v.tensor_tensor(m1v, cu, cl, ALU.min))
            link(v.tensor_tensor(diag, cd, m1v, ALU.is_le))
            link(v.tensor_tensor(m1v, cu, cd, ALU.min))
            v.tensor_tensor(left, cl, m1v, ALU.is_lt).then_inc(s["choices_ready"], 2)
            ve.wait_ge(s["choices_ready"], 2)
            for c in range(SC):
                w = view(iota, 0, [[1, 2], [1, S]], (0, T)) if c == 0 else \
                    view(big, o_cc + (c - 1) % 2 * (S + 1), [[1, 2], [1, S]], (0, T))
                link(v.tensor_tensor(Tt, dl[:, :, c * S:(c + 1) * S], w, ALU.mult))
                ins = v.tensor_tensor_scan(Cc[:, c % 2, 1:S + 1], Tt[:, 0, :], Tt[:, 1, :], 0.0, ALU.max, ALU.max)
                if c < SC - 1:
                    link(ins)
            ins.then_inc(s["compose_done"], 1)
            ve.wait_ge(s["compose_done"], 1)
            ve.wait_ge(s["exits_ready"], 1)
            link(v.tensor_tensor_scan(Ex, U[:, 0:NS], Ex, 0.0, ALU.mult, ALU.add))
            ve.wait_ge(s["cw_moved"], 16 * (SEG - 1))
            for g in range(SEG - 1, 0, -1):
                link(v.scalar_tensor_tensor(junk[0:B, :], iota[0:B, 1:S + 1], einb[:, g:g + 1], Cw[:, g, :],
                                            ALU.is_equal, ALU.mult, accum_out=einb[:, g - 1:g]))
            ve.wait_ge(s["consts_ready"], 4)
            v.tensor_tensor(esel[:].rearrange("p (s b) -> p s b", b=B), esel[:].rearrange("p (s b) -> p s b", b=B),
                            view(einb, 0, [[1, SEG], [0, B]]), ALU.mult).then_inc(s["esel_ready"], 1)
            empty(r_e[0], v.tensor_copy(ecol[:, SC - 1:SC], bank(r_e[0])[0:T, 0:1]))
            ve.wait_ge(free[dve], r_e[0].count)
            for c in range(SC - 1, -1, -1):
                ins = v.tensor_scalar(OH[:, c * S:(c + 1) * S], iota[0:T, 1:S + 1], ecol[:, c:c + 1], None, ALU.is_equal)
                if c:
                    ins = v.scalar_tensor_tensor(junk[:, :], iota[0:T, 1:S + 1], ecol[:, c:c + 1],
                                                 Ex[:, c * S:(c + 1) * S], ALU.is_equal, ALU.mult,
                                                 accum_out=ecol[:, c - 1:c])
                link(ins)
            v.tensor_tensor_scan(view(Pm, NS - 1, [[-1, NS]]), view(U, NS, [[-1, NS]]),
                                 view(OH, NS - 1, [[-1, NS]]), 0.0, ALU.mult, ALU.add).then_inc(s["path_ready"], 1)
            for i, slot in enumerate(r_ptm):
                if slot.reader == dve:
                    h, c4 = i // 2, i % 2
                    empty(slot, v.tensor_copy(
                        PTs[:, h, :, :, 4 * c4:4 * c4 + 4].rearrange("p b s c -> p c s b"),
                        bank(slot)[0:CR, 0:4 * T].rearrange("p (c s b) -> p c s b", c=4, s=SEG)))

            def add_to_x(slots, before=None):
                for i, slot in enumerate(slots):
                    if before is not None:
                        ve.wait_ge(free[dve], before[i].count)
                    x2 = X[:, 2 * i:2 * i + 2, :]
                    empty(slot, v.tensor_tensor(x2, bank(slot)[0:T, :].rearrange("p (b d) -> p b d", b=2), x2, ALU.add))

            add_to_x(r_exp)
            ve.wait_ge(full, r_vc[-1].n + 1)
            layer_norm(2, lambda b: ve.wait_ge(free[dve], r_exp[b // 2].count))

            def gates(n, slot, E):
                lg, p, c = gl[:, :, 0:E], gp[:, :, 0:E], cw[:, :, 0:E]
                src = bank(slot)[0:T, 0:B * E].rearrange("p (b e) -> p b e", b=B)
                if n == 0:
                    ve.wait_ge(s["aux_loaded"], 64)
                    ins = v.tensor_tensor(lg, src, view(brb, 0, [[0, B], [1, E]]), ALU.add)
                else:
                    ins = v.tensor_copy(lg, src)
                empty(slot, ins)
                ve.wait_ge(free[dve], slot.count)
                link(v.tensor_reduce(mx[:, 0, :], lg, AX_X, ALU.max))
                v.tensor_tensor(lg, lg, view(mx, 0, [[1, B], [0, E]]), ALU.subtract).then_inc(s["logits_ready"], 1)
                ve.wait_ge(s["logits_exp"], n + 1)
                link(v.tensor_reduce(rs[:, 0, :], p, AX_X, ALU.add))
                link(v.reciprocal(rs[:, 1, :], rs[:, 0, :]))
                link(v.tensor_tensor(p, p, view(rs, B, [[1, B], [0, E]]), ALU.mult))
                more = big[0:T, o_ra:o_ra + B * E * E].rearrange("p (b e o) -> p b e o", b=B, e=E)
                same = big[0:T, o_re:o_re + B * E * E].rearrange("p (b e o) -> p b e o", b=B, e=E)
                p_o, p_e = view(gp, 0, [[E1, B], [0, E], [1, E]]), view(gp, 0, [[E1, B], [1, E], [0, E]])
                v.tensor_tensor(more, p_o, p_e, ALU.is_gt)
                link(v.tensor_tensor(same, p_o, p_e, ALU.is_equal))
                ve.wait_ge(s["tri_ready"], 1)
                link(v.tensor_tensor(same, same, view(junk, 0, [[0, B], [E1, E], [1, E]]), ALU.mult))
                link(v.tensor_tensor(more, more, same, ALU.add))
                rank = rk[:, 0:B * E].rearrange("p (b e) -> p b e", b=B)
                link(v.tensor_reduce(rank, more, AX_X, ALU.add))
                v.scalar_tensor_tensor(c, rank, 1.5, p, ALU.is_lt, ALU.mult).then_inc(s["gates_ready"], 1)
                ve.wait_ge(s["gates_ready"], n + 1)

            gates(0, r_g0[0], E0)
            add_to_x(r_b2, r_exp)
            def turn_by_position(z):
                pairs = lambda a: a.rearrange("p (n two) -> p n two", two=2)
                t1, t2 = rope[:, 0, :], rope[:, 1, :]
                n = 2 * D // HD
                z3 = z.rearrange("p (n d) -> p n d", d=HD)
                link(v.tensor_tensor(t1.rearrange("p (n d) -> p n d", d=HD), z3, view(big, o_cs, [[0, n], [1, HD]]), ALU.mult))
                for odd in range(2):
                    link(v.tensor_tensor(
                        t2.rearrange("p (n i two) -> p n i two", i=HD // 2, two=2)[:, :, :, odd],
                        z.rearrange("p (n i two) -> p n i two", i=HD // 2, two=2)[:, :, :, 1 - odd],
                        view(big, o_cs + HD + odd, [[0, n], [2, HD // 2]]), ALU.mult))
                for odd in range(2):
                    link(v.tensor_tensor(pairs(z)[:, :, odd], pairs(t1)[:, :, odd], pairs(t2)[:, :, odd],
                                         (ALU.subtract, ALU.add)[odd]))
            ve.wait_ge(s["attn_w_loaded"], 96)
            ve.wait_ge(free[act], r_wt[-1].count)
            for k in range(KD):
                turn_by_position(wT[:, k, 0:2, :].rearrange("p w n -> p (w n)"))
            turn_by_position(bqkv[:, 0:2, :].rearrange("p w n -> p (w n)"))
            ve.sem_inc(s["rope_ready"], 1)

            def gated(slots, before, gate):
                for i, slot in enumerate(slots):
                    src = bank(slot)
                    ve.wait_ge(free[dve], before[i].count)
                    for j in range(2):
                        b = 2 * i + j
                        ins = v.scalar_tensor_tensor(X[:, b, :], src[0:T, j * D:(j + 1) * D], gate(b), X[:, b, :],
                                                     ALU.mult, ALU.add)
                    empty(slot, ins)

            for e in range(E0):
                gated(r_dn0[e], r_dn0[e - 1] if e else r_b2, lambda b: cw[:, b, e:e + 1])
            layer_norm(3, lambda b: ve.wait_ge(free[dve], r_dn0[E0 - 1][b // 2].count))
            for i, slot in enumerate(r_qkv):
                b = i // 2
                w0_, w1_ = (0, 2) if i % 2 == 0 else (2, 3)
                cut = dict(w=w1_ - w0_, c=NH // 2)
                empty(slot, v.tensor_tensor(
                    QKV[:, w0_:w1_, b // HB, :, b % HB, :],
                    bank(slot)[0:T, 0:(w1_ - w0_) * D].rearrange("p (w c d) -> p w c d", **cut),
                    big[0:T, o_bq + w0_ * D:o_bq + w1_ * D].rearrange("p (w c d) -> p w c d", **cut), ALU.add))
            for i, slot in enumerate(r_hT):
                if slot.reader == dve:
                    empty(slot, v.tensor_copy(turned(i), bank(slot)[:, 0:4 * T].rearrange("p (c t) -> p c t", c=4)))
            for n in range(NG + 2):
                if n < NG:
                    src = bank(r_s1[n])[0:T, 0:HT].rearrange("p (j n) -> p j n", j=4)
                    link(v.tensor_reduce(hm[:, 0, 0:4], src, AX_X, ALU.max))
                    if n >= 2:
                        ve.wait_ge(s["heads_exp"], n - 1)
                    empty(r_s1[n], v.tensor_tensor(Sx[:, n % 2].rearrange("p (j n) -> p j n", j=4), src,
                                                   view(hm, 0, [[1, 4], [0, T]]), ALU.subtract))
                if n >= 2:
                    slot = r_o1[n - 2]
                    g, hq, b4 = (n - 2) // 16, ((n - 2) // 4) % 4, (n - 2) % 4
                    src = bank(slot)[0:T, 0:4 * HV].rearrange("p (j d) -> p j d", j=4)
                    link(v.reciprocal(hm[:, 1, 0:4], src[:, :, HD]))
                    dst = N[:, g * HB + b4, 4 * hq * HD:(4 * hq + 4) * HD].rearrange("p (j d) -> p j d", j=4)
                    empty(slot, v.tensor_tensor(dst, src[:, :, 0:HD], view(hm, 8, [[1, 4], [0, HD]]), ALU.mult))
                    ve.wait_ge(free[dve], slot.count)
                elif n < NG:
                    ve.wait_ge(free[dve], r_s1[n].count)
            ve.wait_ge(s["bias_added"], 1)
            add_to_x(r_wo)
            ve.wait_ge(full, r_oT[-1].n + 1)
            layer_norm(4, lambda b: ve.wait_ge(free[dve], r_wo[b // 2].count))
            ve.wait_ge(s["norm_ready"], 5 * B)
            for n in range(B + 2):
                if n < B:
                    link(v.tensor_reduce(mx[:, 0, n:n + 1], bank(r_sc[n])[0:T, 0:S], AX_X, ALU.max))
                    v.tensor_scalar(mx[:, 1, n:n + 1], mx[:, 0, n:n + 1], -(D ** -0.5), None, ALU.mult)\
                        .then_inc(s["pc_shift"], 1)
                if n >= 2:
                    b = n - 2
                    ve.wait_ge(free[act], r_sc[b].count)
                    link(v.reciprocal(rs[:, 1, b:b + 1], rs[:, 0, b:b + 1]))
                    ve.wait_ge(s["bias_added"], 2)
                    empty(r_oc[b], v.scalar_tensor_tensor(X[:, b, :], bank(r_oc[b])[0:T, 0:D], rs[:, 1, b:b + 1],
                                                          X[:, b, :], ALU.mult, ALU.add))
            layer_norm(5, lambda b: ve.wait_ge(free[dve], r_oc[b].count))
            gates(1, r_g1[0], E1)
            for e in range(NX + 1):
                if e < NX:
                    for h in range(2):
                        slot = r_up1[e][2 * h + 1]
                        if h == 0 and e >= 2:
                            ve.wait_ge(full, r_dn1[e - 2][-1].n + 1)
                        ve.wait_ge(free[act], r_up1[e][2 * h].count)
                        empty(slot, v.tensor_tensor(hx[:, e % 2, x_cols(h)], bank(slot)[:, 0:HT],
                                                    sg[:, e % 2, x_cols(h)], ALU.mult))
                if e:
                    f = e - 1
                    gated(r_dn1[f], r_dn1[f - 1] if f else [r_g1[0]] * 4,
                          lambda b: cw[:, b, f:f + 1] if f < E1 else 1.0)


_INS = ['x', 'ctx_1024', 'L0_attn_Wk', 'L0_attn_Wq', 'L0_attn_Wv', 'L0_ffn_Wr', 'L0_ffn_br', 'L0_ffn_W1',
        'L0_ffn_b1', 'L0_ffn_W2', 'L0_ffn_b2', 'L1_attn_wq', 'L1_attn_bq', 'L1_attn_wk', 'L1_attn_bk',
        'L1_attn_wv', 'L1_attn_bv', 'L1_attn_wo', 'L1_attn_bo', 'L1_attn_cos', 'L1_attn_sin',
        'L1_xattn_Wq', 'L1_xattn_bq', 'L1_xattn_Wk', 'L1_xattn_bk', 'L1_xattn_Wv', 'L1_xattn_bv',
        'L1_ffn_Wr', 'L1_ffn_Wg', 'L1_ffn_Wu', 'L1_ffn_Wd', 'L1_ffn_Sg', 'L1_ffn_Su', 'L1_ffn_Sd']


def kernel(**inputs):
    import numpy as _np
    import concourse.bacc as _bacc
    from concourse import mybir as _mybir
    from concourse.bass_utils import run_bass_kernel_spmd as _run

    nc = _bacc.Bacc("TRN2", target_bir_lowering=False, num_devices=1)
    arrays, args = {}, {}
    for name in _INS:
        a = _np.ascontiguousarray(inputs[name])
        arrays[f"in_{name}"] = a
        args[name] = nc.dram_tensor(f"in_{name}", a.shape, _mybir.dt.from_np(a.dtype), kind="ExternalInput").ap()
    shape = tuple(inputs["x"].shape)
    out = nc.dram_tensor("out_0", shape, _mybir.dt.from_np(_np.dtype("float32")), kind="ExternalOutput").ap()
    decoder_kernel(nc, args, out)
    r = _run(nc, [arrays], core_ids=[0])
    return r.results[0]["out_0"]
```

```python
from contextlib import ExitStack

import concourse.bass as bass
from concourse import mybir

F32 = mybir.dt.float32
F32R = mybir.dt.float32r
ALU = mybir.AluOpType
ACT = mybir.ActivationFunctionType
AX_X = mybir.AxisListType.X

BIG = 1e30
BANKS = 8
EPS = 1e-5
TINY = 1e-14


class Slot:

    def __init__(self, bank, before):
        self.bank, self.before = bank, before


class BankRing:

    def __init__(self):
        self.turns = list(range(BANKS))
        self.last = {}
        self.filled = 0
        self.counts = {}

    def open(self, bank):
        slot = Slot(bank, self.last.get(bank))
        self.last[bank] = slot
        return slot

    def close(self, slot, reader):
        self.counts[reader] = self.counts.get(reader, 0) + 1
        slot.n, slot.reader, slot.count = self.filled, reader, self.counts[reader]
        self.filled += 1
        return slot

    def take(self, *readers):
        out = []
        for reader in readers:
            self.turns.append(self.turns.pop(0))
            out.append(self.close(self.open(self.turns[-1]), reader))
        return out


def view(t, offset, dims, parts=None):
    x = t[:] if parts is None else t[parts[0]:parts[1]]
    return bass.AP(x.tensor, x.offset + offset, [x.ap[0]] + dims)


def rows_of(a, parts):
    n = a.shape[-1]
    return bass.AP(a.tensor, a.offset, [[0, parts], [1, n]])


def decoder_kernel(nc, A, out):
    B, T, D = A["x"].shape
    S = A["ctx_1024"].shape[1]
    KD = D // 128
    CH = 3
    CR = S // CH
    HB = B // 2
    HT = HB * T
    E0, F0 = A["L0_ffn_b1"].shape
    M0 = F0 // 128
    E1, _, F1 = A["L1_ffn_Wg"].shape
    NX = E1 + A["L1_ffn_Sg"].shape[1] // F1
    G = 4
    RC = -(-S // G)
    KC = 4
    STEPS = T // KC + G - 1
    NSLOT = STEPS * KC + 1
    SC = 8
    SEG = T // SC
    NH, HD = 16, D // 16
    assert B * HD == 128
    VZ = B * 128 + 112
    TC = 4 * CR
    NQ = B * CH // 4
    assert S == CH * CR and SEG * B == T and T * HD == NH * T and 2 * HB == B

    with ExitStack() as ctx:
        def sb(name, shape):
            return ctx.enter_context(nc.sbuf_tensor(name, shape, F32))

        def sem(name):
            return ctx.enter_context(nc.semaphore(name))

        ps = ctx.enter_context(nc.psum_tensor("ps", [128, BANKS, 512], F32))

        X = sb("X", [T, B, D])
        NT = sb("NT", [128, KD, B * T])
        BIGN = 26930
        large = (("N_r", B * D),
                 ("ctxT_r", 3 * 2048),
                 ("KcT_r", KD * B * S),
                 ("Vc_r", B * CH * D),
                 ("big", BIGN))
        with ExitStack() as plain:
            N_r, ctxT_r, KcT_r, Vc_r, big = (plain.enter_context(nc.sbuf_tensor(n, [128, c], F32)) for n, c in large)
        N_s, ctxT_s, KcT_s, Vc_s, big_s = (
            ctx.enter_context(nc.sbuf_tensor(n + "_split", [128, c], F32R)) for n, c in large)
        KcT = KcT_r[:, :].rearrange("p (k n) -> p k n", k=KD)
        ident = sb("ident", [128, 128])
        iota = sb("iota", [128, S + 1])
        ones = sb("ones", [128, T])
        stats = sb("stats", [T, B, 6])
        mv = sb("mv", [T, B, 2])
        veps = sb("veps", [T, B])
        mhalf = sb("mhalf", [T, B])
        rstd = sb("rstd", [T, B])
        mx = sb("mx", [T, 2, B])
        rs = sb("rs", [T, 2, B])
        bb = sb("bb", [T, B])
        NB = E0 * M0 + 2 * KD
        brow = KcT[0:NB, 0, 0:128]
        bcol = sb("bcol", [128, NB])
        b1c = bcol[:, 0:E0 * M0].rearrange("p (e m) -> p e m", e=E0)
        bqk = bcol[:, E0 * M0:NB].rearrange("p (w k) -> p w k", w=2)
        brb = sb("brb", [T, E0])
        cw = sb("cw", [T, B, E1])
        einb = sb("einb", [B, SEG])
        esel = sb("esel", [B, T])
        ecol = sb("ecol", [T, SC])

        ctxT = ctxT_r[:, 0:KD * B * S].rearrange("p (k n) -> p k n", k=KD)
        N = N_r[0:T, :].rearrange("p (b d) -> p b d", b=B)
        Vc = Vc_r[0:CR, :].rearrange("p (b c d) -> p b c d", b=B, c=CH)

        def place(start, *sizes):
            offs, o = [], start
            for n in sizes:
                offs.append(o)
                o += n
            assert o <= BIGN, (start, sizes, o)
            return offs

        NS = SC * S
        RB = S + 2
        o_dsk, o_rs, o_rb = place(0, STEPS * KC * RC, NSLOT * (RC + 1), (SC + 1) * RB)
        ctxN0 = big[0:CR, 0:B * CH * D].rearrange("p (j d) -> p j d", d=D)
        o_w0, o_qk0, o_v0, o_p0, o_pt0, o_cm, o_sq = place(
            o_rs, 3 * KD * D, 2 * KD * B * T, B * D, B * T, B * T, T, 2 * KD * TC)
        w0 = big[:, o_w0:o_qk0].rearrange("p (w k n) -> p w k n", w=3, k=KD)
        qkT0 = big[:, o_qk0:o_v0].rearrange("p (w k n) -> p w k n", w=2, k=KD)
        V0 = big[0:T, o_v0:o_p0].rearrange("p (b d) -> p b d", b=B)
        P0 = big[0:T, o_p0:o_pt0].rearrange("p (b n) -> p b n", b=B)
        PT0 = big[0:T, o_pt0:o_cm].rearrange("p (b n) -> p b n", b=B)
        cmask = big[0:T, o_cm:o_cm + T]
        csq = big[:, o_sq:o_sq + 2 * KD * TC].rearrange("p (a k n) -> p a k n", a=2, k=KD)
        assert o_sq + 2 * KD * TC <= o_rb
        Dd = Vc_r[0:T, 0:B * S].rearrange("p (b n) -> p b n", b=B)
        aaB = Vc_r[0:T, B * S:2 * B * S].rearrange("p (b n) -> p b n", b=B)
        inv = big[0:T, o_rb:o_rb + B * S].rearrange("p (b n) -> p b n", b=B)
        Dsk = big[0:G * B, o_dsk:o_rs]
        RS = big[0:G * B, o_rs:o_rb].rearrange("p (q i) -> p q i", i=RC + 1)
        mtmp = sb("mtmp", [G * B, RC])
        Rb = big[0:T, o_rb:o_rb + (SC + 1) * RB].rearrange("p (c i) -> p c i", c=SC + 1)
        ctxN = big[0:CR, 0:B * CH * D].rearrange("p (b c d) -> p b c d", b=B, c=CH)
        o_m1, o_cc, o_tt = place(B * CH * D, NS, 2 * (S + 1), 2 * S)
        assert o_tt + 2 * S <= o_rs
        o_dl, o_u, o_pts = place(o_rs, 2 * NS, NS + 1, CH * B * T)
        assert o_pts + CH * B * T <= o_rb
        m1 = big[0:T, o_m1:o_m1 + NS]
        dl = big[0:T, o_dl:o_dl + 2 * NS].rearrange("p (a n) -> p a n", a=2)
        U = big[0:T, o_u:o_u + NS + 1]
        Ex = m1
        Cc = big[0:T, o_cc:o_cc + 2 * (S + 1)].rearrange("p (a i) -> p a i", a=2)
        Tt = big[0:T, o_tt:o_tt + 2 * S].rearrange("p (a i) -> p a i", a=2)
        Cw = big[0:B, 0:SEG * S].rearrange("p (s i) -> p s i", s=SEG)
        assert SEG * S <= B * CH * D
        T1 = big[0:T, o_rb:o_rb + NS]
        OH = big[0:T, o_rb:o_rb + NS]
        Pm = big[0:T, o_dl:o_dl + NS]
        PTs = big[0:CR, o_pts:o_pts + CH * B * T].rearrange("p (h b s c) -> p h b s c", h=CH, b=B, s=SEG)
        junk = sb("junk", [T, S])
        junk2 = junk[:, 0:D]
        wkv = N_r[:, 0:2 * KD * D].rearrange("p (w k n) -> p w k n", w=2, k=KD)
        NW0 = 2
        WN0 = KD * F0 + M0 * D
        W0f = ctxT_r[:, 0:NW0 * WN0].rearrange("p (r n) -> p r n", r=NW0)
        NP = 4
        (o_h0, o_qkv, o_vh, o_vz, o_px1, o_wn, o_wt, o_bq, o_cs, o_b2, o_ps, o_pq) = place(
            0, 2 * M0 * B * T, 3 * B * D, B * D, 2 * VZ, NP * HT, 2 * KD * D, 4 * KD * D,
            4 * D, 2 * HD, D, 4 * HT, 2 * HT)
        hs = big_s[:, o_h0:o_qkv].rearrange("p (r a m n) -> p r a m n", r=2, a=2, m=M0)
        W0s = big_s[:, o_qkv:o_qkv + 4 * WN0].rearrange("p (r a n) -> p r a n", r=2, a=2)
        W1s = W0s[:, :, :, 0:KD * F0].rearrange("p r a (k f) -> p r a k f", k=KD)
        W2s = W0s[:, :, :, KD * F0:WN0].rearrange("p r a (m d) -> p r a m d", m=M0)
        o_r0, o_hf = place(o_qkv + 4 * WN0, 2 * B * E0 * E0, M0 * HT)
        assert o_hf + M0 * HT <= o_wn
        hf = big[:, o_hf:o_hf + M0 * HT].rearrange("p (m n) -> p m n", m=M0)
        NTs0 = [ctxT_s[:, NW0 * WN0:NW0 * WN0 + KD * B * T].rearrange("p (k n) -> p k n", k=KD),
                N_s[:, 0:KD * B * T].rearrange("p (k n) -> p k n", k=KD)]
        NTs1 = [KcT_s[:, a * KD * B * T:(a + 1) * KD * B * T].rearrange("p (k n) -> p k n", k=KD) for a in range(2)]
        WXN = 2 * KD * F1 + D
        WXs = Vc_s[:, :].rearrange("p (r a n) -> p r a n", r=4, a=2)
        assert 4 * 2 * WXN == B * CH * D
        hxs = [KcT_s[:, 2 * KD * B * T:2 * KD * B * T + 2 * B * T].rearrange("p (r n) -> p r n", r=2),
               N_s[:, 0:2 * B * T].rearrange("p (r n) -> p r n", r=2)]
        QKV = big[0:T, o_qkv:o_qkv + 3 * B * D].rearrange("p (w c b d) -> p w c b d", w=3, c=NH, b=B)
        o_qt, o_km = place(o_h0, 3 * NH * T, 3 * HT)
        assert o_km + 3 * HT <= o_qkv
        QKVT = big[:, o_qt:o_km].rearrange("p (w n) -> p w n", w=3)
        Km = big[:, o_km:o_km + 3 * HT].rearrange("p (r n) -> p r n", r=3)
        Vh = big[0:T, o_vh:o_vz].rearrange("p (h n) -> p h n", h=NH)
        Vz = big[0:T, o_vz:o_px1].rearrange("p (r n) -> p r n", r=2)
        Px = big[0:T, o_px1:o_wn].rearrange("p (r n) -> p r n", r=NP)
        PxT = big[0:T, o_ps:o_ps + 3 * HT].rearrange("p (r n) -> p r n", r=3)
        wn = big[:, o_wn:o_wt].rearrange("p (w r n) -> p w r n", w=2, r=KD)
        wT = big[:, o_wt:o_bq].rearrange("p (k w n) -> p k w n", k=KD, w=4)
        bqkv = big[:, o_bq:o_cs].rearrange("p (w n) -> p w n", w=4)
        cs = big[:, o_cs:o_b2].rearrange("p (w n) -> p w n", w=2)
        b2s = big[0:E0, o_b2:o_ps]
        cwT = big[0:E0, o_pq:o_pq + B * T]
        wr0 = sb("wr0", [128, KD, E0])
        wr1 = sb("wr1", [128, KD, E1])
        rope = big[:, o_ps:o_ps + 4 * D].rearrange("p (a n) -> p a n", a=2)
        rk = sb("rk", [T, B * E1])
        gl = sb("gl", [T, B, E1])
        gp = sb("gp", [T, B, E1])
        hm = rk[:, 0:NP * 4 * HB].rearrange("p (r q j) -> p r q j", r=NP, q=4)
        bmask = iota[:, 0:B]
        o_ra, o_re = place(o_qkv, B * E1 * E1, B * E1 * E1)
        tri = junk[:, 0:E1 * E1].rearrange("p (e o) -> p e o", e=E1)
        boB = bqkv[0:T, 3, :]
        bvB = big[0:T, o_b2:o_b2 + D]
        o_qx, o_sx, o_px, o_ptx, o_wq = place(o_qkv, KD * B * T, 2 * S, 2 * S, 2 * CH * T, KD * D)
        assert o_wq + KD * D <= o_vh
        qxT = big[:, o_qx:o_sx].rearrange("p (k n) -> p k n", k=KD)
        Pc = big[0:T, o_px:o_px + 2 * S].rearrange("p (r n) -> p r n", r=2)
        PcT = big[0:CR, o_ptx:o_ptx + 2 * CH * T].rearrange("p (r h n) -> p r h n", r=2, h=CH)
        wq1 = big[:, o_wq:o_wq + KD * D].rearrange("p (k n) -> p k n", k=KD)
        NF = 8
        WXA = ctxT_r[:, :].rearrange("p (e n) -> p e n", e=NF)
        o_wx, o_sg, o_hx = place(o_vh, (NX - NF) * 768, 2 * B * T, 2 * B * T)
        WXB = big[:, o_wx:o_sg].rearrange("p (e n) -> p e n", e=NX - NF)
        sg = big[:, o_sg:o_hx].rearrange("p (r n) -> p r n", r=2)
        hx = big[:, o_hx:o_hx + 2 * B * T].rearrange("p (r n) -> p r n", r=2)

        def wx(e):
            return WXA[:, e, :] if e < NF else WXB[:, e - NF, :]

        def three(w):
            n = KD * F1
            return (w[:, 0:n].rearrange("p (k f) -> p k f", k=KD),
                    w[:, n:2 * n].rearrange("p (k f) -> p k f", k=KD), w[:, 2 * n:2 * n + D])

        CTX_CUTS, AA_CUT = (6, 8), NQ - 2
        ring = BankRing()
        act, dve = "act", "dve"
        ln_slots = {}
        ln_slots[0] = ring.take(*[act] * 4)
        r_qk0 = ring.take(*[act] * 8)
        r_v0 = ring.take(*[act] * 4)
        r_s0 = ring.take(dve, dve)
        r_ctx = ring.take(*[act] * CTX_CUTS[0])
        r_pt0 = ring.take(dve, dve)
        r_ctx += ring.take(*[act] * (CTX_CUTS[1] - CTX_CUTS[0]))
        r_pv0 = ring.take(*[dve] * 4)
        r_ctx += ring.take(*[act] * (KD * NQ - CTX_CUTS[1]))
        (r_bias,) = ring.take(act)
        r_aa = ring.take(*[act] * AA_CUT)
        ln_slots[1] = ring.take(*[act] * 4)
        r_aa += ring.take(*[act] * (NQ - AA_CUT))
        r_dist = ring.take(*[dve] * B)
        r_kc = ring.take(*[act] * (KD * NQ))
        r_vc = ring.take(*[act] * (B * CH // 2))
        r_e = ring.take(dve)
        r_ptm = ring.take(*[act, dve] * 3)
        r_exp = ring.take(*[dve] * 4)
        ln_slots[2] = ring.take(*[act] * 4)
        r_g0 = ring.take(dve)
        r_up0 = {}
        r_dn0 = {}
        r_up0[0] = ring.take(*[act] * M0)
        r_cwt = ring.take(act, act)
        r_b2 = ring.take(*[dve] * 4)
        r_wt = ring.take(*[act] * 4)
        for u in range(1, 2 * E0 + 1):
            if u < 2 * E0:
                r_up0[u] = ring.take(*[act] * M0)
            r_dn0[u - 1] = ring.take(dve, dve)
        ln_slots[3] = ring.take(*[act] * 4)
        r_qkv = ring.take(*[dve] * (2 * B))
        r_hT = ring.take(*[act, dve] * 6)
        r_vh = ring.take(*[act] * 4)
        NG = 2 * NH
        LN, LT, LV = 2, 3, 4
        r_s1, r_pt1, r_o1 = {}, {}, {}
        ring.turns = [x for x in ring.turns if x < BANKS - 2]
        for n in range(NG + LV):
            if n < NG:
                (r_s1[n],) = ring.take(act)
            if LT <= n < NG + LT:
                (r_pt1[n - LT],) = ring.take(act)
            if n >= LV:
                h, g = (n - LV) // 2, (n - LV) % 2
                if h % 8 == 0:
                    r_o1[h // 8, g] = ring.open(BANKS - 2 + g)
                if h % 8 == 7:
                    ring.close(r_o1[h // 8, g], act)
        ring.turns += [BANKS - 2, BANKS - 1]
        r_wo = ring.take(*[dve] * 4)
        ln_slots[4] = ring.take(*[act] * 4)
        r_qx = ring.take(*[act] * 4)
        r_sc, r_ptc, r_oc = {}, {}, {}
        for n in range(B + 2):
            if n < B:
                (r_sc[n],) = ring.take(act)
            if 1 <= n <= B:
                (r_ptc[n - 1],) = ring.take(act)
            if n >= 2:
                (r_oc[n - 2],) = ring.take(dve)
        ln_slots[5] = ring.take(*[act] * 4)
        r_g1 = ring.take(dve)
        r_up1, r_dn1 = {}, {}
        for e in range(NX + 1):
            if e < NX:
                r_up1[e] = ring.take(act, dve, act, dve)
            if e:
                r_dn1[e - 1] = ring.take(*[dve] * 4)

        full = sem("banks_filled")
        free = {act: sem("banks_emptied_by_act"), dve: sem("banks_emptied_by_dve")}
        names = ("ident_ready", "consts_ready", "x_loaded0", "x_loaded1", "w0_loaded", "aux_loaded",
                 "stats_ready", "rstd_ready", "norm_ready", "p0_exp", "s0_ready",
                 "bb_ready", "csq_ready", "dsk_clear", "costs_clear", "ln_arg", "inv_ready", "dist_ready",
                 "dist_moved", "wkv_loaded",
                 "dtw_step", "costs_moved", "ctx_reloaded", "choices_ready", "exits_ready", "ups_ready",
                 "compose_done", "esel_ready", "path_ready", "logits_exp", "logits_ready",
                 "gates_ready", "attn_w_loaded", "wn_loaded0", "wn_loaded1", "wn_used", "heads_exp",
                 "heads_shifted", "heads_normed", "keys_masked", "values_spread", "values_used", "wo_loaded", "ffn_aux_loaded", "rope_ready", "tri_ready", "bias_loaded", "bias_added", "router_loaded", "out_stored1",
                 "vh_ones", "wq1_loaded", "pc_shift", "pc_exp", "silu_ready", "hx_ready",
                 "wxa_loaded", "wxb_loaded", "attn1_done", "out_stored", "x_final", "mask_ready",
                 "edge_ready", "norm_lo_ready", "w0_hi_ready", "w0_lo_ready", "hidden_lo_ready",
                 "wx_hi_ready", "wx_lo_ready", "hx_whole", "hx_hi_ready", "hx_lo_ready", "dve_link", "act_link", "pool_link", "ucol_ready", "shared_one")
        s = {name: sem(name) for name in names}
        ctx_loaded = [sem(f"ctx_loaded{i}") for i in range(4)]
        cw_moved = [sem(f"segment_rows_moved{i}") for i in range(SEG)]
        w0x_loaded = [sem(f"expert_w_loaded{i}") for i in range(NW0)]

        block = ctx.enter_context(nc.Block())

        def halves():
            for h in range(2):
                yield h, range(h * HB, h * HB + HB)

        def x_cols(h):
            return slice(h * HT, (h + 1) * HT)

        def tok(b):
            return slice(b * T, (b + 1) * T)

        def step_of(seg, g):
            return 2 * seg + 1 + g

        def turned(i):
            w, cq = i // 4, i % 4
            return QKVT[:, w].rearrange("p (t c) -> p c t", c=NH)[:, 4 * cq:4 * cq + 4, :]

        @block.sync
        def _(sp):
            x_d = A["x"].rearrange("b t d -> t b d")
            sp.dma_start(X[:, 0:HB, :], x_d[:, 0:HB, :]).then_inc(s["x_loaded0"], 16)
            sp.dma_start(X[:, HB:B, :], x_d[:, HB:B, :]).then_inc(s["x_loaded1"], 16)
            c_d = A["ctx_1024"].rearrange("b (c p) d -> p b c d", c=CH)
            for i in range(4):
                sp.dma_start(ctxN0[:, 6 * i:6 * i + 6, :].rearrange("p (b c) d -> p b c d", c=CH),
                             c_d[:, 2 * i:2 * i + 2]).then_inc(ctx_loaded[i], 16)
            sp.wait_ge(s["dsk_clear"], 1)
            for q4 in range(B // 2):
                sp.wait_ge(s["dist_ready"], q4 + 1)
                for b in (2 * q4, 2 * q4 + 1):
                    for g in range(G):
                        n = min(RC, S - g * RC)
                        dst = view(Dsk, g * KC * RC, [[RC, T], [1, n]], (g * B + b, g * B + b + 1))
                        src = Dd[:, b, g * RC:g * RC + n]
                        src = bass.AP(src.tensor, src.offset, [src.ap[0], [1, n]])
                        sp.dma_start(dst, src).then_inc(s["dist_moved"], 16)
            sp.wait_ge(s["edge_ready"], 1)
            for seg in range(SEG):
                for g in range(G):
                    n = min(RC, S - g * RC)
                    sp.wait_ge(s["dtw_step"], min(step_of(seg, g) + 1, STEPS))
                    q = seg * SC + g * KC
                    sp.dma_start(Rb[seg * B:(seg + 1) * B, :, 1 + g * RC:1 + g * RC + n],
                                 RS[g * B:(g + 1) * B, q:q + SC + 1, 1:1 + n]).then_inc(s["costs_moved"], 16)
            sp.wait_ge(s["compose_done"], 1)
            for seg in range(SEG - 1, 0, -1):
                sp.dma_start(Cw[:, seg, :], Cc[seg * B:(seg + 1) * B, (SC - 1) % 2, 1:S + 1])\
                    .then_inc(cw_moved[seg], 16)
            sp.wait_ge(s["esel_ready"], 1)
            for i in range(4):
                sp.dma_start(ctxN[:, 2 * i:2 * i + 2], c_d[:, 2 * i:2 * i + 2]).then_inc(s["ctx_reloaded"], 16)
            sp.wait_ge(free[dve], r_exp[-1].count)
            sp.dma_start(b2s, A["L0_ffn_b2"]).then_inc(s["ffn_aux_loaded"], 16)
            sp.dma_start(cs[:, 0, :], rows_of(A["L1_attn_cos"][T:T + 1, :], 128)).then_inc(s["attn_w_loaded"], 16)
            sp.dma_start(cs[:, 1, :], rows_of(A["L1_attn_sin"][T:T + 1, :], 128)).then_inc(s["attn_w_loaded"], 16)
            for w, name in enumerate(("bq", "bk", "bv", "bo")):
                sp.dma_start(bqkv[:, w, :], rows_of(A["L1_attn_" + name], 128)).then_inc(s["attn_w_loaded"], 16)
            for i, pair in enumerate((("wq", "wk"), ("wv", "wo"))):
                if i:
                    sp.wait_ge(s["wn_used"], 1)
                for w, name in enumerate(pair):
                    sp.dma_start(wn[:, w], A["L1_attn_" + name].rearrange("(r p) n -> p r n", p=128))\
                        .then_inc(s[f"wn_loaded{i}"], 16)
            sp.wait_ge(full, r_b2[-1].n + 1)
            sp.dma_start(bvB, rows_of(A["L1_xattn_bv"], T)).then_inc(s["bias_loaded"], 16)
            def load_expert(e, name):
                g, u, d = three(wx(e))
                if e < E1:
                    srcs = (A["L1_ffn_Wg"][e], A["L1_ffn_Wu"][e], A["L1_ffn_Wd"][e])
                else:
                    f = slice((e - E1) * F1, (e - E1 + 1) * F1)
                    srcs = (A["L1_ffn_Sg"][:, f], A["L1_ffn_Su"][:, f], A["L1_ffn_Sd"][f, :])
                sp.dma_start(g, srcs[0].rearrange("(k p) f -> p k f", p=128)).then_inc(s[name], 16)
                sp.dma_start(u, srcs[1].rearrange("(k p) f -> p k f", p=128)).then_inc(s[name], 16)
                sp.dma_start(d, srcs[2]).then_inc(s[name], 16)
            sp.wait_ge(full, r_dn0[2 * E0 - 1][-1].n + 1)
            for e in range(NF):
                load_expert(e, "wxa_loaded")
            sp.wait_ge(full, r_vh[-1].n + 1)
            sp.dma_start(wq1, A["L1_xattn_Wq"].rearrange("(k p) n -> p k n", p=128)).then_inc(s["wq1_loaded"], 16)
            sp.wait_ge(free[dve], r_wo[-1].count)
            for e in range(NF, NX):
                load_expert(e, "wxb_loaded")
            for b in range(B):
                if b % 2 == 0:
                    sp.wait_ge(free[dve], r_dn1[NX - 1][b // 2].count)
                sp.dma_start(out[b], X[:, b, :]).then_inc(s["out_stored"], 16)
            sp.wait_ge(s["out_stored"], 16 * B)

        @block.gpsimd
        def _(pool):
            link_n = [0]

            def link(ins):
                link_n[0] += 1
                ins.then_inc(s["pool_link"], 1)
                pool.wait_ge(s["pool_link"], link_n[0])

            link(nc.gpsimd.memset(ident[:], 0.0))
            nc.gpsimd.affine_select(out=ident[:], in_=ident[:], compare_op=ALU.not_equal, fill=1.0, base=0,
                                    pattern=[[-1, 128]], channel_multiplier=1).then_inc(s["ident_ready"], 1)
            nc.gpsimd.memset(ones[:], 1.0).then_inc(s["consts_ready"], 1)
            nc.gpsimd.memset(mhalf[:], -0.5).then_inc(s["consts_ready"], 1)
            link(nc.gpsimd.memset(cmask, 0.0))
            nc.gpsimd.affine_select(out=cmask, in_=cmask, compare_op=ALU.is_ge, fill=-BIG, base=0,
                                    pattern=[[-1, T]], channel_multiplier=1).then_inc(s["mask_ready"], 1)
            nc.gpsimd.iota(iota[:], pattern=[[1, S + 1]], base=-1, channel_multiplier=0,
                           allow_small_or_imprecise_dtypes=True).then_inc(s["consts_ready"], 1)
            link(nc.gpsimd.memset(esel[:], 1.0))
            nc.gpsimd.affine_select(out=esel[:].rearrange("p (s b) -> p s b", b=B),
                                    in_=esel[:].rearrange("p (s b) -> p s b", b=B),
                                    compare_op=ALU.is_equal, fill=0.0, base=0,
                                    pattern=[[0, SEG], [-1, B]], channel_multiplier=1).then_inc(s["consts_ready"], 1)
            def ln_root(n):
                for h in range(2):
                    cols = slice(h * HB, h * HB + HB)
                    pool.wait_ge(s["stats_ready"], 2 * n + h + 1)
                    link(nc.gpsimd.tensor_scalar(veps[:, cols], mv[:, cols, 1], EPS, None, ALU.add))
                    nc.gpsimd.tensor_tensor(rstd[:, cols], veps[:, cols], mhalf[:, cols], ALU.pow)\
                        .then_inc(s["rstd_ready"], 1)

            ln_root(0)
            pool.dma_start(brow[0:E0 * M0, :], A["L0_ffn_b1"].rearrange("e (m p) -> (e m) p", p=128))\
                .then_inc(s["aux_loaded"], 16)
            for w, name in enumerate(("bq", "bk")):
                lo = E0 * M0 + w * KD
                pool.dma_start(brow[lo:lo + KD, :], A["L1_xattn_" + name].rearrange("(k p) -> k p", p=128))\
                    .then_inc(s["aux_loaded"], 16)
            pool.dma_start(brb[:], rows_of(A["L0_ffn_br"], T)).then_inc(s["aux_loaded"], 16)
            pool.dma_start(wr0[:], A["L0_ffn_Wr"].rearrange("(k p) e -> p k e", p=128)).then_inc(s["router_loaded"], 16)
            pool.dma_start(wr1[:], A["L1_ffn_Wr"].rearrange("(k p) e -> p k e", p=128)).then_inc(s["router_loaded"], 16)

            pool.wait_ge(full, r_ctx[-1].n + 1)
            nc.gpsimd.memset(Dsk, BIG).then_inc(s["dsk_clear"], 1)
            ln_root(1)
            pool.wait_ge(full, ln_slots[1][-1].n + 1)
            pool.wait_ge(s["bb_ready"], 1)
            for w, name in enumerate(("Wk", "Wv")):
                pool.dma_start(wkv[:, w], A["L1_xattn_" + name].rearrange("(k p) n -> p k n", p=128))\
                    .then_inc(s["wkv_loaded"], 16)
            pool.wait_ge(free[dve], r_pv0[-1].count)
            pool.wait_ge(full, r_aa[-1].n + 1)
            link(nc.gpsimd.memset(big[0:G * B, o_rs:o_rb], BIG))
            nc.gpsimd.memset(RS[0:B, 0, 0:1], 0.0).then_inc(s["costs_clear"], 1)
            pool.wait_ge(s["dist_ready"], B // 2)
            nc.gpsimd.memset(Rb[:, :, 0:1], BIG).then_inc(s["edge_ready"], 1)
            def load_w0(e):
                r = e % NW0
                if e == 0:
                    pool.wait_ge(full, r_vc[-1].n + 1)
                if e >= NW0:
                    pool.wait_ge(s["w0_lo_ready"], e - NW0 + 1)
                pool.dma_start(W0f[:, r, 0:KD * F0].rearrange("p (k f) -> p k f", k=KD),
                               A["L0_ffn_W1"][e].rearrange("(k p) f -> p k f", p=128)).then_inc(w0x_loaded[r], 16)
                pool.dma_start(W0f[:, r, KD * F0:WN0].rearrange("p (m d) -> p m d", m=M0),
                               A["L0_ffn_W2"][e].rearrange("(m p) d -> p m d", p=128)).then_inc(w0x_loaded[r], 16)
            for e in range(NW0):
                load_w0(e)
            pool.wait_ge(s["choices_ready"], 2)
            rows = Ex.rearrange("p (c i) -> p c i", c=SC)
            nc.gpsimd.tensor_tensor(rows, dl[:, 0, :].rearrange("p (c i) -> p c i", c=SC),
                                    view(iota, 0, [[0, SC], [1, S]], (0, T)), ALU.mult)
            nc.gpsimd.tensor_tensor(T1.rearrange("p (c i) -> p c i", c=SC),
                                    dl[:, 1, :].rearrange("p (c i) -> p c i", c=SC),
                                    view(iota, 1, [[0, SC], [1, S]], (0, T)), ALU.mult).then_inc(s["exits_ready"], 1)
            pool.wait_ge(s["compose_done"], 1)
            link(nc.gpsimd.tensor_tensor(dl[:, 0, :], dl[:, 0, :], dl[:, 1, :], ALU.add))
            nc.gpsimd.tensor_scalar(U[:, 0:NS], dl[:, 0, :], -1.0, 1.0, ALU.mult, ALU.add)
            nc.gpsimd.memset(U[:, NS:NS + 1], 0.0).then_inc(s["ups_ready"], 1)
            pool.wait_ge(s["path_ready"], 2)
            link(nc.gpsimd.memset(tri, 1.0))
            nc.gpsimd.affine_select(out=tri, in_=tri, compare_op=ALU.is_gt, fill=0.0, base=0,
                                    pattern=[[1, E1], [-1, E1]], channel_multiplier=0).then_inc(s["tri_ready"], 1)
            def w0_lo(e):
                pool.wait_ge(s["w0_hi_ready"], e + 1)
                nc.gpsimd.tensor_tensor(W0s[:, e % 2, 1], W0f[:, e % NW0], W0s[:, e % 2, 0], ALU.subtract)\
                    .then_inc(s["w0_lo_ready"], 1)
            ln_root(2)
            w0_lo(0)
            w0_lo(1)
            for e in range(2, E0):
                load_w0(e)
                w0_lo(e)
            pool.wait_ge(full, r_dn0[2 * E0 - 1][-1].n + 1)
            pool.wait_ge(s["hidden_lo_ready"], 2 * M0 * E0)
            nc.gpsimd.memset(big[0:T, o_vz:o_px1], 0.0).then_inc(s["pool_link"], 1)
            link_n[0] += 1
            link(nc.gpsimd.memset(bmask, 1.0))
            link(nc.gpsimd.affine_select(out=bmask, in_=bmask, compare_op=ALU.is_ge, fill=0.0, base=0,
                                         pattern=[[-HD, B]], channel_multiplier=1))
            link(nc.gpsimd.affine_select(out=bmask, in_=bmask, compare_op=ALU.is_ge, fill=0.0, base=HD - 1,
                                         pattern=[[HD, B]], channel_multiplier=-1))

            def add_bias(n, tile, offset):
                pool.wait_ge(s["norm_ready"], (n + 1) * B)
                nc.gpsimd.tensor_tensor(X[:, :, :], X[:, :, :], view(tile, offset, [[0, B], [1, D]], (0, T)), ALU.add)\
                    .then_inc(s["bias_added"], 1)

            ln_root(3)
            pool.wait_ge(s["attn_w_loaded"], 96)
            add_bias(3, big, o_bq + 3 * D)
            pool.wait_ge(free[dve], r_hT[-1].count)
            pool.wait_ge(free[act], r_hT[-2].count)
            for n in range(NG + 2):
                h, g = n // 2, n % 2
                if n < NG:
                    if n >= 3:
                        pool.wait_ge(full, r_s1[n - 3].n + 1)
                    nc.gpsimd.tensor_tensor(Km[:, n % 3].rearrange("p (j n) -> p j n", j=HB),
                                            view(big, o_qt + (NH + h) * T, [[0, HB], [1, T]]),
                                            view(iota, g * HB, [[1, HB], [0, T]]), ALU.mult)\
                        .then_inc(s["keys_masked"], 1)
                if n >= 2 and g == 0:
                    h -= 1
                    if h == 0:
                        pool.wait_ge(free[act], r_vh[-1].count)
                    if h >= 2:
                        pool.wait_ge(s["values_used"], 2 * (h - 1))
                    dst = view(big, o_vz + h % 2 * VZ + 112, [[128, B], [1, HD]], (0, T))
                    nc.gpsimd.tensor_copy(dst, Vh[:, h].rearrange("p (b d) -> p b d", b=B)).then_inc(s["values_spread"], 1)
            ln_root(4)
            pool.wait_ge(s["bias_loaded"], 16)
            add_bias(4, big, o_b2)

            def wx_lo(e):
                pool.wait_ge(s["wx_hi_ready"], e + 1)
                nc.gpsimd.tensor_tensor(WXs[:, e % 4, 1], wx(e), WXs[:, e % 4, 0], ALU.subtract)\
                    .then_inc(s["wx_lo_ready"], 1)
            wx_lo(0)
            ln_root(5)
            for e in range(1, NX):
                wx_lo(e)

        @block.scalar
        def _(sc):
            link_n = [0]

            def link(ins):
                link_n[0] += 1
                ins.then_inc(s["act_link"], 1)
                sc.wait_ge(s["act_link"], link_n[0])

            def copy(slot, dst, src, func=ACT.Copy, **kw):
                sc.wait_ge(full, slot.n + 1)
                return nc.scalar.activation(dst, src, func, **kw).then_inc(free[act], 1)

            def bank(slot):
                return ps[:, slot.bank, :]

            def ln_turned(n, parts=None):
                for i, slot in enumerate(ln_slots[n]):
                    h, k = i // KD, i % KD
                    if parts is not None:
                        sc.wait_ge(full, slot.n + 1)
                        nc.scalar.activation(parts[0][:, k, x_cols(h)], bank(slot)[:, 0:HT], ACT.Copy)
                    copy(slot, NT[:, k, x_cols(h)], bank(slot)[:, 0:HT])

            for w, name in enumerate(("Wq", "Wk", "Wv")):
                sc.dma_start(w0[:, w], A["L0_attn_" + name].rearrange("(k p) n -> p k n", p=128))\
                    .then_inc(s["w0_loaded"], 16)

            def ctx_turned(lo, hi):
                for i in range(lo, hi):
                    q, k = i // KD, i % KD
                    copy(r_ctx[i], ctxT[:, k, q * TC:(q + 1) * TC], bank(r_ctx[i])[:, 0:TC])

            ln_turned(0)
            i = 0
            for w in range(2):
                for m in range(KD):
                    for h in range(2):
                        copy(r_qk0[i], qkT0[:, w, m, x_cols(h)], bank(r_qk0[i])[:, 0:HT])
                        i += 1
            for i, slot in enumerate(r_v0):
                copy(slot, V0[:, 2 * i:2 * i + 2, :], bank(slot)[0:T, :].rearrange("p (b d) -> p b d", b=2))
            for h, bs in halves():
                ctx_turned(2 * h, 2 * h + 2)
                sc.wait_ge(s["s0_ready"], h + 1)
                for b in bs:
                    nc.scalar.activation(P0[:, b, :], P0[:, b, :], ACT.Exp, bias=mx[:, 1, b:b + 1],
                                         accum_out=rs[:, 0, b:b + 1]).then_inc(s["p0_exp"], 1)
            nc.scalar.preload_act_table_set("natural_log_exp_and_others")
            ctx_turned(4, KD * NQ)
            copy(r_bias, bcol[:, :], bank(r_bias)[:, 0:NB])

            def squares(q):
                if q >= 2:
                    sc.wait_ge(full, r_aa[q - 2].n + 1)
                if q == 0:
                    sc.wait_ge(free[act], r_ctx[-1].count)
                nc.scalar.activation(csq[:, q % 2], ctxT[:, :, q * TC:(q + 1) * TC], ACT.Square)\
                    .then_inc(s["csq_ready"], 1)

            def norms(q):
                lo = q * TC
                copy(r_aa[q], Vc_r[0:T, B * S + lo:B * S + lo + TC], bank(r_aa[q])[0:T, 0:TC])
            squares(0)
            squares(1)
            for q in range(AA_CUT):
                norms(q)
                squares(q + 2)
            for b in range(B):
                sc.wait_ge(s["norm_ready"], B + b + 1)
                link(nc.scalar.activation(junk2[:, :], N[:, b, :], ACT.Square, accum_out=bb[:, b:b + 1]))
            sc.sem_inc(s["bb_ready"], 1)
            ln_turned(1)
            for q in range(AA_CUT, NQ):
                norms(q)
            for q4 in range(B // 2):
                sl = slice(2 * q4, 2 * q4 + 2)
                sc.wait_ge(s["ln_arg"], q4 + 1)
                link(nc.scalar.activation(inv[:, sl, :], inv[:, sl, :], ACT.Ln))
                link(nc.scalar.activation(inv[:, sl, :], inv[:, sl, :], ACT.Exp, scale=-0.5))
                nc.scalar.activation(aaB[:, sl, :], inv[:, sl, :], ACT.Square).then_inc(s["inv_ready"], 1)
            sc.wait_ge(free[act], r_bias.count)
            i = 0
            for m in range(KD):
                for q in range(NQ):
                    copy(r_kc[i], KcT[:, m, q * TC:(q + 1) * TC], bank(r_kc[i])[:, 0:TC], ACT.Identity,
                         bias=bqk[:, 1, m:m + 1])
                    i += 1
            sc.wait_ge(s["dist_moved"], 16 * B * G)
            for i, slot in enumerate(r_vc):
                copy(slot, Vc_r[0:CR, 2 * i * D:(2 * i + 2) * D], bank(slot)[0:CR, :])
            for i, slot in enumerate(r_ptm):
                if slot.reader == act:
                    h, c4 = i % CH, 1 - i // CH
                    copy(slot, PTs[:, h, :, :, 4 * c4:4 * c4 + 4].rearrange("p b s c -> p c s b"),
                         bank(slot)[0:CR, 0:4 * T].rearrange("p (c s b) -> p c s b", c=4, s=SEG))

            def w0_hi(e):
                if e < 2:
                    sc.wait_ge(full, r_exp[-1].n + 1)
                else:
                    sc.wait_ge(full, r_dn0[2 * (e - 2) + 1][-1].n + 1)
                sc.wait_ge(w0x_loaded[e % NW0], 32 * (e // NW0 + 1))
                nc.scalar.activation(W0s[:, e % 2, 0], W0f[:, e % NW0], ACT.Copy).then_inc(s["w0_hi_ready"], 1)
            w0_hi(0)
            w0_hi(1)
            ln_turned(2, NTs0)

            def up0(u):
                e, r = u // 2, u % 2
                if u >= 2:
                    sc.wait_ge(full, r_dn0[u - 2][-1].n + 1)
                for m, slot in enumerate(r_up0[u]):
                    sc.wait_ge(full, slot.n + 1)
                    nc.scalar.activation(hs[:, r, 0, m], bank(slot)[:, 0:HT], ACT.Relu, bias=b1c[:, e, m:m + 1])
                    if u:
                        sc.wait_ge(s["hidden_lo_ready"], M0 * (u - 1) + m + 1)
                    copy(slot, hf[:, m], bank(slot)[:, 0:HT], ACT.Relu, bias=b1c[:, e, m:m + 1])

            def gate_exp(n):
                E = (E0, E1)[n]
                sc.wait_ge(s["logits_ready"], n + 1)
                nc.scalar.activation(gp[:, :, 0:E], gl[:, :, 0:E], ACT.Exp).then_inc(s["logits_exp"], 1)
            gate_exp(0)
            up0(0)
            for i, slot in enumerate(r_cwt):
                copy(slot, cwT[:, x_cols(i)], bank(slot)[0:E0, 0:HT])
            for w, slot in enumerate(r_wt):
                copy(slot, wT[:, :, w, :], bank(slot).rearrange("p (k n) -> p k n", k=KD))
            for u in range(1, 2 * E0):
                up0(u)
                if u % 2 == 0 and u // 2 + 1 < E0:
                    w0_hi(u // 2 + 1)
            ln_turned(3)
            for i, slot in enumerate(r_hT):
                if slot.reader == act:
                    copy(slot, turned(i), bank(slot)[:, 0:4 * T].rearrange("p (c t) -> p c t", c=4))
            for i, slot in enumerate(r_vh):
                copy(slot, Vh[:, 4 * i:4 * i + 4, :], bank(slot)[0:T, :].rearrange("p (h n) -> p h n", h=4))
            for n in range(NG + LV):
                if n < NG:
                    sc.wait_ge(s["heads_shifted"], n + 1)
                    if n >= NP:
                        sc.wait_ge(full, r_pt1[n - NP].n + 1)
                    for j in range(HB):
                        ins = nc.scalar.activation(
                            Px[:, n % NP, j * T:(j + 1) * T], bank(r_s1[n])[0:T, j * T:(j + 1) * T], ACT.Exp,
                            bias=hm[:, n % NP, 1, j:j + 1], scale=HD ** -0.5, accum_out=hm[:, n % NP, 2, j:j + 1])
                    ins.then_inc(free[act], 1)
                if LT <= n < NG + LT:
                    m = n - LT
                    if m >= 3:
                        sc.wait_ge(s["values_used"], m - 2)
                    copy(r_pt1[m], PxT[:, m % 3], bank(r_pt1[m])[0:T, 0:HT])
                if n >= LV:
                    h, g = (n - LV) // 2, (n - LV) % 2
                    if h % 8 == 7:
                        copy(r_o1[h // 8, g], NT[:, h // 8, x_cols(g)], bank(r_o1[h // 8, g])[:, 0:HT])
            ln_turned(4)
            i = 0
            for m in range(KD):
                for h in range(2):
                    copy(r_qx[i], qxT[:, m, x_cols(h)], bank(r_qx[i])[:, 0:HT], ACT.Identity, bias=bqk[:, 0, m:m + 1])
                    i += 1
            for b in range(B + 1):
                if b < B:
                    sc.wait_ge(s["pc_shift"], b + 1)
                    if b >= 2:
                        sc.wait_ge(full, r_ptc[b - 2].n + 1)
                    copy(r_sc[b], Pc[:, b % 2], bank(r_sc[b])[0:T, 0:S], ACT.Exp,
                         bias=mx[:, 1, b:b + 1], scale=D ** -0.5, accum_out=rs[:, 0, b:b + 1])
                if b >= 1:
                    if b >= 3:
                        sc.wait_ge(full, r_oc[b - 3].n + 1)
                    copy(r_ptc[b - 1], PcT[:, (b - 1) % 2],
                         bank(r_ptc[b - 1])[0:CR, 0:CH * T].rearrange("p (h n) -> p h n", h=CH))
            def wx_hi(e):
                if e < 4:
                    sc.wait_ge(full, r_oc[B - 1].n + 1)
                else:
                    sc.wait_ge(full, r_dn1[e - 4][-1].n + 1)
                if e == 0:
                    sc.wait_ge(s["wxa_loaded"], 48 * NF)
                if e == NF:
                    sc.wait_ge(s["wxb_loaded"], 48 * (NX - NF))
                nc.scalar.activation(WXs[:, e % 4, 0], wx(e), ACT.Copy).then_inc(s["wx_hi_ready"], 1)
            wx_hi(0)
            wx_hi(1)
            ln_turned(5, NTs1)
            gate_exp(1)
            for e in range(NX):
                for h in range(2):
                    if e >= 2:
                        sc.wait_ge(free[dve], r_up1[e - 2][2 * h + 1].count)
                    copy(r_up1[e][2 * h], sg[:, e % 2, x_cols(h)], bank(r_up1[e][2 * h])[:, 0:HT], ACT.Silu)
                if e + 2 < NX:
                    wx_hi(e + 2)
                if e >= 2:
                    sc.wait_ge(full, r_dn1[e - 2][-1].n + 1)
                for h in range(2):
                    sc.wait_ge(free[dve], r_up1[e][2 * h + 1].count)
                    nc.scalar.activation(hxs[0][:, e % 2, x_cols(h)], hx[:, e % 2, x_cols(h)], ACT.Copy)\
                        .then_inc(s["hx_hi_ready"], 1)

        @block.tensor
        def _(pe):
            def bank(slot):
                if slot.before is not None:
                    pe.wait_ge(free[slot.before.reader], slot.before.count)
                return ps[:, slot.bank, :]

            def mm(dst, lhsT, rhs, first=True, last=True):
                return nc.tensor.matmul(dst, lhsT, rhs, start=first, stop=last)

            def turn(dst, src, n):
                return nc.tensor.transpose(dst, src, ident[0:n, 0:n])

            def filled(ins):
                ins.then_inc(full, 1)

            def ln_turn(n):
                for i, slot in enumerate(ln_slots[n]):
                    h, k = i // KD, i % KD
                    pe.wait_ge(s["norm_ready"], n * B + (h + 1) * HB)
                    dst = bank(slot)
                    for j in range(HB):
                        m = turn(dst[:, j * T:(j + 1) * T], N[:, h * HB + j, k * 128:(k + 1) * 128], T)
                    filled(m)

            def wait_act(slot):
                pe.wait_ge(free[act], slot.count)

            def wait_dve(slot):
                pe.wait_ge(free[dve], slot.count)

            def ctx_turn(lo, hi):
                for i in range(lo, hi):
                    q, k = i // KD, i % KD
                    for l in range(2 * q // 3, (4 * q + 3) // 6 + 1):
                        pe.wait_ge(ctx_loaded[l], 16)
                    dst = bank(r_ctx[i])
                    for j in range(4):
                        m = turn(dst[:, j * CR:(j + 1) * CR], ctxN0[:, 4 * q + j, k * 128:(k + 1) * 128], CR)
                    filled(m)

            pe.wait_ge(s["ident_ready"], 1)
            ln_turn(0)
            pe.wait_ge(s["w0_loaded"], 48)
            wait_act(ln_slots[0][-1])
            i = 0
            for w in range(2):
                for m in range(KD):
                    for h in range(2):
                        dst = bank(r_qk0[i])[:, 0:HT]
                        for k in range(KD):
                            last = mm(dst, w0[:, w, k, m * 128:(m + 1) * 128], NT[:, k, x_cols(h)], k == 0, k == KD - 1)
                        filled(last)
                        i += 1
            for i, slot in enumerate(r_v0):
                dst = bank(slot)
                for j in range(2):
                    for k in range(KD):
                        last = mm(dst[0:T, j * D:(j + 1) * D], NT[:, k, tok(2 * i + j)], w0[:, 2, k, :],
                                  k == 0, k == KD - 1)
                filled(last)
            wait_act(r_qk0[-1])
            for i, slot in enumerate(r_s0):
                dst = bank(slot)
                for j in range(HB):
                    b = i * HB + j
                    for k in range(KD):
                        last = mm(dst[0:T, j * T:(j + 1) * T], qkT0[:, 0, k, tok(b)], qkT0[:, 1, k, tok(b)],
                                  k == 0, k == KD - 1)
                filled(last)
            def norms(lo, hi):
                for q in range(lo, hi):
                    pe.wait_ge(s["csq_ready"], q + 1)
                    dst = bank(r_aa[q])
                    for k in range(KD):
                        last = mm(dst[0:T, 0:TC], ones[:, :], csq[:, q % 2, k, :], k == 0, k == KD - 1)
                    filled(last)

            ctx_turn(0, CTX_CUTS[0])
            for i, slot in enumerate(r_pt0):
                pe.wait_ge(s["p0_exp"], (i + 1) * HB)
                dst = bank(slot)
                for j in range(HB):
                    last = turn(dst[0:T, j * T:(j + 1) * T], P0[:, i * HB + j, :], T)
                filled(last)
            ctx_turn(*CTX_CUTS)
            wait_act(r_v0[-1])
            for i, slot in enumerate(r_pv0):
                wait_dve(r_pt0[i // 2])
                dst = bank(slot)
                for j in range(2):
                    b = 2 * i + j
                    last = mm(dst[0:T, j * D:(j + 1) * D], PT0[:, b, :], V0[:, b, :])
                filled(last)
            ctx_turn(CTX_CUTS[1], KD * NQ)
            pe.wait_ge(s["aux_loaded"], 64)
            filled(turn(bank(r_bias)[:, 0:NB], brow, NB))
            pe.wait_ge(s["consts_ready"], 1)
            norms(0, AA_CUT)
            ln_turn(1)
            norms(AA_CUT, NQ)
            wait_act(ln_slots[1][-1])
            for b, slot in enumerate(r_dist):
                dst = bank(slot)[0:T, 0:S]
                for k in range(KD):
                    last = mm(dst, NT[:, k, tok(b)], ctxT[:, k, b * S:(b + 1) * S], k == 0, k == KD - 1)
                filled(last)
            pe.wait_ge(s["wkv_loaded"], 32)
            i = 0
            for m in range(KD):
                for q in range(NQ):
                    dst = bank(r_kc[i])[:, 0:TC]
                    for k in range(KD):
                        last = mm(dst, wkv[:, 0, k, m * 128:(m + 1) * 128], ctxT[:, k, q * TC:(q + 1) * TC],
                                  k == 0, k == KD - 1)
                    filled(last)
                    i += 1
            for i, slot in enumerate(r_vc):
                dst = bank(slot)
                for j in range(2):
                    lo = (2 * i + j) * CR
                    for k in range(KD):
                        last = mm(dst[0:CR, j * D:(j + 1) * D], ctxT[:, k, lo:lo + CR], wkv[:, 1, k, :],
                                  k == 0, k == KD - 1)
                filled(last)
            pe.wait_ge(s["esel_ready"], 1)
            filled(mm(bank(r_e[0])[0:T, 0:1], esel[:, :], ones[0:B, 0:1]))
            for i, slot in enumerate(r_ptm):
                h, c4 = i % CH, 1 - i // CH
                pe.wait_ge(s["path_ready"], 2 - c4)
                dst = bank(slot)
                for j in range(4):
                    c = 4 * c4 + j
                    last = turn(dst[0:CR, j * T:(j + 1) * T], Pm[:, c * S + h * CR:c * S + (h + 1) * CR], T)
                filled(last)
            pe.wait_ge(s["ctx_reloaded"], 64)
            wait_act(r_ptm[4])
            wait_dve(r_ptm[5])
            for i, slot in enumerate(r_exp):
                dst = bank(slot)
                for j in range(2):
                    b = 2 * i + j
                    for h in range(CH):
                        last = mm(dst[0:T, j * D:(j + 1) * D], PTs[:, h, b].rearrange("p s c -> p (s c)"),
                                  ctxN[:, b, h, :], h == 0, h == CH - 1)
                filled(last)
            ln_turn(2)

            def gate_logits(slot, wr, E):
                dst = bank(slot)
                for b in range(B):
                    for k in range(KD):
                        last = mm(dst[0:T, b * E:(b + 1) * E], NT[:, k, tok(b)], wr[:, k, :], k == 0, k == KD - 1)
                filled(last)

            def split_mm(dst, lhsT, rhs, K):
                todo = [(a, b, k) for a, b in ((0, 0), (1, 0), (0, 1)) for k in range(K)]
                for i, (a, b, k) in enumerate(todo):
                    last = mm(dst, lhsT(a, k), rhs(b, k), i == 0, i == len(todo) - 1)
                return last

            def up0(u):
                e, h = u // 2, u % 2
                r = e % 2
                pe.wait_ge(s["w0_lo_ready"], e + 1)
                pe.wait_ge(s["norm_lo_ready"], KD * min(h + e + 1, 2))
                for m, slot in enumerate(r_up0[u]):
                    filled(split_mm(bank(slot)[:, 0:HT], lambda a, k: W1s[:, r, a, k, m * 128:(m + 1) * 128],
                                    lambda a, k: NTs0[a][:, k, x_cols(h)], KD))

            def down0(u):
                e, h = u // 2, u % 2
                pe.wait_ge(s["hidden_lo_ready"], M0 * (u + 1))
                for i, slot in enumerate(r_dn0[u]):
                    dst = bank(slot)
                    for j in range(2):
                        last = split_mm(dst[0:T, j * D:(j + 1) * D], lambda a, m: hs[:, u % 2, a, m, tok(2 * i + j)],
                                        lambda a, m: W2s[:, e % 2, a, m, :], M0)
                    filled(last)

            wait_act(ln_slots[2][-1])
            pe.wait_ge(s["router_loaded"], 32)
            gate_logits(r_g0[0], wr0, E0)
            up0(0)
            pe.wait_ge(s["gates_ready"], 1)
            for i, slot in enumerate(r_cwt):
                dst = bank(slot)
                for j in range(HB):
                    last = turn(dst[0:E0, j * T:(j + 1) * T], cw[:, i * HB + j, 0:E0], T)
                filled(last)
            wait_act(r_cwt[-1])
            pe.wait_ge(s["ffn_aux_loaded"], 16)
            for i, slot in enumerate(r_b2):
                dst = bank(slot)
                for j in range(2):
                    last = mm(dst[0:T, j * D:(j + 1) * D], cwT[:, tok(2 * i + j)], b2s[:, :])
                filled(last)
            for w, slot in enumerate(r_wt):
                if w % 2 == 0:
                    pe.wait_ge(s[f"wn_loaded{w // 2}"], 32)
                dst = bank(slot).rearrange("p (k n) -> p k n", k=KD)
                for k in range(KD):
                    for r in range(KD):
                        last = turn(dst[:, k, r * 128:(r + 1) * 128], wn[:, w % 2, r, k * 128:(k + 1) * 128], 128)
                filled(last)
                if w == 1:
                    pe.wait_ge(full, slot.n + 1)
                    pe.sem_inc(s["wn_used"], 1)
            for u in range(1, 2 * E0 + 1):
                if u < 2 * E0:
                    up0(u)
                down0(u - 1)
            ln_turn(3)
            wait_act(ln_slots[3][-1])
            pe.wait_ge(s["rope_ready"], 1)
            for i, slot in enumerate(r_qkv):
                b = i // 2
                cols = slice(0, 2 * D) if i % 2 == 0 else slice(2 * D, 3 * D)
                dst = bank(slot)[0:T, 0:cols.stop - cols.start]
                for k in range(KD):
                    last = mm(dst, NT[:, k, tok(b)], wT[:, k].rearrange("p w n -> p (w n)")[:, cols],
                              k == 0, k == KD - 1)
                filled(last)
            wait_dve(r_qkv[-1])
            for i, slot in enumerate(r_hT):
                dst = bank(slot)
                for j in range(4):
                    lo = o_qkv + (4 * i + j) * 128
                    last = turn(dst[:, j * T:(j + 1) * T], big[0:T, lo:lo + 128], T)
                filled(last)
            wait_act(r_hT[-2])
            wait_dve(r_hT[-1])
            for i, slot in enumerate(r_vh):
                dst = bank(slot)
                for j in range(4):
                    h = 4 * i + j
                    last = turn(dst[0:T, j * 128:(j + 1) * 128], QKVT[:, 2, h * T:(h + 1) * T], 128)
                filled(last)
            for n in range(NG + LV):
                if n < NG:
                    h = n // 2
                    pe.wait_ge(s["keys_masked"], n + 1)
                    filled(mm(bank(r_s1[n])[0:T, 0:HT], QKVT[:, 0, h * T:(h + 1) * T], Km[:, n % 3]))
                if LT <= n < NG + LT:
                    m = n - LT
                    pe.wait_ge(s["heads_normed"], m + 1)
                    dst = bank(r_pt1[m])
                    for j in range(4):
                        last = turn(dst[0:T, j * T:(j + 1) * T], Px[:, m % NP, j * T:(j + 1) * T], T)
                    filled(last)
                if n >= LV:
                    m = n - LV
                    h, g = m // 2, m % 2
                    slot = r_o1[h // 8, g]
                    pe.wait_ge(s["values_spread"], h + 1)
                    wait_act(r_pt1[m])
                    dst = bank(slot) if h % 8 == 0 else ps[:, slot.bank, :]
                    for j in range(HB):
                        lo = 112 + (g * HB + j) * 128 - h % 8 * HD
                        last = mm(dst[:, j * T:(j + 1) * T], Vz[:, h % 2, lo:lo + 128], PxT[:, m % 3, j * T:(j + 1) * T],
                                  h % 8 == 0 and j == 0, h % 8 == 7 and j == HB - 1)
                    if h % 8 == 7:
                        filled(last)
                        pe.wait_ge(full, slot.n + 1)
                        pe.sem_inc(s["values_used"], 1)
                    else:
                        last.then_inc(s["values_used"], 1)
            wait_act(r_o1[1, 1])
            for i, slot in enumerate(r_wo):
                dst = bank(slot)
                for j in range(2):
                    for k in range(KD):
                        last = mm(dst[0:T, j * D:(j + 1) * D], NT[:, k, tok(2 * i + j)], wT[:, k, 3, :],
                                  k == 0, k == KD - 1)
                filled(last)
            ln_turn(4)
            wait_act(ln_slots[4][-1])
            pe.wait_ge(s["wq1_loaded"], 16)
            i = 0
            for m in range(KD):
                for h in range(2):
                    dst = bank(r_qx[i])[:, 0:HT]
                    for k in range(KD):
                        last = mm(dst, wq1[:, k, m * 128:(m + 1) * 128], NT[:, k, x_cols(h)], k == 0, k == KD - 1)
                    filled(last)
                    i += 1
            wait_act(r_qx[-1])
            for n in range(B + 2):
                if n < B:
                    dst = bank(r_sc[n])[0:T, 0:S]
                    for k in range(KD):
                        last = mm(dst, qxT[:, k, tok(n)], KcT[:, k, n * S:(n + 1) * S], k == 0, k == KD - 1)
                    filled(last)
                if 1 <= n <= B:
                    wait_act(r_sc[n - 1])
                    dst = bank(r_ptc[n - 1])
                    for h in range(CH):
                        last = turn(dst[0:CR, h * T:(h + 1) * T], Pc[:, (n - 1) % 2, h * CR:(h + 1) * CR], T)
                    filled(last)
                if n >= 2:
                    wait_act(r_ptc[n - 2])
                    dst = bank(r_oc[n - 2])[0:T, 0:D]
                    for h in range(CH):
                        last = mm(dst, PcT[:, n % 2, h, :], Vc[:, n - 2, h, :], h == 0, h == CH - 1)
                    filled(last)
            ln_turn(5)
            wait_act(ln_slots[5][-1])
            gate_logits(r_g1[0], wr1, E1)
            for e in range(NX + 1):
                if e < NX:
                    w = [three(WXs[:, e % 4, a]) for a in range(2)]
                    pe.wait_ge(s["wx_lo_ready"], e + 1)
                    if e == 0:
                        pe.wait_ge(s["norm_lo_ready"], 4 * KD)
                    for i, slot in enumerate(r_up1[e]):
                        h, gu = i // 2, i % 2
                        filled(split_mm(bank(slot)[:, 0:HT], lambda a, k: w[a][gu][:, k, :],
                                        lambda a, k: NTs1[a][:, k, x_cols(h)], KD))
                if e:
                    f = e - 1
                    w = [three(WXs[:, f % 4, a]) for a in range(2)]
                    for i, slot in enumerate(r_dn1[f]):
                        pe.wait_ge(s["hx_lo_ready"], 2 * f + i // 2 + 1)
                        dst = bank(slot)
                        for j in range(2):
                            last = split_mm(dst[0:T, j * D:(j + 1) * D],
                                            lambda a, k: hxs[a][:, f % 2, tok(2 * i + j)], lambda a, k: w[a][2], 1)
                        filled(last)

        @block.vector
        def _(ve):
            link_n = [0]

            def link(ins):
                link_n[0] += 1
                ins.then_inc(s["dve_link"], 1)
                ve.wait_ge(s["dve_link"], link_n[0])

            v = nc.vector

            def bank(slot):
                ve.wait_ge(full, slot.n + 1)
                return ps[:, slot.bank, :]

            def empty(slot, ins):
                ins.then_inc(free[dve], 1)

            def ln_stats(n, h, x_ready=None):
                bs = range(h * HB, (h + 1) * HB)
                for b in bs:
                    if x_ready:
                        x_ready(b)
                    ins = v.bn_stats(stats[:, b, :], X[:, b, :])
                link(ins)
                for b in bs:
                    ins = v.bn_aggr(mv[:, b, :], stats[:, b, :])
                ins.then_inc(s["stats_ready"], 1)

            def ln_norm(n, h):
                ve.wait_ge(s["rstd_ready"], 2 * n + h + 1)
                for b in range(h * HB, (h + 1) * HB):
                    v.tensor_scalar(N[:, b, :], X[:, b, :], mv[:, b, 0:1], rstd[:, b:b + 1],
                                    ALU.subtract, ALU.mult).then_inc(s["norm_ready"], 1)

            for h in range(2):
                ln_stats(0, h, lambda b: ve.wait_ge(s[f"x_loaded{b // HB}"], 16))
            for h in range(2):
                ln_norm(0, h)
            ve.wait_ge(s["mask_ready"], 1)
            for i, slot in enumerate(r_s0):
                bs = slice(i * HB, (i + 1) * HB)
                src = bank(slot)[0:T, 0:HT].rearrange("p (b n) -> p b n", b=HB)
                ins = v.scalar_tensor_tensor(P0[:, bs, :], src, D ** -0.5, view(cmask, 0, [[0, HB], [1, T]]),
                                             ALU.mult, ALU.add)
                empty(slot, ins)
                ve.wait_ge(free[dve], slot.count)
                link(v.tensor_reduce(mx[:, 0, bs], P0[:, bs, :], AX_X, ALU.max))
                v.tensor_scalar(mx[:, 1, bs], mx[:, 0, bs], -1.0, None, ALU.mult).then_inc(s["s0_ready"], 1)
            for i, slot in enumerate(r_pt0):
                bs = slice(i * HB, (i + 1) * HB)
                empty(slot, v.tensor_copy(PT0[:, bs, :], bank(slot)[0:T, 0:HT].rearrange("p (b n) -> p b n", b=HB)))
            ve.wait_ge(s["p0_exp"], B)
            link(v.reciprocal(rs[:, 1, :], rs[:, 0, :]))
            for i, slot in enumerate(r_pv0):
                src = bank(slot)
                for j in range(2):
                    b = 2 * i + j
                    ins = v.scalar_tensor_tensor(X[:, b, :], src[0:T, j * D:(j + 1) * D], rs[:, 1, b:b + 1],
                                                 X[:, b, :], ALU.mult, ALU.add)
                empty(slot, ins)
                if i % 2:
                    ln_stats(1, i // 2, lambda b: ve.wait_ge(free[dve], r_pv0[b // 2].count))
            ve.wait_ge(full, ln_slots[0][-1].n + 1)
            for h in range(2):
                ln_norm(1, h)
            ve.wait_ge(s["bb_ready"], 1)

            def distances(q4):
                ve.wait_ge(free[act], r_aa[((2 * q4 + 2) * S - 1) // TC].count)
                for b in (2 * q4, 2 * q4 + 1):
                    ins = v.tensor_scalar(aaB[:, b, :], aaB[:, b, :], bb[:, b:b + 1], None, ALU.add)
                link(ins)
                for b in (2 * q4, 2 * q4 + 1):
                    slot = r_dist[b]
                    empty(slot, v.scalar_tensor_tensor(Dd[:, b, :], bank(slot)[0:T, 0:S], -2.0, aaB[:, b, :],
                                                       ALU.mult, ALU.add))
                ve.wait_ge(free[dve], slot.count)
                hb = slice(2 * q4, 2 * q4 + 2)
                v.tensor_scalar(inv[:, hb, :], Dd[:, hb, :], TINY, None, ALU.max).then_inc(s["ln_arg"], 1)

            def roots(q4):
                hb = slice(2 * q4, 2 * q4 + 2)
                d, r, z = Dd[:, hb, :], inv[:, hb, :], aaB[:, hb, :]
                ve.wait_ge(s["inv_ready"], q4 + 1)
                link(v.scalar_tensor_tensor(z, z, -0.5, d, ALU.mult, ALU.mult))
                link(v.scalar_tensor_tensor(d, d, 0.0, r, ALU.max, ALU.mult))
                v.scalar_tensor_tensor(d, z, 1.5, d, ALU.add, ALU.mult).then_inc(s["dist_ready"], 1)

            distances(0)
            for q4 in range(B // 2):
                if q4 + 1 < B // 2:
                    distances(q4 + 1)
                roots(q4)
            ve.wait_ge(s["costs_clear"], 1)
            ve.wait_ge(s["dist_moved"], 16 * B * G)
            for t in range(STEPS):
                for k in range(KC):
                    q = t * KC + k + 1
                    link(v.tensor_tensor(mtmp[:, :], RS[:, q - 1, 0:RC], RS[:, q - 1, 1:RC + 1], ALU.min))
                    ins = v.tensor_tensor_scan(RS[:, q, 1:RC + 1], mtmp[:, :], Dsk[:, (q - 1) * RC:q * RC],
                                               RS[:, q, 0:1], ALU.min, ALU.add)
                    if k < KC - 1:
                        link(ins)
                ins.then_inc(s["dtw_step"], 1)
                ve.wait_ge(s["dtw_step"], t + 1)
                if t < STEPS - 1:
                    link(v.stream_shuffle(RS[:, q + 1:q + KC + 1, 0], RS[:, q - KC + 1:q + 1, RC],
                                          [(p - B) % 32 for p in range(32)]))
            link(v.memset(Cc[:, :, 0:1], 0.0))
            link(v.memset(einb[:, SEG - 1:SEG], float(S - 1)))
            ve.wait_ge(s["costs_moved"], 16 * SEG * G)
            cd, cu, cl = Rb[:, 0:SC, 0:S], Rb[:, 1:SC + 1, 0:S], Rb[:, 0:SC, 1:S + 1]
            m1v = m1.rearrange("p (c i) -> p c i", c=SC)
            diag, left = (dl[:, a, :].rearrange("p (c i) -> p c i", c=SC) for a in range(2))
            link(v.tensor_tensor(m1v, cu, cl, ALU.min))
            link(v.tensor_tensor(diag, cd, m1v, ALU.is_le))
            link(v.tensor_tensor(m1v, cu, cd, ALU.min))
            v.tensor_tensor(left, cl, m1v, ALU.is_lt).then_inc(s["choices_ready"], 2)
            ve.wait_ge(s["choices_ready"], 2)
            for c in range(SC):
                w = view(iota, 0, [[1, 2], [1, S]], (0, T)) if c == 0 else \
                    view(big, o_cc + (c - 1) % 2 * (S + 1), [[1, 2], [1, S]], (0, T))
                link(v.tensor_tensor(Tt, dl[:, :, c * S:(c + 1) * S], w, ALU.mult))
                ins = v.tensor_tensor_scan(Cc[:, c % 2, 1:S + 1], Tt[:, 0, :], Tt[:, 1, :], 0.0, ALU.max, ALU.max)
                if c < SC - 1:
                    link(ins)
            ins.then_inc(s["compose_done"], 1)
            ve.wait_ge(s["compose_done"], 1)
            ve.wait_ge(s["exits_ready"], 1)
            for c in range(SC):
                ins = v.tensor_tensor_scan(Ex[:, c * S:(c + 1) * S], Ex[:, c * S:(c + 1) * S], T1[:, c * S:(c + 1) * S],
                                           0.0, ALU.max, ALU.max)
            link(ins)
            for g in range(SEG - 1, 0, -1):
                ve.wait_ge(cw_moved[g], 16)
                link(v.scalar_tensor_tensor(junk[0:B, :], iota[0:B, 1:S + 1], einb[:, g:g + 1], Cw[:, g, :],
                                            ALU.is_equal, ALU.mult, accum_out=einb[:, g - 1:g]))
            ve.wait_ge(s["consts_ready"], 4)
            v.tensor_tensor(esel[:].rearrange("p (s b) -> p s b", b=B), esel[:].rearrange("p (s b) -> p s b", b=B),
                            view(einb, 0, [[1, SEG], [0, B]]), ALU.mult).then_inc(s["esel_ready"], 1)
            empty(r_e[0], v.tensor_copy(ecol[:, SC - 1:SC], bank(r_e[0])[0:T, 0:1]))
            ve.wait_ge(free[dve], r_e[0].count)
            for c in range(SC - 1, -1, -1):
                ins = v.tensor_scalar(OH[:, c * S:(c + 1) * S], iota[0:T, 1:S + 1], ecol[:, c:c + 1], None, ALU.is_equal)
                if c:
                    ins = v.scalar_tensor_tensor(junk[:, :], iota[0:T, 1:S + 1], ecol[:, c:c + 1],
                                                 Ex[:, c * S:(c + 1) * S], ALU.is_equal, ALU.mult,
                                                 accum_out=ecol[:, c - 1:c])
                link(ins)
            ve.wait_ge(s["ups_ready"], 1)
            for hi in (NS, NS // 2):
                n = NS // 2
                v.tensor_tensor_scan(view(Pm, hi - 1, [[-1, n]]), view(U, hi, [[-1, n]]),
                                     view(OH, hi - 1, [[-1, n]]), 0.0, ALU.mult, ALU.add).then_inc(s["path_ready"], 1)
            for i, slot in enumerate(r_ptm):
                if slot.reader == dve:
                    h, c4 = i % CH, 1 - i // CH
                    empty(slot, v.tensor_copy(
                        PTs[:, h, :, :, 4 * c4:4 * c4 + 4].rearrange("p b s c -> p c s b"),
                        bank(slot)[0:CR, 0:4 * T].rearrange("p (c s b) -> p c s b", c=4, s=SEG)))

            def add_to_x(slots, before=None, ln=None):
                for i, slot in enumerate(slots):
                    if before is not None:
                        ve.wait_ge(free[dve], before[i].count)
                    x2 = X[:, 2 * i:2 * i + 2, :]
                    empty(slot, v.tensor_tensor(x2, bank(slot)[0:T, :].rearrange("p (b d) -> p b d", b=2), x2, ALU.add))
                    if ln and i % 2:
                        ln_stats(ln, i // 2, lambda b: ve.wait_ge(free[dve], slots[b // 2].count))
                        if i > 1:
                            ln_norm(ln, 0)
                            ln_norm(ln, 1)

            ve.wait_ge(full, r_vc[-1].n + 1)
            add_to_x(r_exp, ln=2)

            def norm_lo(n, parts):
                ve.wait_ge(full, ln_slots[n][-1].n + 1)
                for i, slot in enumerate(ln_slots[n]):
                    h, k = i // KD, i % KD
                    ve.wait_ge(free[act], slot.count)
                    v.tensor_tensor(parts[1][:, k, x_cols(h)], NT[:, k, x_cols(h)], parts[0][:, k, x_cols(h)],
                                    ALU.subtract).then_inc(s["norm_lo_ready"], 1)

            norm_lo(2, NTs0)

            def gates(n, slot, E):
                lg, p, c = gl[:, :, 0:E], gp[:, :, 0:E], cw[:, :, 0:E]
                src = bank(slot)[0:T, 0:B * E].rearrange("p (b e) -> p b e", b=B)
                if n == 0:
                    ve.wait_ge(s["aux_loaded"], 64)
                    ins = v.tensor_tensor(lg, src, view(brb, 0, [[0, B], [1, E]]), ALU.add)
                else:
                    ins = v.tensor_copy(lg, src)
                empty(slot, ins)
                ve.wait_ge(free[dve], slot.count)
                link(v.tensor_reduce(mx[:, 0, :], lg, AX_X, ALU.max))
                v.tensor_tensor(lg, lg, view(mx, 0, [[1, B], [0, E]]), ALU.subtract).then_inc(s["logits_ready"], 1)
                ve.wait_ge(s["logits_exp"], n + 1)
                link(v.tensor_reduce(rs[:, 0, :], p, AX_X, ALU.add))
                link(v.reciprocal(rs[:, 1, :], rs[:, 0, :]))
                link(v.tensor_tensor(p, p, view(rs, B, [[1, B], [0, E]]), ALU.mult))
                lo = (o_r0, o_ra)[n]
                more = big[0:T, lo:lo + B * E * E].rearrange("p (b e o) -> p b e o", b=B, e=E)
                same = big[0:T, lo + B * E * E:lo + 2 * B * E * E].rearrange("p (b e o) -> p b e o", b=B, e=E)
                p_o, p_e = view(gp, 0, [[E1, B], [0, E], [1, E]]), view(gp, 0, [[E1, B], [1, E], [0, E]])
                v.tensor_tensor(more, p_o, p_e, ALU.is_gt)
                link(v.tensor_tensor(same, p_o, p_e, ALU.is_equal))
                ve.wait_ge(s["tri_ready"], 1)
                link(v.tensor_tensor(same, same, view(junk, 0, [[0, B], [E1, E], [1, E]]), ALU.mult))
                link(v.tensor_tensor(more, more, same, ALU.add))
                rank = rk[:, 0:B * E].rearrange("p (b e) -> p b e", b=B)
                link(v.tensor_reduce(rank, more, AX_X, ALU.add))
                v.scalar_tensor_tensor(c, rank, 1.5, p, ALU.is_lt, ALU.mult).then_inc(s["gates_ready"], 1)
                ve.wait_ge(s["gates_ready"], n + 1)

            def hidden_lo(u):
                if u >= 2:
                    ve.wait_ge(full, r_dn0[u - 2][-1].n + 1)
                for m, slot in enumerate(r_up0[u]):
                    ve.wait_ge(free[act], slot.count)
                    v.tensor_tensor(hs[:, u % 2, 1, m], hf[:, m], hs[:, u % 2, 0, m], ALU.subtract)\
                        .then_inc(s["hidden_lo_ready"], 1)

            gates(0, r_g0[0], E0)
            hidden_lo(0)
            add_to_x(r_b2, r_exp)
            def turn_by_position(z):
                pairs = lambda a: a.rearrange("p (n two) -> p n two", two=2)
                t1, t2 = rope[:, 0, :], rope[:, 1, :]
                n = 2 * D // HD
                z3 = z.rearrange("p (n d) -> p n d", d=HD)
                link(v.tensor_tensor(t1.rearrange("p (n d) -> p n d", d=HD), z3, view(big, o_cs, [[0, n], [1, HD]]), ALU.mult))
                for odd in range(2):
                    link(v.tensor_tensor(
                        t2.rearrange("p (n i two) -> p n i two", i=HD // 2, two=2)[:, :, :, odd],
                        z.rearrange("p (n i two) -> p n i two", i=HD // 2, two=2)[:, :, :, 1 - odd],
                        view(big, o_cs + HD + odd, [[0, n], [2, HD // 2]]), ALU.mult))
                for odd in range(2):
                    link(v.tensor_tensor(pairs(z)[:, :, odd], pairs(t1)[:, :, odd], pairs(t2)[:, :, odd],
                                         (ALU.subtract, ALU.add)[odd]))
            ve.wait_ge(s["attn_w_loaded"], 96)
            ve.wait_ge(free[act], r_wt[-1].count)
            for k in range(KD):
                turn_by_position(wT[:, k, 0:2, :].rearrange("p w n -> p (w n)"))
            turn_by_position(bqkv[:, 0:2, :].rearrange("p w n -> p (w n)"))
            ve.sem_inc(s["rope_ready"], 1)

            def gated(slots, before, gate, first=0):
                for i, slot in enumerate(slots, first):
                    src = bank(slot)
                    ve.wait_ge(free[dve], before[i - first].count)
                    for j in range(2):
                        b = 2 * i + j
                        ins = v.scalar_tensor_tensor(X[:, b, :], src[0:T, j * D:(j + 1) * D], gate(b), X[:, b, :],
                                                     ALU.mult, ALU.add)
                    empty(slot, ins)

            for u in range(2 * E0):
                if u + 1 < 2 * E0:
                    hidden_lo(u + 1)
                e, h = u // 2, u % 2
                gated(r_dn0[u], r_dn0[u - 2] if e else r_b2[2 * h:2 * h + 2], lambda b: cw[:, b, e:e + 1], 2 * h)
                if e == E0 - 1:
                    ln_stats(3, h, lambda b: ve.wait_ge(free[dve], r_dn0[u][b // 2 % 2].count))
                    ln_norm(3, h)
            for i, slot in enumerate(r_qkv):
                b = i // 2
                w0_, w1_ = (0, 2) if i % 2 == 0 else (2, 3)
                cut = dict(w=w1_ - w0_, c=NH)
                empty(slot, v.tensor_tensor(
                    QKV[:, w0_:w1_, :, b, :],
                    bank(slot)[0:T, 0:(w1_ - w0_) * D].rearrange("p (w c d) -> p w c d", **cut),
                    big[0:T, o_bq + w0_ * D:o_bq + w1_ * D].rearrange("p (w c d) -> p w c d", **cut), ALU.add))
            for i, slot in enumerate(r_hT):
                if slot.reader == dve:
                    empty(slot, v.tensor_copy(turned(i), bank(slot)[:, 0:4 * T].rearrange("p (c t) -> p c t", c=4)))
            for n in range(NG + LN):
                if n < NG:
                    src = bank(r_s1[n])[0:T, 0:HT].rearrange("p (j n) -> p j n", j=4)
                    link(v.tensor_reduce(hm[:, n % NP, 0, :], src, AX_X, ALU.max))
                    v.tensor_scalar(hm[:, n % NP, 1, :], hm[:, n % NP, 0, :], -(HD ** -0.5), None, ALU.mult)\
                        .then_inc(s["heads_shifted"], 1)
                if n >= LN:
                    m = n - LN
                    ve.wait_ge(free[act], r_s1[m].count)
                    link(v.reciprocal(hm[:, m % NP, 3, :], hm[:, m % NP, 2, :]))
                    p = Px[:, m % NP].rearrange("p (j n) -> p j n", j=4)
                    v.tensor_tensor(p, p, view(rk, m % NP * 4 * HB + 3 * HB, [[1, HB], [0, T]]), ALU.mult)\
                        .then_inc(s["heads_normed"], 1)
            ve.wait_ge(s["bias_added"], 1)
            add_to_x(r_wo, ln=4)
            ve.wait_ge(s["norm_ready"], 5 * B)
            for n in range(B + 2):
                if n < B:
                    link(v.tensor_reduce(mx[:, 0, n:n + 1], bank(r_sc[n])[0:T, 0:S], AX_X, ALU.max))
                    v.tensor_scalar(mx[:, 1, n:n + 1], mx[:, 0, n:n + 1], -(D ** -0.5), None, ALU.mult)\
                        .then_inc(s["pc_shift"], 1)
                if n >= 2:
                    b = n - 2
                    ve.wait_ge(free[act], r_sc[b].count)
                    link(v.reciprocal(rs[:, 1, b:b + 1], rs[:, 0, b:b + 1]))
                    ve.wait_ge(s["bias_added"], 2)
                    empty(r_oc[b], v.scalar_tensor_tensor(X[:, b, :], bank(r_oc[b])[0:T, 0:D], rs[:, 1, b:b + 1],
                                                          X[:, b, :], ALU.mult, ALU.add))
                    if b % HB == HB - 1:
                        ln_stats(5, b // HB, lambda b: ve.wait_ge(free[dve], r_oc[b].count))
            ln_norm(5, 0)
            ln_norm(5, 1)
            norm_lo(5, NTs1)
            gates(1, r_g1[0], E1)
            for e in range(NX + 1):
                if e < NX:
                    for h in range(2):
                        slot = r_up1[e][2 * h + 1]
                        ve.wait_ge(free[act], r_up1[e][2 * h].count)
                        empty(slot, v.tensor_tensor(hx[:, e % 2, x_cols(h)], bank(slot)[:, 0:HT],
                                                    sg[:, e % 2, x_cols(h)], ALU.mult))
                    for h in range(2):
                        ve.wait_ge(s["hx_hi_ready"], 2 * e + h + 1)
                        v.tensor_tensor(hxs[1][:, e % 2, x_cols(h)], hx[:, e % 2, x_cols(h)],
                                        hxs[0][:, e % 2, x_cols(h)], ALU.subtract).then_inc(s["hx_lo_ready"], 1)
                if e:
                    f = e - 1
                    gated(r_dn1[f], r_dn1[f - 1] if f else [r_g1[0]] * 4,
                          lambda b: cw[:, b, f:f + 1] if f < E1 else 1.0)


_INS = ['x', 'ctx_1024', 'L0_attn_Wk', 'L0_attn_Wq', 'L0_attn_Wv', 'L0_ffn_Wr', 'L0_ffn_br', 'L0_ffn_W1',
        'L0_ffn_b1', 'L0_ffn_W2', 'L0_ffn_b2', 'L1_attn_wq', 'L1_attn_bq', 'L1_attn_wk', 'L1_attn_bk',
        'L1_attn_wv', 'L1_attn_bv', 'L1_attn_wo', 'L1_attn_bo', 'L1_attn_cos', 'L1_attn_sin',
        'L1_xattn_Wq', 'L1_xattn_bq', 'L1_xattn_Wk', 'L1_xattn_bk', 'L1_xattn_Wv', 'L1_xattn_bv',
        'L1_ffn_Wr', 'L1_ffn_Wg', 'L1_ffn_Wu', 'L1_ffn_Wd', 'L1_ffn_Sg', 'L1_ffn_Su', 'L1_ffn_Sd']


def kernel(**inputs):
    import numpy as _np
    import concourse.bacc as _bacc
    from concourse import mybir as _mybir
    from concourse.bass_utils import run_bass_kernel_spmd as _run

    nc = _bacc.Bacc("TRN2", target_bir_lowering=False, num_devices=1)
    arrays, args = {}, {}
    for name in _INS:
        a = _np.ascontiguousarray(inputs[name])
        arrays[f"in_{name}"] = a
        args[name] = nc.dram_tensor(f"in_{name}", a.shape, _mybir.dt.from_np(a.dtype), kind="ExternalInput").ap()
    shape = tuple(inputs["x"].shape)
    out = nc.dram_tensor("out_0", shape, _mybir.dt.from_np(_np.dtype("float32")), kind="ExternalOutput").ap()
    decoder_kernel(nc, args, out)
    r = _run(nc, [arrays], core_ids=[0])
    return r.results[0]["out_0"]
```

```python
from contextlib import ExitStack

import concourse.bass as bass
from concourse import mybir

F32 = mybir.dt.float32
F32R = mybir.dt.float32r
ALU = mybir.AluOpType
ACT = mybir.ActivationFunctionType
AX_X = mybir.AxisListType.X

BIG = 1e30
BANKS = 8
EPS = 1e-5
TINY = 1e-14


class Slot:

    def __init__(self, bank, before):
        self.bank, self.before = bank, before


class BankRing:

    def __init__(self):
        self.turns = list(range(BANKS))
        self.last = {}
        self.filled = 0
        self.counts = {}

    def open(self, bank):
        slot = Slot(bank, self.last.get(bank))
        self.last[bank] = slot
        return slot

    def close(self, slot, reader):
        self.counts[reader] = self.counts.get(reader, 0) + 1
        slot.n, slot.reader, slot.count = self.filled, reader, self.counts[reader]
        self.filled += 1
        return slot

    def take(self, *readers):
        out = []
        for reader in readers:
            self.turns.append(self.turns.pop(0))
            out.append(self.close(self.open(self.turns[-1]), reader))
        return out


def view(t, offset, dims, parts=None):
    x = t[:] if parts is None else t[parts[0]:parts[1]]
    return bass.AP(x.tensor, x.offset + offset, [x.ap[0]] + dims)


def rows_of(a, parts):
    n = a.shape[-1]
    return bass.AP(a.tensor, a.offset, [[0, parts], [1, n]])


def decoder_kernel(nc, A, out):
    B, T, D = A["x"].shape
    S = A["ctx_1024"].shape[1]
    KD = D // 128
    CH = 3
    CR = S // CH
    HB = B // 2
    HT = HB * T
    E0, F0 = A["L0_ffn_b1"].shape
    M0 = F0 // 128
    E1, _, F1 = A["L1_ffn_Wg"].shape
    NX = E1 + A["L1_ffn_Sg"].shape[1] // F1
    G = 4
    RC = -(-S // G)
    KC = 4
    STEPS = T // KC + G - 1
    NSLOT = STEPS * KC + 1
    SC = 8
    SEG = T // SC
    NH, HD = 16, D // 16
    assert B * HD == 128
    VZ = B * 128 + 112
    TC = 4 * CR
    NQ = B * CH // 4
    assert S == CH * CR and SEG * B == T and T * HD == NH * T and 2 * HB == B

    with ExitStack() as ctx:
        def sb(name, shape):
            return ctx.enter_context(nc.sbuf_tensor(name, shape, F32))

        def sem(name):
            return ctx.enter_context(nc.semaphore(name))

        ps = ctx.enter_context(nc.psum_tensor("ps", [128, BANKS, 512], F32))

        X = sb("X", [T, B, D])
        NT = sb("NT", [128, KD, B * T])
        BIGN = 26930
        large = (("N_r", B * D),
                 ("ctxT_r", 3 * 2048),
                 ("KcT_r", KD * B * S),
                 ("Vc_r", B * CH * D),
                 ("big", BIGN))
        with ExitStack() as plain:
            N_r, ctxT_r, KcT_r, Vc_r, big = (plain.enter_context(nc.sbuf_tensor(n, [128, c], F32)) for n, c in large)
        N_s, ctxT_s, KcT_s, Vc_s, big_s = (
            ctx.enter_context(nc.sbuf_tensor(n + "_split", [128, c], F32R)) for n, c in large)
        KcT = KcT_r[:, :].rearrange("p (k n) -> p k n", k=KD)
        ident = sb("ident", [128, 128])
        iota = sb("iota", [128, S + 1])
        ones = sb("ones", [128, T])
        stats = sb("stats", [T, B, 6])
        mv = sb("mv", [T, B, 2])
        veps = sb("veps", [T, B])
        mhalf = sb("mhalf", [T, B])
        tiny = sb("tiny", [T, 1])
        rstd = sb("rstd", [T, B])
        mx = sb("mx", [T, 2, B])
        rs = sb("rs", [T, 2, B])
        bb = sb("bb", [T, B])
        NB = E0 * M0 + 2 * KD
        brow = KcT[0:NB, 0, 0:128]
        bcol = sb("bcol", [128, NB])
        b1c = bcol[:, 0:E0 * M0].rearrange("p (e m) -> p e m", e=E0)
        bqk = bcol[:, E0 * M0:NB].rearrange("p (w k) -> p w k", w=2)
        brb = sb("brb", [T, E0])
        cw = sb("cw", [T, B, E1])
        einb = sb("einb", [B, SEG])
        esel = sb("esel", [B, T])
        ecol = sb("ecol", [T, SC])

        ctxT = ctxT_r[:, 0:KD * B * S].rearrange("p (k n) -> p k n", k=KD)
        N = N_r[0:T, :].rearrange("p (b d) -> p b d", b=B)
        Vc = Vc_r[0:CR, :].rearrange("p (b c d) -> p b c d", b=B, c=CH)

        def place(start, *sizes):
            offs, o = [], start
            for n in sizes:
                offs.append(o)
                o += n
            assert o <= BIGN, (start, sizes, o)
            return offs

        NS = SC * S
        RB = S + 2
        o_dsk, o_rs, o_rb = place(0, STEPS * KC * RC, NSLOT * (RC + 1), (SC + 1) * RB)
        ctxN0 = big[0:CR, 0:B * CH * D].rearrange("p (j d) -> p j d", d=D)
        o_w0, o_qk0, o_v0, o_p0, o_pt0, o_cm, o_sq = place(
            o_rs, 3 * KD * D, 2 * KD * B * T, B * D, B * T, B * T, T, 2 * KD * TC)
        w0 = big[:, o_w0:o_qk0].rearrange("p (w k n) -> p w k n", w=3, k=KD)
        qkT0 = big[:, o_qk0:o_v0].rearrange("p (w k n) -> p w k n", w=2, k=KD)
        V0 = big[0:T, o_v0:o_p0].rearrange("p (b d) -> p b d", b=B)
        P0 = big[0:T, o_p0:o_pt0].rearrange("p (b n) -> p b n", b=B)
        PT0 = big[0:T, o_pt0:o_cm].rearrange("p (b n) -> p b n", b=B)
        cmask = big[0:T, o_cm:o_cm + T]
        csq = big[:, o_sq:o_sq + 2 * KD * TC].rearrange("p (a k n) -> p a k n", a=2, k=KD)
        assert o_sq + 2 * KD * TC <= o_rb
        w0s = big_s[:, o_sq + 2 * KD * TC:o_sq + 2 * KD * (TC + 3 * D)].rearrange(
            "p (a w k n) -> p a w k n", a=2, w=3, k=KD)
        assert o_sq + 2 * KD * (TC + 3 * D) <= BIGN
        NTs_0 = [KcT_s[:, 128 + a * KD * B * T:128 + (a + 1) * KD * B * T].rearrange("p (k n) -> p k n", k=KD)
                 for a in range(2)]
        Dd = Vc_r[0:T, 0:B * S].rearrange("p (b n) -> p b n", b=B)
        aaB = Vc_r[0:T, B * S:2 * B * S].rearrange("p (b n) -> p b n", b=B)
        inv = big[0:T, o_rb:o_rb + B * S].rearrange("p (b n) -> p b n", b=B)
        Dsk = big[0:G * B, o_dsk:o_rs]
        RS = big[0:G * B, o_rs:o_rb].rearrange("p (q i) -> p q i", i=RC + 1)
        mtmp = sb("mtmp", [G * B, RC])
        Rb = big[0:T, o_rb:o_rb + (SC + 1) * RB].rearrange("p (c i) -> p c i", c=SC + 1)
        ctxN = big[0:CR, 0:B * CH * D].rearrange("p (b c d) -> p b c d", b=B, c=CH)
        o_m1, o_cc, o_tt = place(B * CH * D, NS, 2 * (S + 1), 2 * S)
        assert o_tt + 2 * S <= o_rs
        o_dl, o_u, o_pts = place(o_rs, 2 * NS, NS + 1, CH * B * T)
        assert o_pts + CH * B * T <= o_rb
        m1 = big[0:T, o_m1:o_m1 + NS]
        dl = big[0:T, o_dl:o_dl + 2 * NS].rearrange("p (a n) -> p a n", a=2)
        U = big[0:T, o_u:o_u + NS + 1]
        Ex = m1
        Cc = big[0:T, o_cc:o_cc + 2 * (S + 1)].rearrange("p (a i) -> p a i", a=2)
        Tt = big[0:T, o_tt:o_tt + 2 * S].rearrange("p (a i) -> p a i", a=2)
        Cw = big[0:B, 0:SEG * S].rearrange("p (s i) -> p s i", s=SEG)
        assert SEG * S <= B * CH * D
        T1 = big[0:T, o_rb:o_rb + NS]
        OH = big[0:T, o_rb:o_rb + NS]
        Pm = big[0:T, o_dl:o_dl + NS]
        PTs = big[0:CR, o_pts:o_pts + CH * B * T].rearrange("p (h b s c) -> p h b s c", h=CH, b=B, s=SEG)
        junk = sb("junk", [T, S])
        junk2 = junk[:, 0:D]
        wkv = N_r[:, 0:2 * KD * D].rearrange("p (w k n) -> p w k n", w=2, k=KD)
        NW0 = 2
        WN0 = KD * F0 + M0 * D
        W0f = ctxT_r[:, 0:NW0 * WN0].rearrange("p (r n) -> p r n", r=NW0)
        NP = 4
        (o_h0, o_qkv, o_vh, o_vz, o_px1, o_wn, o_wt, o_bq, o_cs, o_b2, o_ps, o_pq) = place(
            0, 2 * M0 * B * T, 3 * B * D, B * D, 2 * VZ, NP * HT, 2 * KD * D, 4 * KD * D,
            4 * D, 2 * HD, D, 4 * HT, 2 * HT)
        hs = big_s[:, o_h0:o_qkv].rearrange("p (r a m n) -> p r a m n", r=2, a=2, m=M0)
        W0s = big_s[:, o_qkv:o_qkv + 4 * WN0].rearrange("p (r a n) -> p r a n", r=2, a=2)
        W1s = W0s[:, :, :, 0:KD * F0].rearrange("p r a (k f) -> p r a k f", k=KD)
        W2s = W0s[:, :, :, KD * F0:WN0].rearrange("p r a (m d) -> p r a m d", m=M0)
        o_r0, o_hf = place(o_qkv + 4 * WN0, 3 * B * E0, M0 * HT)
        assert o_hf + M0 * HT <= o_wn
        hf = big[:, o_hf:o_hf + M0 * HT].rearrange("p (m n) -> p m n", m=M0)
        NTs0 = [ctxT_s[:, NW0 * WN0:NW0 * WN0 + KD * B * T].rearrange("p (k n) -> p k n", k=KD),
                N_s[:, 0:KD * B * T].rearrange("p (k n) -> p k n", k=KD)]
        NTs1 = [KcT_s[:, a * KD * B * T:(a + 1) * KD * B * T].rearrange("p (k n) -> p k n", k=KD) for a in range(2)]
        NTs3 = [big_s[:, o_h0 + a * KD * B * T:o_h0 + (a + 1) * KD * B * T].rearrange("p (k n) -> p k n", k=KD)
                for a in range(2)]
        wTs = ctxT_s[:, 0:2 * KD * 3 * D].rearrange("p (a k n) -> p a k n", a=2, k=KD)
        assert 2 * KD * 3 * D <= NW0 * WN0 and 2 * KD * B * T <= o_qkv - o_h0
        WXN = 2 * KD * F1 + D
        WXs = Vc_s[:, :].rearrange("p (r a n) -> p r a n", r=4, a=2)
        assert 4 * 2 * WXN == B * CH * D
        hxs = [KcT_s[:, 2 * KD * B * T:2 * KD * B * T + 2 * B * T].rearrange("p (r n) -> p r n", r=2),
               N_s[:, 0:2 * B * T].rearrange("p (r n) -> p r n", r=2)]
        QKV = big[0:T, o_qkv:o_qkv + 3 * B * D].rearrange("p (w c b d) -> p w c b d", w=3, c=NH, b=B)
        o_qt, o_km = place(o_h0, 3 * NH * T, 3 * HT)
        assert o_km + 3 * HT <= o_qkv
        QKVT = big[:, o_qt:o_km].rearrange("p (w n) -> p w n", w=3)
        Km = big[:, o_km:o_km + 3 * HT].rearrange("p (r n) -> p r n", r=3)
        Vh = big[0:T, o_vh:o_vz].rearrange("p (h n) -> p h n", h=NH)
        Vz = big[0:T, o_vz:o_px1].rearrange("p (r n) -> p r n", r=2)
        Px = big[0:T, o_px1:o_wn].rearrange("p (r n) -> p r n", r=NP)
        PxT = big[0:T, o_ps:o_ps + 3 * HT].rearrange("p (r n) -> p r n", r=3)
        wn = big[:, o_wn:o_wt].rearrange("p (w r n) -> p w r n", w=2, r=KD)
        wT = big[:, o_wt:o_bq].rearrange("p (k w n) -> p k w n", k=KD, w=4)
        bqkv = big[:, o_bq:o_cs].rearrange("p (w n) -> p w n", w=4)
        cs = big[:, o_cs:o_b2].rearrange("p (w n) -> p w n", w=2)
        b2s = big[0:E0, o_b2:o_ps]
        cwT = big[0:E0, o_pq:o_pq + B * T]
        wr0 = sb("wr0", [128, KD, E0])
        wr1 = sb("wr1", [128, KD, E1])
        rope = big[:, o_ps:o_ps + 4 * D].rearrange("p (a n) -> p a n", a=2)
        rk = sb("rk", [T, B * E1])
        gl = sb("gl", [T, B, E1])
        gp = sb("gp", [T, B, E1])
        hm = rk[:, 0:NP * 4 * HB].rearrange("p (r q j) -> p r q j", r=NP, q=4)
        bmask = iota[:, 0:B]
        (o_ra,) = place(o_qkv, 3 * B * E1)
        bvB = big[0:T, o_b2:o_b2 + D]
        o_qx, o_sx, o_px, o_ptx, o_wq = place(o_qkv, KD * B * T, 2 * S, 2 * S, 2 * CH * T, KD * D)
        assert o_wq + KD * D <= o_vh
        qxT = big[:, o_qx:o_sx].rearrange("p (k n) -> p k n", k=KD)
        Pc = big[0:T, o_px:o_px + 2 * S].rearrange("p (r n) -> p r n", r=2)
        PcT = big[0:CR, o_ptx:o_ptx + 2 * CH * T].rearrange("p (r h n) -> p r h n", r=2, h=CH)
        wq1 = big[:, o_wq:o_wq + KD * D].rearrange("p (k n) -> p k n", k=KD)
        NF = 8
        WXA = ctxT_r[:, :].rearrange("p (e n) -> p e n", e=NF)
        o_wx, o_sg, o_hx = place(o_vh, (NX - NF) * 768, 2 * B * T, 2 * B * T)
        WXB = big[:, o_wx:o_sg].rearrange("p (e n) -> p e n", e=NX - NF)
        sg = big[:, o_sg:o_hx].rearrange("p (r n) -> p r n", r=2)
        hx = big[:, o_hx:o_hx + 2 * B * T].rearrange("p (r n) -> p r n", r=2)

        def wx(e):
            return WXA[:, e, :] if e < NF else WXB[:, e - NF, :]

        def three(w):
            n = KD * F1
            return (w[:, 0:n].rearrange("p (k f) -> p k f", k=KD),
                    w[:, n:2 * n].rearrange("p (k f) -> p k f", k=KD), w[:, 2 * n:2 * n + D])

        WARM = ((20, 0), (0, 0), (0, 0), (8, 12), (8, 8), (0, 14))
        WARM_PATH = 28
        CTX_CUTS, AA_CUT = (6, 8), NQ - 2
        ring = BankRing()
        act, dve = "act", "dve"
        ln_slots = {}
        ln_slots[0] = ring.take(*[dve] * 4)
        r_qk0 = ring.take(*[act] * 8)
        r_v0 = ring.take(*[act] * 4)
        r_s0 = ring.take(dve, dve)
        r_ctx = ring.take(*[act] * CTX_CUTS[0])
        r_pt0 = ring.take(dve, dve)
        r_ctx += ring.take(*[act] * (CTX_CUTS[1] - CTX_CUTS[0]))
        r_pv0 = ring.take(*[dve] * 4)
        r_ctx += ring.take(*[act] * (KD * NQ - CTX_CUTS[1]))
        (r_bias,) = ring.take(act)
        r_aa = ring.take(*[act] * AA_CUT)
        ln_slots[1] = ring.take(*[act] * 4)
        r_aa += ring.take(*[act] * (NQ - AA_CUT))
        r_dist = ring.take(*[dve] * B)
        r_kc = ring.take(*[act] * (KD * NQ))
        r_vc = ring.take(*[act] * (B * CH // 2))
        r_e = ring.take(dve)
        r_ptm = ring.take(*[act, dve] * 3)
        r_exp = ring.take(*[dve] * 4)
        ln_slots[2] = ring.take(*[act] * 4)
        r_g0 = ring.take(dve)
        r_up0 = {}
        r_dn0 = {}
        r_up0[0] = ring.take(*[act] * M0)
        r_cwt = ring.take(act, act)
        r_b2 = ring.take(*[dve] * 4)
        r_wt = ring.take(*[act] * 2)
        for u in range(1, 2 * E0 + 1):
            if u < 2 * E0:
                r_up0[u] = ring.take(*[act] * M0)
            if u == 1:
                r_wt += ring.take(*[act] * 2)
            r_dn0[u - 1] = ring.take(dve, dve)
        ln_slots[3] = ring.take(*[dve] * 4)
        r_qkv = ring.take(*[dve] * (2 * B))
        r_hT = ring.take(*[act, dve] * 6)
        r_vh = ring.take(*[act] * 4)
        NG = 2 * NH
        LN, LT, LV = 2, 3, 4
        r_s1, r_pt1, r_o1 = {}, {}, {}
        ring.turns = [x for x in ring.turns if x < BANKS - 2]
        for n in range(NG + LV):
            if n < NG:
                (r_s1[n],) = ring.take(act)
            if LT <= n < NG + LT:
                (r_pt1[n - LT],) = ring.take(act)
            if n >= LV:
                h, g = (n - LV) // 2, (n - LV) % 2
                if h % 8 == 0:
                    r_o1[h // 8, g] = ring.open(BANKS - 2 + g)
                if h % 8 == 7:
                    ring.close(r_o1[h // 8, g], act)
        ring.turns += [BANKS - 2, BANKS - 1]
        r_wo = ring.take(*[dve] * 4)
        ln_slots[4] = ring.take(*[act] * 4)
        r_qx = ring.take(*[act] * 4)
        r_sc, r_ptc, r_oc = {}, {}, {}
        for n in range(B + 2):
            if n < B:
                (r_sc[n],) = ring.take(act)
            if 1 <= n <= B:
                (r_ptc[n - 1],) = ring.take(act)
            if n >= 2:
                (r_oc[n - 2],) = ring.take(dve)
        ln_slots[5] = ring.take(*[act] * 4)
        r_g1 = ring.take(dve)
        r_up1, r_dn1 = {}, {}
        for e in range(NX + 1):
            if e < NX:
                r_up1[e] = ring.take(act, dve, act, dve)
            if e:
                r_dn1[e - 1] = ring.take(*[dve] * 4)

        full = sem("banks_filled")
        free = {act: sem("banks_emptied_by_act"), dve: sem("banks_emptied_by_dve")}
        names = ("ident_ready", "consts_ready", "x_loaded0", "x_loaded1", "w0_loaded", "qkv_w_hi_ready", "qkv_w_lo_ready", "norm_hi_ready", "aux_loaded",
                 "stats_ready", "rstd_ready", "norm_ready", "p0_exp", "s0_ready",
                 "bb_ready", "csq_ready", "dsk_clear", "costs_clear", "ln_arg", "row_found", "column_marked", "column_marked_too", "inv_ready", "dist_ready",
                 "dist_moved", "last_rows_moved", "wkv_loaded",
                 "dtw_op", "costs_moved", "ctx_reloaded", "choices_ready", "exits_ready", "ups_ready",
                 "compose_done", "esel_ready", "path_ready", "logits_exp", "logits_ready",
                 "gates_ready", "attn_w_loaded", "wn_loaded0", "wn_loaded1",                  "heads_shifted", "heads_normed", "keys_masked", "values_spread", "values_used", "ffn_aux_loaded", "rope_ready", "bias_loaded", "bias_added", "router_loaded",                  "wq1_loaded", "pc_shift",                  "wxa_loaded", "wxb_loaded", "out_stored", "mask_ready",
                 "edge_ready", "norm_lo_ready", "w0_hi_ready", "w0_lo_ready", "hidden_lo_ready",
                 "wt_hi_ready", "wt_lo_ready", "wx_hi_ready", "wx_lo_ready", "hx_hi_ready", "hx_lo_ready", "dve_link", "act_link", "pool_link")
        s = {name: sem(name) for name in names}
        ctx_loaded = [sem(f"ctx_loaded{i}") for i in range(4)]
        cw_moved = [sem(f"segment_rows_moved{i}") for i in range(SEG)]
        w0x_loaded = [sem(f"expert_w_loaded{i}") for i in range(NW0)]

        block = ctx.enter_context(nc.Block())

        def halves():
            for h in range(2):
                yield h, range(h * HB, h * HB + HB)

        def x_cols(h):
            return slice(h * HT, (h + 1) * HT)

        def tok(b):
            return slice(b * T, (b + 1) * T)

        def skewed(b, g):
            return view(Dsk, g * KC * RC, [[RC, T], [1, min(RC, S - g * RC)]], (g * B + b, g * B + b + 1))

        def plain_rows(b, g):
            src = Dd[:, b, g * RC:min((g + 1) * RC, S)]
            return bass.AP(src.tensor, src.offset, [src.ap[0], [1, min(RC, S - g * RC)]])

        def step_of(seg, g):
            return 2 * seg + 1 + g

        COLS, SH = STEPS * KC, KC - 1

        def column_done(q):
            return 4 * q + (q < COLS) + min(q - 1, COLS - SH - 1) // SH

        def turned(i):
            w, cq = i // 4, i % 4
            return QKVT[:, w].rearrange("p (t c) -> p c t", c=NH)[:, 4 * cq:4 * cq + 4, :]

        @block.sync
        def _(sp):
            x_d = A["x"].rearrange("b t d -> t b d")
            sp.dma_start(X[:, 0:HB, :], x_d[:, 0:HB, :]).then_inc(s["x_loaded0"], 16)
            sp.dma_start(X[:, HB:B, :], x_d[:, HB:B, :]).then_inc(s["x_loaded1"], 16)
            for w, name in enumerate(("Wq", "Wk", "Wv")):
                sp.dma_start(w0[:, w], A["L0_attn_" + name].rearrange("(k p) n -> p k n", p=128))\
                    .then_inc(s["w0_loaded"], 16)
            c_d = A["ctx_1024"].rearrange("b (c p) d -> p b c d", c=CH)
            for i in range(4):
                sp.dma_start(ctxN0[:, 6 * i:6 * i + 6, :].rearrange("p (b c) d -> p b c d", c=CH),
                             c_d[:, 2 * i:2 * i + 2]).then_inc(ctx_loaded[i], 16)
            sp.wait_ge(s["dsk_clear"], 1)
            for q4 in range(B // 2):
                sp.wait_ge(s["dist_ready"], q4 + 1)
                for b in (2 * q4, 2 * q4 + 1):
                    for g in range(G - 1):
                        sp.dma_start(skewed(b, g), plain_rows(b, g)).then_inc(s["dist_moved"], 16)
            sp.wait_ge(s["edge_ready"], 1)
            for seg in range(SEG):
                for g in range(G):
                    n = min(RC, S - g * RC)
                    sp.wait_ge(s["dtw_op"], column_done(KC * min(step_of(seg, g) + 1, STEPS)))
                    q = seg * SC + g * KC
                    sp.dma_start(Rb[seg * B:(seg + 1) * B, :, 1 + g * RC:1 + g * RC + n],
                                 RS[g * B:(g + 1) * B, q:q + SC + 1, 1:1 + n]).then_inc(s["costs_moved"], 16)
            sp.wait_ge(s["compose_done"], 1)
            for seg in range(SEG - 1, 0, -1):
                sp.dma_start(Cw[:, seg, :], Cc[seg * B:(seg + 1) * B, (SC - 1) % 2, 1:S + 1])\
                    .then_inc(cw_moved[seg], 16)
            sp.wait_ge(s["esel_ready"], 1)
            for i in range(4):
                sp.dma_start(ctxN[:, 2 * i:2 * i + 2], c_d[:, 2 * i:2 * i + 2]).then_inc(s["ctx_reloaded"], 16)
            sp.wait_ge(free[dve], r_exp[-1].count)
            sp.dma_start(b2s, A["L0_ffn_b2"]).then_inc(s["ffn_aux_loaded"], 16)
            sp.dma_start(cs[:, 0, :], rows_of(A["L1_attn_cos"][T:T + 1, :], 128)).then_inc(s["attn_w_loaded"], 16)
            sp.dma_start(cs[:, 1, :], rows_of(A["L1_attn_sin"][T:T + 1, :], 128)).then_inc(s["attn_w_loaded"], 16)
            for w, name in enumerate(("bq", "bk", "bv", "bo")):
                sp.dma_start(bqkv[:, w, :], rows_of(A["L1_attn_" + name], 128)).then_inc(s["attn_w_loaded"], 16)
            for i, pair in enumerate((("wq", "wk"), ("wv", "wo"))):
                if i:
                    sp.wait_ge(full, r_wt[1].n + 1)
                for w, name in enumerate(pair):
                    sp.dma_start(wn[:, w], A["L1_attn_" + name].rearrange("(r p) n -> p r n", p=128))\
                        .then_inc(s[f"wn_loaded{i}"], 16)
            sp.wait_ge(full, r_b2[-1].n + 1)
            sp.dma_start(bvB, rows_of(A["L1_xattn_bv"], T)).then_inc(s["bias_loaded"], 16)
            def load_expert(e, name):
                g, u, d = three(wx(e))
                if e < E1:
                    srcs = (A["L1_ffn_Wg"][e], A["L1_ffn_Wu"][e], A["L1_ffn_Wd"][e])
                else:
                    f = slice((e - E1) * F1, (e - E1 + 1) * F1)
                    srcs = (A["L1_ffn_Sg"][:, f], A["L1_ffn_Su"][:, f], A["L1_ffn_Sd"][f, :])
                sp.dma_start(g, srcs[0].rearrange("(k p) f -> p k f", p=128)).then_inc(s[name], 16)
                sp.dma_start(u, srcs[1].rearrange("(k p) f -> p k f", p=128)).then_inc(s[name], 16)
                sp.dma_start(d, srcs[2]).then_inc(s[name], 16)
            sp.wait_ge(full, r_qkv[-1].n + 1)
            for e in range(NF):
                load_expert(e, "wxa_loaded")
            sp.wait_ge(full, r_vh[-1].n + 1)
            sp.dma_start(wq1, A["L1_xattn_Wq"].rearrange("(k p) n -> p k n", p=128)).then_inc(s["wq1_loaded"], 16)
            sp.wait_ge(free[dve], r_wo[-1].count)
            for e in range(NF, NX):
                load_expert(e, "wxb_loaded")
            for b in range(B):
                if b % 2 == 0:
                    sp.wait_ge(free[dve], r_dn1[NX - 1][b // 2].count)
                sp.dma_start(out[b], X[:, b, :]).then_inc(s["out_stored"], 16)
            sp.wait_ge(s["out_stored"], 16 * B)

        @block.gpsimd
        def _(pool):
            link_n = [0]

            def link(ins):
                link_n[0] += 1
                ins.then_inc(s["pool_link"], 1)
                pool.wait_ge(s["pool_link"], link_n[0])

            link(nc.gpsimd.memset(ident[:], 0.0))
            nc.gpsimd.affine_select(out=ident[:], in_=ident[:], compare_op=ALU.not_equal, fill=1.0, base=0,
                                    pattern=[[-1, 128]], channel_multiplier=1).then_inc(s["ident_ready"], 1)
            nc.gpsimd.memset(ones[:], 1.0).then_inc(s["consts_ready"], 1)
            nc.gpsimd.memset(tiny[:], TINY).then_inc(s["consts_ready"], 1)
            nc.gpsimd.memset(mhalf[:], -0.5).then_inc(s["consts_ready"], 1)
            link(nc.gpsimd.memset(cmask, 0.0))
            nc.gpsimd.affine_select(out=cmask, in_=cmask, compare_op=ALU.is_ge, fill=-BIG, base=0,
                                    pattern=[[-1, T]], channel_multiplier=1).then_inc(s["mask_ready"], 1)
            nc.gpsimd.iota(iota[:], pattern=[[1, S + 1]], base=-1, channel_multiplier=0,
                           allow_small_or_imprecise_dtypes=True).then_inc(s["consts_ready"], 1)
            link(nc.gpsimd.memset(esel[:], 1.0))
            nc.gpsimd.affine_select(out=esel[:].rearrange("p (s b) -> p s b", b=B),
                                    in_=esel[:].rearrange("p (s b) -> p s b", b=B),
                                    compare_op=ALU.is_equal, fill=0.0, base=0,
                                    pattern=[[0, SEG], [-1, B]], channel_multiplier=1).then_inc(s["consts_ready"], 1)
            def ln_root(n):
                for q4 in range(B // 2):
                    cols = slice(2 * q4, 2 * q4 + 2)
                    pool.wait_ge(s["stats_ready"], B // 2 * n + q4 + 1)
                    link(nc.gpsimd.tensor_scalar(veps[:, cols], mv[:, cols, 1], EPS, None, ALU.add))
                    nc.gpsimd.tensor_tensor(rstd[:, cols], veps[:, cols], mhalf[:, cols], ALU.pow)\
                        .then_inc(s["rstd_ready"], 1)

            ln_root(0)
            pool.dma_start(brow[0:E0 * M0, :], A["L0_ffn_b1"].rearrange("e (m p) -> (e m) p", p=128))\
                .then_inc(s["aux_loaded"], 16)
            for w, name in enumerate(("bq", "bk")):
                lo = E0 * M0 + w * KD
                pool.dma_start(brow[lo:lo + KD, :], A["L1_xattn_" + name].rearrange("(k p) -> k p", p=128))\
                    .then_inc(s["aux_loaded"], 16)
            pool.dma_start(brb[:], rows_of(A["L0_ffn_br"], T)).then_inc(s["aux_loaded"], 16)
            pool.dma_start(wr0[:], A["L0_ffn_Wr"].rearrange("(k p) e -> p k e", p=128)).then_inc(s["router_loaded"], 16)
            pool.dma_start(wr1[:], A["L1_ffn_Wr"].rearrange("(k p) e -> p k e", p=128)).then_inc(s["router_loaded"], 16)

            pool.wait_ge(full, r_ctx[-1].n + 1)
            lead = (G - 1) * KC * RC
            ln_root(1)
            nc.gpsimd.memset(view(Dsk, 0, [[T * RC, 2], [1, lead]]), BIG)
            nc.gpsimd.memset(view(Dsk, lead + S - (G - 1) * RC, [[RC, T - (G - 1) * KC]]), BIG).then_inc(s["dsk_clear"], 1)
            pool.wait_ge(full, ln_slots[1][-1].n + 1)
            pool.wait_ge(s["bb_ready"], 1)
            for w, name in enumerate(("Wk", "Wv")):
                pool.dma_start(wkv[:, w], A["L1_xattn_" + name].rearrange("(k p) n -> p k n", p=128))\
                    .then_inc(s["wkv_loaded"], 16)
            pool.wait_ge(free[dve], r_pv0[-1].count)
            pool.wait_ge(full, r_aa[-1].n + 1)
            link(nc.gpsimd.memset(RS[:, 0:KC + 1, :], BIG))
            nc.gpsimd.memset(RS[0:B, 0, 0:1], 0.0).then_inc(s["costs_clear"], 1)
            for q4 in range(B // 2):
                pool.wait_ge(s["dist_ready"], q4 + 1)
                for b in (2 * q4, 2 * q4 + 1):
                    pool.dma_start(skewed(b, G - 1), plain_rows(b, G - 1)).then_inc(s["last_rows_moved"], 16)
            nc.gpsimd.memset(Rb[:, :, 0:1], BIG).then_inc(s["edge_ready"], 1)
            def load_w0(e):
                r = e % NW0
                if e == 0:
                    pool.wait_ge(full, r_vc[-1].n + 1)
                if e >= NW0:
                    pool.wait_ge(s["w0_lo_ready"], e - NW0 + 1)
                pool.dma_start(W0f[:, r, 0:KD * F0].rearrange("p (k f) -> p k f", k=KD),
                               A["L0_ffn_W1"][e].rearrange("(k p) f -> p k f", p=128)).then_inc(w0x_loaded[r], 16)
                pool.dma_start(W0f[:, r, KD * F0:WN0].rearrange("p (m d) -> p m d", m=M0),
                               A["L0_ffn_W2"][e].rearrange("(m p) d -> p m d", p=128)).then_inc(w0x_loaded[r], 16)
            for e in range(NW0):
                load_w0(e)
            pool.wait_ge(s["choices_ready"], 2)
            rows = Ex.rearrange("p (c i) -> p c i", c=SC)
            nc.gpsimd.tensor_tensor(rows, dl[:, 0, :].rearrange("p (c i) -> p c i", c=SC),
                                    view(iota, 0, [[0, SC], [1, S]], (0, T)), ALU.mult)
            nc.gpsimd.tensor_tensor(T1.rearrange("p (c i) -> p c i", c=SC),
                                    dl[:, 1, :].rearrange("p (c i) -> p c i", c=SC),
                                    view(iota, 1, [[0, SC], [1, S]], (0, T)), ALU.mult).then_inc(s["exits_ready"], 1)
            pool.wait_ge(s["compose_done"], 1)
            link(nc.gpsimd.tensor_tensor(dl[:, 0, :], dl[:, 0, :], dl[:, 1, :], ALU.add))
            nc.gpsimd.tensor_scalar(U[:, 0:NS], dl[:, 0, :], -1.0, 1.0, ALU.mult, ALU.add)
            nc.gpsimd.memset(U[:, NS:NS + 1], 0.0).then_inc(s["ups_ready"], 1)
            pool.wait_ge(free[dve], r_e[0].count)
            for c in range(SC - 1, SC // 2 - 1, -1):
                if c < SC - 1:
                    pool.wait_ge(s["row_found"], SC - 1 - c)
                nc.gpsimd.tensor_scalar(OH[:, c * S:(c + 1) * S], iota[0:T, 1:S + 1], ecol[:, c:c + 1], None,
                                        ALU.is_equal).then_inc(s["column_marked"], 1)
            def w0_lo(e):
                pool.wait_ge(s["w0_hi_ready"], e + 1)
                nc.gpsimd.tensor_tensor(W0s[:, e % 2, 1], W0f[:, e % NW0], W0s[:, e % 2, 0], ALU.subtract)\
                    .then_inc(s["w0_lo_ready"], 1)
            ln_root(2)
            w0_lo(0)
            w0_lo(1)
            for e in range(2, E0):
                load_w0(e)
                w0_lo(e)
            pool.wait_ge(s["wt_hi_ready"], 1)
            nc.gpsimd.tensor_tensor(wTs[:, 1].rearrange("p k (w n) -> p k w n", w=3), wT[:, :, 0:3, :],
                                    wTs[:, 0].rearrange("p k (w n) -> p k w n", w=3), ALU.subtract)\
                .then_inc(s["wt_lo_ready"], 1)
            def add_bias(n, tile, offset):
                pool.wait_ge(s["norm_ready"], (n + 1) * B)
                nc.gpsimd.tensor_tensor(X[:, :, :], X[:, :, :], view(tile, offset, [[0, B], [1, D]], (0, T)), ALU.add)\
                    .then_inc(s["bias_added"], 1)

            ln_root(3)
            pool.wait_ge(full, r_dn0[2 * E0 - 1][-1].n + 1)
            pool.wait_ge(s["hidden_lo_ready"], 2 * M0 * E0)
            nc.gpsimd.memset(big[0:T, o_vz:o_px1], 0.0).then_inc(s["pool_link"], 1)
            link_n[0] += 1
            link(nc.gpsimd.memset(bmask, 1.0))
            link(nc.gpsimd.affine_select(out=bmask, in_=bmask, compare_op=ALU.is_ge, fill=0.0, base=0,
                                         pattern=[[-HD, B]], channel_multiplier=1))
            link(nc.gpsimd.affine_select(out=bmask, in_=bmask, compare_op=ALU.is_ge, fill=0.0, base=HD - 1,
                                         pattern=[[HD, B]], channel_multiplier=-1))

            pool.wait_ge(s["attn_w_loaded"], 96)
            add_bias(3, big, o_bq + 3 * D)
            pool.wait_ge(free[dve], r_hT[-1].count)
            pool.wait_ge(free[act], r_hT[-2].count)
            for n in range(NG + 2):
                h, g = n // 2, n % 2
                if n < NG:
                    if n >= 3:
                        pool.wait_ge(full, r_s1[n - 3].n + 1)
                    nc.gpsimd.tensor_tensor(Km[:, n % 3].rearrange("p (j n) -> p j n", j=HB),
                                            view(big, o_qt + (NH + h) * T, [[0, HB], [1, T]]),
                                            view(iota, g * HB, [[1, HB], [0, T]]), ALU.mult)\
                        .then_inc(s["keys_masked"], 1)
                if n >= 2 and g == 0:
                    h -= 1
                    if h == 0:
                        pool.wait_ge(free[act], r_vh[-1].count)
                    if h >= 2:
                        pool.wait_ge(s["values_used"], 2 * (h - 1))
                    dst = view(big, o_vz + h % 2 * VZ + 112, [[128, B], [1, HD]], (0, T))
                    nc.gpsimd.tensor_copy(dst, Vh[:, h].rearrange("p (b d) -> p b d", b=B)).then_inc(s["values_spread"], 1)
            ln_root(4)
            pool.wait_ge(s["bias_loaded"], 16)
            add_bias(4, big, o_b2)

            def wx_lo(e):
                pool.wait_ge(s["wx_hi_ready"], e + 1)
                nc.gpsimd.tensor_tensor(WXs[:, e % 4, 1], wx(e), WXs[:, e % 4, 0], ALU.subtract)\
                    .then_inc(s["wx_lo_ready"], 1)
            ln_root(5)
            for e in range(NX):
                wx_lo(e)

        @block.scalar
        def _(sc):
            link_n = [0]

            def link(ins):
                link_n[0] += 1
                ins.then_inc(s["act_link"], 1)
                sc.wait_ge(s["act_link"], link_n[0])

            def copy(slot, dst, src, func=ACT.Copy, **kw):
                sc.wait_ge(full, slot.n + 1)
                return nc.scalar.activation(dst, src, func, **kw).then_inc(free[act], 1)

            def bank(slot):
                return ps[:, slot.bank, :]

            def ln_hi(n, parts):
                for i, slot in enumerate(ln_slots[n]):
                    h, k = i // KD, i % KD
                    sc.wait_ge(full, slot.n + 1)
                    nc.scalar.activation(parts[0][:, k, x_cols(h)], bank(slot)[:, 0:HT], ACT.Copy)\
                        .then_inc(s["norm_hi_ready"], 1)

            def ln_turned(n, parts=None, halves=(0, 1)):
                for i, slot in enumerate(ln_slots[n]):
                    h, k = i // KD, i % KD
                    if h not in halves:
                        continue
                    if parts is not None:
                        sc.wait_ge(full, slot.n + 1)
                        nc.scalar.activation(parts[0][:, k, x_cols(h)], bank(slot)[:, 0:HT], ACT.Copy)
                    copy(slot, NT[:, k, x_cols(h)], bank(slot)[:, 0:HT])

            def ctx_turned(lo, hi):
                for i in range(lo, hi):
                    q, k = i // KD, i % KD
                    copy(r_ctx[i], ctxT[:, k, q * TC:(q + 1) * TC], bank(r_ctx[i])[:, 0:TC])

            sc.wait_ge(s["w0_loaded"], 48)
            nc.scalar.activation(w0s[:, 0], w0[:], ACT.Copy).then_inc(s["qkv_w_hi_ready"], 1)
            ln_hi(0, NTs_0)
            i = 0
            for w in range(2):
                for m in range(KD):
                    for h in range(2):
                        copy(r_qk0[i], qkT0[:, w, m, x_cols(h)], bank(r_qk0[i])[:, 0:HT])
                        i += 1
            for i, slot in enumerate(r_v0):
                copy(slot, V0[:, 2 * i:2 * i + 2, :], bank(slot)[0:T, :].rearrange("p (b d) -> p b d", b=2))
            for h, bs in halves():
                ctx_turned(2 * h, 2 * h + 2)
                sc.wait_ge(s["s0_ready"], h + 1)
                for b in bs:
                    nc.scalar.activation(P0[:, b, :], P0[:, b, :], ACT.Exp, bias=mx[:, 1, b:b + 1],
                                         accum_out=rs[:, 0, b:b + 1]).then_inc(s["p0_exp"], 1)
            nc.scalar.preload_act_table_set("natural_log_exp_and_others")
            ctx_turned(4, KD * NQ)
            copy(r_bias, bcol[:, :], bank(r_bias)[:, 0:NB])

            def squares(q):
                if q >= 2:
                    sc.wait_ge(full, r_aa[q - 2].n + 1)
                if q == 0:
                    sc.wait_ge(free[act], r_ctx[-1].count)
                nc.scalar.activation(csq[:, q % 2], ctxT[:, :, q * TC:(q + 1) * TC], ACT.Square)\
                    .then_inc(s["csq_ready"], 1)

            def norms(q):
                lo = q * TC
                copy(r_aa[q], Vc_r[0:T, B * S + lo:B * S + lo + TC], bank(r_aa[q])[0:T, 0:TC])
            squares(0)
            squares(1)
            for q in range(AA_CUT):
                norms(q)
                squares(q + 2)
            ln_turned(1)
            for q in range(AA_CUT, NQ):
                norms(q)
            sc.wait_ge(s["consts_ready"], 5)
            for q4 in range(B // 2):
                sl = slice(2 * q4, 2 * q4 + 2)
                sc.wait_ge(s["ln_arg"], q4 + 1)
                link(nc.scalar.activation(inv[:, sl, :], Dd[:, sl, :], ACT.Relu))
                link(nc.scalar.activation(inv[:, sl, :], inv[:, sl, :], ACT.Ln, bias=tiny[:, 0:1]))
                link(nc.scalar.activation(inv[:, sl, :], inv[:, sl, :], ACT.Exp, scale=-0.5))
                nc.scalar.activation(aaB[:, sl, :], inv[:, sl, :], ACT.Square).then_inc(s["inv_ready"], 1)
            sc.wait_ge(free[act], r_bias.count)
            i = 0
            for m in range(KD):
                for q in range(NQ):
                    copy(r_kc[i], KcT[:, m, q * TC:(q + 1) * TC], bank(r_kc[i])[:, 0:TC], ACT.Identity,
                         bias=bqk[:, 1, m:m + 1])
                    i += 1
            sc.wait_ge(s["dist_moved"], 16 * B * (G - 1))
            sc.wait_ge(s["last_rows_moved"], 16 * B)
            for i, slot in enumerate(r_vc):
                copy(slot, Vc_r[0:CR, 2 * i * D:(2 * i + 2) * D], bank(slot)[0:CR, :])
            for i, slot in enumerate(r_ptm):
                if slot.reader == act:
                    h, c4 = i % CH, 1 - i // CH
                    copy(slot, PTs[:, h, :, :, 4 * c4:4 * c4 + 4].rearrange("p b s c -> p c s b"),
                         bank(slot)[0:CR, 0:4 * T].rearrange("p (c s b) -> p c s b", c=4, s=SEG))

            def w0_hi(e):
                if e < 2:
                    sc.wait_ge(full, r_exp[-1].n + 1)
                else:
                    sc.wait_ge(full, r_dn0[2 * (e - 2) + 1][-1].n + 1)
                sc.wait_ge(w0x_loaded[e % NW0], 32 * (e // NW0 + 1))
                nc.scalar.activation(W0s[:, e % 2, 0], W0f[:, e % NW0], ACT.Copy).then_inc(s["w0_hi_ready"], 1)
            ln_turned(2, NTs0, (0,))
            w0_hi(0)
            ln_turned(2, NTs0, (1,))
            w0_hi(1)

            def up0(u):
                e, r = u // 2, u % 2
                if u >= 2:
                    sc.wait_ge(full, r_dn0[u - 2][-1].n + 1)
                for m, slot in enumerate(r_up0[u]):
                    sc.wait_ge(full, slot.n + 1)
                    nc.scalar.activation(hs[:, r, 0, m], bank(slot)[:, 0:HT], ACT.Relu, bias=b1c[:, e, m:m + 1])
                    if u:
                        sc.wait_ge(s["hidden_lo_ready"], M0 * (u - 1) + m + 1)
                    copy(slot, hf[:, m], bank(slot)[:, 0:HT], ACT.Relu, bias=b1c[:, e, m:m + 1])

            def gate_exp(n):
                E = (E0, E1)[n]
                sc.wait_ge(s["logits_ready"], n + 1)
                nc.scalar.activation(gp[:, :, 0:E], gl[:, :, 0:E], ACT.Exp).then_inc(s["logits_exp"], 1)
            gate_exp(0)
            up0(0)
            for i, slot in enumerate(r_cwt):
                copy(slot, cwT[:, x_cols(i)], bank(slot)[0:E0, 0:HT])
            def weights_turned(*which):
                for w in which:
                    copy(r_wt[w], wT[:, :, w, :], bank(r_wt[w]).rearrange("p (k n) -> p k n", k=KD))
            weights_turned(0, 1)
            for u in range(1, 2 * E0):
                up0(u)
                if u == 1:
                    weights_turned(2, 3)
                if u % 2 == 0 and u // 2 + 1 < E0:
                    w0_hi(u // 2 + 1)
                if u == 2 * E0 - 3:
                    sc.wait_ge(s["w0_lo_ready"], E0)
                    sc.wait_ge(s["rope_ready"], KD + 1)
                    nc.scalar.activation(wTs[:, 0].rearrange("p k (w n) -> p k w n", w=3), wT[:, :, 0:3, :], ACT.Copy)\
                        .then_inc(s["wt_hi_ready"], 1)
            ln_hi(3, NTs3)
            for i, slot in enumerate(r_hT):
                if slot.reader == act:
                    copy(slot, turned(i), bank(slot)[:, 0:4 * T].rearrange("p (c t) -> p c t", c=4))
            for i, slot in enumerate(r_vh):
                copy(slot, Vh[:, 4 * i:4 * i + 4, :], bank(slot)[0:T, :].rearrange("p (h n) -> p h n", h=4))
            for n in range(NG + LV):
                if n < NG:
                    sc.wait_ge(s["heads_shifted"], n + 1)
                    if n >= NP:
                        sc.wait_ge(full, r_pt1[n - NP].n + 1)
                    for j in range(HB):
                        ins = nc.scalar.activation(
                            Px[:, n % NP, j * T:(j + 1) * T], bank(r_s1[n])[0:T, j * T:(j + 1) * T], ACT.Exp,
                            bias=hm[:, n % NP, 1, j:j + 1], scale=HD ** -0.5, accum_out=hm[:, n % NP, 2, j:j + 1])
                    ins.then_inc(free[act], 1)
                if LT <= n < NG + LT:
                    m = n - LT
                    if m >= 3:
                        sc.wait_ge(s["values_used"], m - 2)
                    copy(r_pt1[m], PxT[:, m % 3], bank(r_pt1[m])[0:T, 0:HT])
                if n >= LV:
                    h, g = (n - LV) // 2, (n - LV) % 2
                    if h % 8 == 7:
                        copy(r_o1[h // 8, g], NT[:, h // 8, x_cols(g)], bank(r_o1[h // 8, g])[:, 0:HT])
            ln_turned(4)
            i = 0
            for m in range(KD):
                for h in range(2):
                    copy(r_qx[i], qxT[:, m, x_cols(h)], bank(r_qx[i])[:, 0:HT], ACT.Identity, bias=bqk[:, 0, m:m + 1])
                    i += 1
            for b in range(B + 1):
                if b < B:
                    sc.wait_ge(s["pc_shift"], b + 1)
                    if b >= 2:
                        sc.wait_ge(full, r_ptc[b - 2].n + 1)
                    copy(r_sc[b], Pc[:, b % 2], bank(r_sc[b])[0:T, 0:S], ACT.Exp,
                         bias=mx[:, 1, b:b + 1], scale=D ** -0.5, accum_out=rs[:, 0, b:b + 1])
                if b >= 1:
                    if b >= 3:
                        sc.wait_ge(full, r_oc[b - 3].n + 1)
                    copy(r_ptc[b - 1], PcT[:, (b - 1) % 2],
                         bank(r_ptc[b - 1])[0:CR, 0:CH * T].rearrange("p (h n) -> p h n", h=CH))
            def wx_hi(e):
                if e < 4:
                    sc.wait_ge(full, r_oc[B - 1].n + 1)
                else:
                    sc.wait_ge(full, r_dn1[e - 4][-1].n + 1)
                if e == 0:
                    sc.wait_ge(s["wxa_loaded"], 48 * NF)
                if e == NF:
                    sc.wait_ge(s["wxb_loaded"], 48 * (NX - NF))
                nc.scalar.activation(WXs[:, e % 4, 0], wx(e), ACT.Copy).then_inc(s["wx_hi_ready"], 1)
            wx_hi(0)
            wx_hi(1)
            ln_turned(5, NTs1)
            gate_exp(1)
            for e in range(NX):
                for h in range(2):
                    if e >= 2:
                        sc.wait_ge(free[dve], r_up1[e - 2][2 * h + 1].count)
                    copy(r_up1[e][2 * h], sg[:, e % 2, x_cols(h)], bank(r_up1[e][2 * h])[:, 0:HT], ACT.Silu)
                if e + 2 < NX:
                    wx_hi(e + 2)
                if e >= 2:
                    sc.wait_ge(full, r_dn1[e - 2][-1].n + 1)
                for h in range(2):
                    sc.wait_ge(free[dve], r_up1[e][2 * h + 1].count)
                    nc.scalar.activation(hxs[0][:, e % 2, x_cols(h)], hx[:, e % 2, x_cols(h)], ACT.Copy)\
                        .then_inc(s["hx_hi_ready"], 1)

        @block.tensor
        def _(pe):
            def bank(slot):
                if slot.before is not None:
                    pe.wait_ge(free[slot.before.reader], slot.before.count)
                return ps[:, slot.bank, :]

            def mm(dst, lhsT, rhs, first=True, last=True):
                return nc.tensor.matmul(dst, lhsT, rhs, start=first, stop=last)

            def turn(dst, src, n):
                return nc.tensor.transpose(dst, src, ident[0:n, 0:n])

            def filled(ins):
                ins.then_inc(full, 1)

            def keep_warm(slot, n):
                dst = bank(slot)
                for _ in range(n):
                    mm(dst[:, 0:128], ident[:, :], ident[:, :])

            def ln_turn(n):
                for i, slot in enumerate(ln_slots[n]):
                    h, k = i // KD, i % KD
                    if k == 0 and WARM[n][h]:
                        keep_warm(slot, WARM[n][h])
                    dst = bank(slot)
                    for j in range(HB):
                        if k == 0:
                            pe.wait_ge(s["norm_ready"], n * B + h * HB + j + 1)
                        m = turn(dst[:, j * T:(j + 1) * T], N[:, h * HB + j, k * 128:(k + 1) * 128], T)
                    filled(m)

            def wait_act(slot):
                pe.wait_ge(free[act], slot.count)

            def wait_dve(slot):
                pe.wait_ge(free[dve], slot.count)

            def split_mm(dst, lhsT, rhs, K):
                todo = [(a, b, k) for a, b in ((0, 0), (1, 0), (0, 1)) for k in range(K)]
                for i, (a, b, k) in enumerate(todo):
                    last = mm(dst, lhsT(a, k), rhs(b, k), i == 0, i == len(todo) - 1)
                return last

            def ctx_turn(lo, hi):
                for i in range(lo, hi):
                    q, k = i // KD, i % KD
                    for l in range(2 * q // 3, (4 * q + 3) // 6 + 1):
                        pe.wait_ge(ctx_loaded[l], 16)
                    dst = bank(r_ctx[i])
                    for j in range(4):
                        m = turn(dst[:, j * CR:(j + 1) * CR], ctxN0[:, 4 * q + j, k * 128:(k + 1) * 128], CR)
                    filled(m)

            pe.wait_ge(s["ident_ready"], 1)
            ln_turn(0)
            pe.wait_ge(s["qkv_w_lo_ready"], 1)
            i = 0
            for w in range(2):
                for m in range(KD):
                    for h in range(2):
                        wait_dve(ln_slots[0][KD * h + KD - 1])
                        filled(split_mm(bank(r_qk0[i])[:, 0:HT], lambda a, k: w0s[:, a, w, k, m * 128:(m + 1) * 128],
                                        lambda a, k: NTs_0[a][:, k, x_cols(h)], KD))
                        i += 1
            for i, slot in enumerate(r_v0):
                dst = bank(slot)
                for j in range(2):
                    last = split_mm(dst[0:T, j * D:(j + 1) * D], lambda a, k: NTs_0[a][:, k, tok(2 * i + j)],
                                    lambda a, k: w0s[:, a, 2, k, :], KD)
                filled(last)
            wait_act(r_qk0[-1])
            for i, slot in enumerate(r_s0):
                dst = bank(slot)
                for j in range(HB):
                    b = i * HB + j
                    for k in range(KD):
                        last = mm(dst[0:T, j * T:(j + 1) * T], qkT0[:, 0, k, tok(b)], qkT0[:, 1, k, tok(b)],
                                  k == 0, k == KD - 1)
                filled(last)
            def norms(lo, hi):
                for q in range(lo, hi):
                    pe.wait_ge(s["csq_ready"], q + 1)
                    dst = bank(r_aa[q])
                    for k in range(KD):
                        last = mm(dst[0:T, 0:TC], ones[:, :], csq[:, q % 2, k, :], k == 0, k == KD - 1)
                    filled(last)

            ctx_turn(0, CTX_CUTS[0])
            for i, slot in enumerate(r_pt0):
                pe.wait_ge(s["p0_exp"], (i + 1) * HB)
                dst = bank(slot)
                for j in range(HB):
                    last = turn(dst[0:T, j * T:(j + 1) * T], P0[:, i * HB + j, :], T)
                filled(last)
            ctx_turn(*CTX_CUTS)
            wait_act(r_v0[-1])
            for i, slot in enumerate(r_pv0):
                wait_dve(r_pt0[i // 2])
                dst = bank(slot)
                for j in range(2):
                    b = 2 * i + j
                    last = mm(dst[0:T, j * D:(j + 1) * D], PT0[:, b, :], V0[:, b, :])
                filled(last)
            ctx_turn(CTX_CUTS[1], KD * NQ)
            pe.wait_ge(s["aux_loaded"], 64)
            filled(turn(bank(r_bias)[:, 0:NB], brow, NB))
            pe.wait_ge(s["consts_ready"], 1)
            norms(0, AA_CUT)
            ln_turn(1)
            norms(AA_CUT, NQ)
            wait_act(ln_slots[1][-1])
            for b, slot in enumerate(r_dist):
                dst = bank(slot)[0:T, 0:S]
                for k in range(KD):
                    last = mm(dst, NT[:, k, tok(b)], ctxT[:, k, b * S:(b + 1) * S], k == 0, k == KD - 1)
                filled(last)
            pe.wait_ge(s["wkv_loaded"], 32)
            i = 0
            for m in range(KD):
                for q in range(NQ):
                    dst = bank(r_kc[i])[:, 0:TC]
                    for k in range(KD):
                        last = mm(dst, wkv[:, 0, k, m * 128:(m + 1) * 128], ctxT[:, k, q * TC:(q + 1) * TC],
                                  k == 0, k == KD - 1)
                    filled(last)
                    i += 1
            for i, slot in enumerate(r_vc):
                dst = bank(slot)
                for j in range(2):
                    lo = (2 * i + j) * CR
                    for k in range(KD):
                        last = mm(dst[0:CR, j * D:(j + 1) * D], ctxT[:, k, lo:lo + CR], wkv[:, 1, k, :],
                                  k == 0, k == KD - 1)
                filled(last)
            pe.wait_ge(s["esel_ready"], 1)
            filled(mm(bank(r_e[0])[0:T, 0:1], esel[:, :], ones[0:B, 0:1]))
            keep_warm(r_ptm[0], WARM_PATH)
            for i, slot in enumerate(r_ptm):
                h, c4 = i % CH, 1 - i // CH
                pe.wait_ge(s["path_ready"], 2 - c4)
                dst = bank(slot)
                for j in range(4):
                    c = 4 * c4 + j
                    last = turn(dst[0:CR, j * T:(j + 1) * T], Pm[:, c * S + h * CR:c * S + (h + 1) * CR], T)
                filled(last)
            pe.wait_ge(s["ctx_reloaded"], 64)
            wait_act(r_ptm[4])
            wait_dve(r_ptm[5])
            for i, slot in enumerate(r_exp):
                dst = bank(slot)
                for j in range(2):
                    b = 2 * i + j
                    for h in range(CH):
                        last = mm(dst[0:T, j * D:(j + 1) * D], PTs[:, h, b].rearrange("p s c -> p (s c)"),
                                  ctxN[:, b, h, :], h == 0, h == CH - 1)
                filled(last)
            ln_turn(2)

            def gate_logits(slot, wr, E):
                dst = bank(slot)
                for b in range(B):
                    for k in range(KD):
                        last = mm(dst[0:T, b * E:(b + 1) * E], NT[:, k, tok(b)], wr[:, k, :], k == 0, k == KD - 1)
                filled(last)

            def up0(u):
                e, h = u // 2, u % 2
                r = e % 2
                pe.wait_ge(s["w0_lo_ready"], e + 1)
                pe.wait_ge(s["norm_lo_ready"], KD * min(h + e + 1, 2))
                for m, slot in enumerate(r_up0[u]):
                    filled(split_mm(bank(slot)[:, 0:HT], lambda a, k: W1s[:, r, a, k, m * 128:(m + 1) * 128],
                                    lambda a, k: NTs0[a][:, k, x_cols(h)], KD))

            def down0(u):
                e, h = u // 2, u % 2
                pe.wait_ge(s["hidden_lo_ready"], M0 * (u + 1))
                for i, slot in enumerate(r_dn0[u]):
                    dst = bank(slot)
                    for j in range(2):
                        last = split_mm(dst[0:T, j * D:(j + 1) * D], lambda a, m: hs[:, u % 2, a, m, tok(2 * i + j)],
                                        lambda a, m: W2s[:, e % 2, a, m, :], M0)
                    filled(last)

            wait_act(ln_slots[2][-1])
            pe.wait_ge(s["router_loaded"], 32)
            gate_logits(r_g0[0], wr0, E0)
            up0(0)
            pe.wait_ge(s["gates_ready"], 1)
            for i, slot in enumerate(r_cwt):
                dst = bank(slot)
                for j in range(HB):
                    last = turn(dst[0:E0, j * T:(j + 1) * T], cw[:, i * HB + j, 0:E0], T)
                filled(last)
            wait_act(r_cwt[-1])
            pe.wait_ge(s["ffn_aux_loaded"], 16)
            for i, slot in enumerate(r_b2):
                dst = bank(slot)
                for j in range(2):
                    last = mm(dst[0:T, j * D:(j + 1) * D], cwT[:, tok(2 * i + j)], b2s[:, :])
                filled(last)
            def weights_turn(pair):
                pe.wait_ge(s[f"wn_loaded{pair}"], 32)
                for w in range(2):
                    slot = r_wt[2 * pair + w]
                    dst = bank(slot).rearrange("p (k n) -> p k n", k=KD)
                    for k in range(KD):
                        for r in range(KD):
                            last = turn(dst[:, k, r * 128:(r + 1) * 128], wn[:, w, r, k * 128:(k + 1) * 128], 128)
                    filled(last)

            weights_turn(0)
            for u in range(1, 2 * E0 + 1):
                if u < 2 * E0:
                    up0(u)
                if u == 1:
                    weights_turn(1)
                down0(u - 1)
            ln_turn(3)
            pe.wait_ge(s["wt_lo_ready"], 1)
            for i, slot in enumerate(r_qkv):
                b = i // 2
                cols = slice(0, 2 * D) if i % 2 == 0 else slice(2 * D, 3 * D)
                wait_dve(ln_slots[3][KD * (b // HB) + KD - 1])
                filled(split_mm(bank(slot)[0:T, 0:cols.stop - cols.start], lambda a, k: NTs3[a][:, k, tok(b)],
                                lambda a, k: wTs[:, a, k, cols], KD))
            wait_dve(r_qkv[-1])
            for i, slot in enumerate(r_hT):
                dst = bank(slot)
                for j in range(4):
                    lo = o_qkv + (4 * i + j) * 128
                    last = turn(dst[:, j * T:(j + 1) * T], big[0:T, lo:lo + 128], T)
                filled(last)
            wait_act(r_hT[-2])
            wait_dve(r_hT[-1])
            for i, slot in enumerate(r_vh):
                dst = bank(slot)
                for j in range(4):
                    h = 4 * i + j
                    last = turn(dst[0:T, j * 128:(j + 1) * 128], QKVT[:, 2, h * T:(h + 1) * T], 128)
                filled(last)
            for n in range(NG + LV):
                if n < NG:
                    h = n // 2
                    pe.wait_ge(s["keys_masked"], n + 1)
                    filled(mm(bank(r_s1[n])[0:T, 0:HT], QKVT[:, 0, h * T:(h + 1) * T], Km[:, n % 3]))
                if LT <= n < NG + LT:
                    m = n - LT
                    pe.wait_ge(s["heads_normed"], m + 1)
                    dst = bank(r_pt1[m])
                    for j in range(4):
                        last = turn(dst[0:T, j * T:(j + 1) * T], Px[:, m % NP, j * T:(j + 1) * T], T)
                    filled(last)
                if n >= LV:
                    m = n - LV
                    h, g = m // 2, m % 2
                    slot = r_o1[h // 8, g]
                    pe.wait_ge(s["values_spread"], h + 1)
                    wait_act(r_pt1[m])
                    dst = bank(slot) if h % 8 == 0 else ps[:, slot.bank, :]
                    for j in range(HB):
                        lo = 112 + (g * HB + j) * 128 - h % 8 * HD
                        last = mm(dst[:, j * T:(j + 1) * T], Vz[:, h % 2, lo:lo + 128], PxT[:, m % 3, j * T:(j + 1) * T],
                                  h % 8 == 0 and j == 0, h % 8 == 7 and j == HB - 1)
                    if h % 8 == 7:
                        filled(last)
                        pe.wait_ge(full, slot.n + 1)
                        pe.sem_inc(s["values_used"], 1)
                    else:
                        last.then_inc(s["values_used"], 1)
            wait_act(r_o1[1, 1])
            for i, slot in enumerate(r_wo):
                dst = bank(slot)
                for j in range(2):
                    for k in range(KD):
                        last = mm(dst[0:T, j * D:(j + 1) * D], NT[:, k, tok(2 * i + j)], wT[:, k, 3, :],
                                  k == 0, k == KD - 1)
                filled(last)
            ln_turn(4)
            wait_act(ln_slots[4][-1])
            pe.wait_ge(s["wq1_loaded"], 16)
            i = 0
            for m in range(KD):
                for h in range(2):
                    dst = bank(r_qx[i])[:, 0:HT]
                    for k in range(KD):
                        last = mm(dst, wq1[:, k, m * 128:(m + 1) * 128], NT[:, k, x_cols(h)], k == 0, k == KD - 1)
                    filled(last)
                    i += 1
            wait_act(r_qx[-1])
            for n in range(B + 2):
                if n < B:
                    dst = bank(r_sc[n])[0:T, 0:S]
                    for k in range(KD):
                        last = mm(dst, qxT[:, k, tok(n)], KcT[:, k, n * S:(n + 1) * S], k == 0, k == KD - 1)
                    filled(last)
                if 1 <= n <= B:
                    wait_act(r_sc[n - 1])
                    dst = bank(r_ptc[n - 1])
                    for h in range(CH):
                        last = turn(dst[0:CR, h * T:(h + 1) * T], Pc[:, (n - 1) % 2, h * CR:(h + 1) * CR], T)
                    filled(last)
                if n >= 2:
                    wait_act(r_ptc[n - 2])
                    dst = bank(r_oc[n - 2])[0:T, 0:D]
                    for h in range(CH):
                        last = mm(dst, PcT[:, n % 2, h, :], Vc[:, n - 2, h, :], h == 0, h == CH - 1)
                    filled(last)
            ln_turn(5)
            wait_act(ln_slots[5][-1])
            gate_logits(r_g1[0], wr1, E1)
            for e in range(NX + 1):
                if e < NX:
                    w = [three(WXs[:, e % 4, a]) for a in range(2)]
                    pe.wait_ge(s["wx_lo_ready"], e + 1)
                    if e == 0:
                        pe.wait_ge(s["norm_lo_ready"], 4 * KD)
                    for i, slot in enumerate(r_up1[e]):
                        h, gu = i // 2, i % 2
                        filled(split_mm(bank(slot)[:, 0:HT], lambda a, k: w[a][gu][:, k, :],
                                        lambda a, k: NTs1[a][:, k, x_cols(h)], KD))
                if e:
                    f = e - 1
                    w = [three(WXs[:, f % 4, a]) for a in range(2)]
                    for i, slot in enumerate(r_dn1[f]):
                        pe.wait_ge(s["hx_lo_ready"], 2 * f + i // 2 + 1)
                        dst = bank(slot)
                        for j in range(2):
                            last = split_mm(dst[0:T, j * D:(j + 1) * D],
                                            lambda a, k: hxs[a][:, f % 2, tok(2 * i + j)], lambda a, k: w[a][2], 1)
                        filled(last)

        @block.vector
        def _(ve):
            link_n = [0]

            def link(ins):
                link_n[0] += 1
                ins.then_inc(s["dve_link"], 1)
                ve.wait_ge(s["dve_link"], link_n[0])

            v = nc.vector

            def bank(slot):
                ve.wait_ge(full, slot.n + 1)
                return ps[:, slot.bank, :]

            def empty(slot, ins):
                ins.then_inc(free[dve], 1)

            def ln_stats(n, q4, x_ready):
                bs = (2 * q4, 2 * q4 + 1)
                for b in bs:
                    x_ready(b)
                    ins = v.bn_stats(stats[:, b, :], X[:, b, :])
                link(ins)
                for b in bs:
                    ins = v.bn_aggr(mv[:, b, :], stats[:, b, :])
                ins.then_inc(s["stats_ready"], 1)

            def ln_norm(n, q4):
                ve.wait_ge(s["rstd_ready"], B // 2 * n + q4 + 1)
                for b in (2 * q4, 2 * q4 + 1):
                    v.tensor_scalar(N[:, b, :], X[:, b, :], mv[:, b, 0:1], rstd[:, b:b + 1],
                                    ALU.subtract, ALU.mult).then_inc(s["norm_ready"], 1)

            def ln_step(n, q4, x_ready):
                ln_stats(n, q4, x_ready)
                if q4 >= 1:
                    ln_norm(n, q4 - 1)
                if q4 == B // 2 - 1:
                    ln_norm(n, q4)

            def norm_lo(n, parts):
                if n == 2:
                    ve.wait_ge(full, ln_slots[n][-1].n + 1)
                for i, slot in enumerate(ln_slots[n]):
                    h, k = i // KD, i % KD
                    ve.wait_ge(free[act], slot.count)
                    v.tensor_tensor(parts[1][:, k, x_cols(h)], NT[:, k, x_cols(h)], parts[0][:, k, x_cols(h)],
                                    ALU.subtract).then_inc(s["norm_lo_ready"], 1)

            def norm_lo_from_bank(n, parts):
                for i, slot in enumerate(ln_slots[n]):
                    h, k = i // KD, i % KD
                    ve.wait_ge(s["norm_hi_ready"], (2 * KD if n else 0) + i + 1)
                    empty(slot, v.tensor_tensor(parts[1][:, k, x_cols(h)], bank(slot)[:, 0:HT],
                                                parts[0][:, k, x_cols(h)], ALU.subtract))

            for q4 in range(B // 2):
                ln_step(0, q4, lambda b: ve.wait_ge(s[f"x_loaded{b // HB}"], 16))
            ve.wait_ge(s["qkv_w_hi_ready"], 1)
            v.tensor_tensor(w0s[:, 1], w0[:], w0s[:, 0], ALU.subtract).then_inc(s["qkv_w_lo_ready"], 1)
            norm_lo_from_bank(0, NTs_0)
            ve.wait_ge(s["mask_ready"], 1)
            for i, slot in enumerate(r_s0):
                bs = slice(i * HB, (i + 1) * HB)
                src = bank(slot)[0:T, 0:HT].rearrange("p (b n) -> p b n", b=HB)
                ins = v.scalar_tensor_tensor(P0[:, bs, :], src, D ** -0.5, view(cmask, 0, [[0, HB], [1, T]]),
                                             ALU.mult, ALU.add)
                empty(slot, ins)
                ve.wait_ge(free[dve], slot.count)
                link(v.tensor_reduce(mx[:, 0, bs], P0[:, bs, :], AX_X, ALU.max))
                v.tensor_scalar(mx[:, 1, bs], mx[:, 0, bs], -1.0, None, ALU.mult).then_inc(s["s0_ready"], 1)
            for i, slot in enumerate(r_pt0):
                bs = slice(i * HB, (i + 1) * HB)
                empty(slot, v.tensor_copy(PT0[:, bs, :], bank(slot)[0:T, 0:HT].rearrange("p (b n) -> p b n", b=HB)))
            ve.wait_ge(s["p0_exp"], B)
            link(v.reciprocal(rs[:, 1, :], rs[:, 0, :]))
            ve.wait_ge(full, ln_slots[0][-1].n + 1)
            for i, slot in enumerate(r_pv0):
                src = bank(slot)
                for j in range(2):
                    b = 2 * i + j
                    ins = v.scalar_tensor_tensor(X[:, b, :], src[0:T, j * D:(j + 1) * D], rs[:, 1, b:b + 1],
                                                 X[:, b, :], ALU.mult, ALU.add)
                empty(slot, ins)
                ln_step(1, i, lambda b: ve.wait_ge(free[dve], r_pv0[b // 2].count))
            def both_norms(q4):
                ve.wait_ge(free[act], r_aa[((2 * q4 + 2) * S - 1) // TC].count)
                for b in (2 * q4, 2 * q4 + 1):
                    ins = v.tensor_scalar(aaB[:, b, :], aaB[:, b, :], bb[:, b:b + 1], None, ALU.add)
                link(ins)

            def squares(q4):
                for b in (2 * q4, 2 * q4 + 1):
                    slot = r_dist[b]
                    empty(slot, v.scalar_tensor_tensor(Dd[:, b, :], bank(slot)[0:T, 0:S], -2.0, aaB[:, b, :],
                                                       ALU.mult, ALU.add))
                ve.wait_ge(free[dve], slot.count)
                ve.sem_inc(s["ln_arg"], 1)

            def roots(q4):
                hb = slice(2 * q4, 2 * q4 + 2)
                d, r, z = Dd[:, hb, :], inv[:, hb, :], aaB[:, hb, :]
                ve.wait_ge(s["inv_ready"], q4 + 1)
                link(v.scalar_tensor_tensor(z, z, -0.5, d, ALU.mult, ALU.mult))
                link(v.scalar_tensor_tensor(d, d, 0.0, r, ALU.max, ALU.mult))
                v.scalar_tensor_tensor(d, z, 1.5, d, ALU.add, ALU.mult).then_inc(s["dist_ready"], 1)

            for b in range(B):
                ve.wait_ge(s["norm_ready"], B + b + 1)
                ins = v.scalar_tensor_tensor(junk2, N[:, b, :], 1.0, N[:, b, :], ALU.mult, ALU.mult,
                                             accum_out=bb[:, b:b + 1])
                link(ins)
            ve.sem_inc(s["bb_ready"], 1)
            for q4 in range(B // 2):
                both_norms(q4)
            squares(0)
            for q4 in range(B // 2):
                if q4 + 1 < B // 2:
                    squares(q4 + 1)
                roots(q4)
            ve.wait_ge(s["costs_clear"], 1)
            ve.wait_ge(s["dist_moved"], 16 * B * (G - 1))
            ve.wait_ge(s["last_rows_moved"], 16 * B)
            ops = [0]

            def step(ins):
                ops[0] += 1
                ins.then_inc(s["dtw_op"], 1)
                return ops[0]

            def lesser(q, part, after):
                lo, hi = part
                ve.wait_ge(s["dtw_op"], after)
                return step(v.tensor_tensor(mtmp[:, lo:hi], RS[:, q - 1, lo:hi], RS[:, q - 1, lo + 1:hi + 1], ALU.min))

            def scan(q, part, after):
                lo, hi = part
                ve.wait_ge(s["dtw_op"], after)
                return step(v.tensor_tensor_scan(RS[:, q, lo + 1:hi + 1], mtmp[:, lo:hi],
                                                 Dsk[:, (q - 1) * RC + lo:(q - 1) * RC + hi],
                                                 RS[:, q, lo:lo + 1], ALU.min, ALU.add))

            upper, lower = (0, RC // 2), (RC // 2, RC)
            lu = step(v.tensor_tensor(mtmp[:, 0:RC // 2], RS[:, 0, 0:RC // 2], RS[:, 0, 1:RC // 2 + 1], ALU.min))
            for q in range(1, COLS + 1):
                su = scan(q, upper, lu)
                ll = lesser(q, lower, sl) if q > 1 else \
                    step(v.tensor_tensor(mtmp[:, RC // 2:RC], RS[:, 0, RC // 2:RC], RS[:, 0, RC // 2 + 1:RC + 1], ALU.min))
                if q < COLS:
                    lu = lesser(q + 1, upper, su)
                if q % SH == 1 and SH < q <= COLS - SH:
                    lu = step(v.stream_shuffle(RS[:, q + 1:q + 1 + SH, 0], RS[:, q - SH:q, RC],
                                               [(p - B) % 32 for p in range(32)]))
                sl = scan(q, lower, max(ll, su))
                assert sl == column_done(q)
            ve.wait_ge(s["dtw_op"], sl)
            link(v.memset(Cc[:, :, 0:1], 0.0))
            link(v.memset(einb[:, SEG - 1:SEG], float(S - 1)))
            ve.wait_ge(s["costs_moved"], 16 * SEG * G)
            cd, cu, cl = Rb[:, 0:SC, 0:S], Rb[:, 1:SC + 1, 0:S], Rb[:, 0:SC, 1:S + 1]
            m1v = m1.rearrange("p (c i) -> p c i", c=SC)
            diag, left = (dl[:, a, :].rearrange("p (c i) -> p c i", c=SC) for a in range(2))
            link(v.tensor_tensor(m1v, cu, cl, ALU.min))
            link(v.tensor_tensor(diag, cd, m1v, ALU.is_le))
            ve.sem_inc(s["choices_ready"], 1)
            link(v.tensor_tensor(m1v, cu, cd, ALU.min))
            v.tensor_tensor(left, cl, m1v, ALU.is_lt).then_inc(s["choices_ready"], 1)
            ve.wait_ge(s["choices_ready"], 2)
            for c in range(SC):
                w = view(iota, 0, [[1, 2], [1, S]], (0, T)) if c == 0 else \
                    view(big, o_cc + (c - 1) % 2 * (S + 1), [[1, 2], [1, S]], (0, T))
                link(v.tensor_tensor(Tt, dl[:, :, c * S:(c + 1) * S], w, ALU.mult))
                ins = v.tensor_tensor_scan(Cc[:, c % 2, 1:S + 1], Tt[:, 0, :], Tt[:, 1, :], 0.0, ALU.max, ALU.max)
                if c < SC - 1:
                    link(ins)
            ins.then_inc(s["compose_done"], 1)
            ve.wait_ge(s["compose_done"], 1)
            ve.wait_ge(s["exits_ready"], 1)
            for c in range(SC):
                ins = v.tensor_tensor_scan(Ex[:, c * S:(c + 1) * S], Ex[:, c * S:(c + 1) * S], T1[:, c * S:(c + 1) * S],
                                           0.0, ALU.max, ALU.max)
            link(ins)
            for g in range(SEG - 1, 0, -1):
                ve.wait_ge(cw_moved[g], 16)
                link(v.scalar_tensor_tensor(junk[0:B, :], iota[0:B, 1:S + 1], einb[:, g:g + 1], Cw[:, g, :],
                                            ALU.is_equal, ALU.mult, accum_out=einb[:, g - 1:g]))
            ve.wait_ge(s["consts_ready"], 5)
            v.tensor_tensor(esel[:].rearrange("p (s b) -> p s b", b=B), esel[:].rearrange("p (s b) -> p s b", b=B),
                            view(einb, 0, [[1, SEG], [0, B]]), ALU.mult).then_inc(s["esel_ready"], 1)
            empty(r_e[0], v.tensor_copy(ecol[:, SC - 1:SC], bank(r_e[0])[0:T, 0:1]))
            ve.wait_ge(free[dve], r_e[0].count)
            for c in range(SC - 1, 0, -1):
                v.scalar_tensor_tensor(junk[:, :], iota[0:T, 1:S + 1], ecol[:, c:c + 1],
                                       Ex[:, c * S:(c + 1) * S], ALU.is_equal, ALU.mult,
                                       accum_out=ecol[:, c - 1:c]).then_inc(s["row_found"], 1)
                ve.wait_ge(s["row_found"], SC - c)
            for c in range(SC // 2):
                v.tensor_scalar(OH[:, c * S:(c + 1) * S], iota[0:T, 1:S + 1], ecol[:, c:c + 1], None,
                                ALU.is_equal).then_inc(s["column_marked_too"], 1)
            ve.wait_ge(s["ups_ready"], 1)
            ve.wait_ge(s["column_marked"], SC // 2)
            for hi in (NS, NS // 2):
                n = NS // 2
                if hi == n:
                    ve.wait_ge(s["column_marked_too"], SC // 2)
                v.tensor_tensor_scan(view(Pm, hi - 1, [[-1, n]]), view(U, hi, [[-1, n]]),
                                     view(OH, hi - 1, [[-1, n]]), 0.0, ALU.mult, ALU.add).then_inc(s["path_ready"], 1)
            for i, slot in enumerate(r_ptm):
                if slot.reader == dve:
                    h, c4 = i % CH, 1 - i // CH
                    empty(slot, v.tensor_copy(
                        PTs[:, h, :, :, 4 * c4:4 * c4 + 4].rearrange("p b s c -> p c s b"),
                        bank(slot)[0:CR, 0:4 * T].rearrange("p (c s b) -> p c s b", c=4, s=SEG)))

            def add_to_x(slots, before=None, ln=None):
                for i, slot in enumerate(slots):
                    if before is not None:
                        ve.wait_ge(free[dve], before[i].count)
                    x2 = X[:, 2 * i:2 * i + 2, :]
                    empty(slot, v.tensor_tensor(x2, bank(slot)[0:T, :].rearrange("p (b d) -> p b d", b=2), x2, ALU.add))
                    if ln:
                        ln_step(ln, i, lambda b: ve.wait_ge(free[dve], slots[b // 2].count))

            ve.wait_ge(full, r_vc[-1].n + 1)
            add_to_x(r_exp, ln=2)

            norm_lo(2, NTs0)

            def gates(n, slot, E):
                lg, p, c = gl[:, :, 0:E], gp[:, :, 0:E], cw[:, :, 0:E]
                src = bank(slot)[0:T, 0:B * E].rearrange("p (b e) -> p b e", b=B)
                if n == 0:
                    ve.wait_ge(s["aux_loaded"], 64)
                    ins = v.tensor_tensor(lg, src, view(brb, 0, [[0, B], [1, E]]), ALU.add)
                else:
                    ins = v.tensor_copy(lg, src)
                empty(slot, ins)
                ve.wait_ge(free[dve], slot.count)
                link(v.tensor_reduce(mx[:, 0, :], lg, AX_X, ALU.max))
                v.tensor_tensor(lg, lg, view(mx, 0, [[1, B], [0, E]]), ALU.subtract).then_inc(s["logits_ready"], 1)
                ve.wait_ge(s["logits_exp"], n + 1)
                link(v.tensor_reduce(rs[:, 0, :], p, AX_X, ALU.add))
                link(v.reciprocal(rs[:, 1, :], rs[:, 0, :]))
                link(v.tensor_tensor(p, p, view(rs, B, [[1, B], [0, E]]), ALU.mult))
                lo = (o_r0, o_ra)[n]
                w, first, p2 = (big[0:T, lo + a * B * E:lo + (a + 1) * B * E].rearrange("p (b e) -> p b e", b=B)
                                for a in range(3))
                falling = view(iota, 64, [[0, B], [-1, E]], (0, T))
                most = view(mx, 0, [[1, B], [0, E]])
                for pick, q in ((first, p), (w, p2)):
                    link(v.tensor_reduce(mx[:, 0, :], q, AX_X, ALU.max))
                    link(v.tensor_tensor(w, q, most, ALU.is_equal))
                    link(v.tensor_tensor(w, w, falling, ALU.mult))
                    link(v.tensor_reduce(mx[:, 0, :], w, AX_X, ALU.max))
                    link(v.tensor_tensor(pick, w, most, ALU.is_equal))
                    if q is p:
                        link(v.scalar_tensor_tensor(p2, first, -2.0, p, ALU.mult, ALU.add))
                link(v.tensor_tensor(w, w, first, ALU.add))
                v.tensor_tensor(c, w, p, ALU.mult).then_inc(s["gates_ready"], 1)
                ve.wait_ge(s["gates_ready"], n + 1)

            def hidden_lo(u):
                if u >= 2:
                    ve.wait_ge(full, r_dn0[u - 2][-1].n + 1)
                for m, slot in enumerate(r_up0[u]):
                    ve.wait_ge(free[act], slot.count)
                    v.tensor_tensor(hs[:, u % 2, 1, m], hf[:, m], hs[:, u % 2, 0, m], ALU.subtract)\
                        .then_inc(s["hidden_lo_ready"], 1)

            gates(0, r_g0[0], E0)
            hidden_lo(0)
            add_to_x(r_b2, r_exp)
            def turn_by_position(z):
                pairs = lambda a: a.rearrange("p (n two) -> p n two", two=2)
                t1, t2 = rope[:, 0, :], rope[:, 1, :]
                n = 2 * D // HD
                z3 = z.rearrange("p (n d) -> p n d", d=HD)
                link(v.tensor_tensor(t1.rearrange("p (n d) -> p n d", d=HD), z3, view(big, o_cs, [[0, n], [1, HD]]), ALU.mult))
                for odd in range(2):
                    link(v.tensor_tensor(
                        t2.rearrange("p (n i two) -> p n i two", i=HD // 2, two=2)[:, :, :, odd],
                        z.rearrange("p (n i two) -> p n i two", i=HD // 2, two=2)[:, :, :, 1 - odd],
                        view(big, o_cs + HD + odd, [[0, n], [2, HD // 2]]), ALU.mult))
                for odd in range(2):
                    link(v.tensor_tensor(pairs(z)[:, :, odd], pairs(t1)[:, :, odd], pairs(t2)[:, :, odd],
                                         (ALU.subtract, ALU.add)[odd]))

            def turn_weights(part):
                ve.wait_ge(s["attn_w_loaded"], 96)
                ve.wait_ge(free[act], r_wt[-1].count)
                z = wT[:, part, 0:2, :] if part < KD else bqkv[:, 0:2, :]
                turn_by_position(z.rearrange("p w n -> p (w n)"))
                ve.sem_inc(s["rope_ready"], 1)

            def gated(slots, before, gate, first=0, ln=None):
                for i, slot in enumerate(slots, first):
                    src = bank(slot)
                    ve.wait_ge(free[dve], before[i - first].count)
                    for j in range(2):
                        b = 2 * i + j
                        ins = v.scalar_tensor_tensor(X[:, b, :], src[0:T, j * D:(j + 1) * D], gate(b), X[:, b, :],
                                                     ALU.mult, ALU.add)
                    empty(slot, ins)
                    if ln:
                        ln_step(ln, i, lambda b: ve.wait_ge(free[dve], slot.count))

            for u in range(2 * E0):
                if u + 1 < 2 * E0:
                    hidden_lo(u + 1)
                e, h = u // 2, u % 2
                gated(r_dn0[u], r_dn0[u - 2] if e else r_b2[2 * h:2 * h + 2], lambda b: cw[:, b, e:e + 1], 2 * h,
                      ln=3 if e == E0 - 1 else None)
                if 1 <= u <= 3:
                    turn_weights(u - 1)
            norm_lo_from_bank(3, NTs3)
            for i, slot in enumerate(r_qkv):
                b = i // 2
                w0_, w1_ = (0, 2) if i % 2 == 0 else (2, 3)
                cut = dict(w=w1_ - w0_, c=NH)
                empty(slot, v.tensor_tensor(
                    QKV[:, w0_:w1_, :, b, :],
                    bank(slot)[0:T, 0:(w1_ - w0_) * D].rearrange("p (w c d) -> p w c d", **cut),
                    big[0:T, o_bq + w0_ * D:o_bq + w1_ * D].rearrange("p (w c d) -> p w c d", **cut), ALU.add))
            for i, slot in enumerate(r_hT):
                if slot.reader == dve:
                    empty(slot, v.tensor_copy(turned(i), bank(slot)[:, 0:4 * T].rearrange("p (c t) -> p c t", c=4)))
            for n in range(NG + LN):
                if n < NG:
                    src = bank(r_s1[n])[0:T, 0:HT].rearrange("p (j n) -> p j n", j=4)
                    link(v.tensor_reduce(hm[:, n % NP, 0, :], src, AX_X, ALU.max))
                    v.tensor_scalar(hm[:, n % NP, 1, :], hm[:, n % NP, 0, :], -(HD ** -0.5), None, ALU.mult)\
                        .then_inc(s["heads_shifted"], 1)
                if n >= LN:
                    m = n - LN
                    ve.wait_ge(free[act], r_s1[m].count)
                    link(v.reciprocal(hm[:, m % NP, 3, :], hm[:, m % NP, 2, :]))
                    p = Px[:, m % NP].rearrange("p (j n) -> p j n", j=4)
                    v.tensor_tensor(p, p, view(rk, m % NP * 4 * HB + 3 * HB, [[1, HB], [0, T]]), ALU.mult)\
                        .then_inc(s["heads_normed"], 1)
            ve.wait_ge(s["bias_added"], 1)
            add_to_x(r_wo, ln=4)
            ve.wait_ge(s["norm_ready"], 5 * B)
            for n in range(B + 2):
                if n < B:
                    link(v.tensor_reduce(mx[:, 0, n:n + 1], bank(r_sc[n])[0:T, 0:S], AX_X, ALU.max))
                    v.tensor_scalar(mx[:, 1, n:n + 1], mx[:, 0, n:n + 1], -(D ** -0.5), None, ALU.mult)\
                        .then_inc(s["pc_shift"], 1)
                if n >= 2:
                    b = n - 2
                    ve.wait_ge(free[act], r_sc[b].count)
                    link(v.reciprocal(rs[:, 1, b:b + 1], rs[:, 0, b:b + 1]))
                    ve.wait_ge(s["bias_added"], 2)
                    empty(r_oc[b], v.scalar_tensor_tensor(X[:, b, :], bank(r_oc[b])[0:T, 0:D], rs[:, 1, b:b + 1],
                                                          X[:, b, :], ALU.mult, ALU.add))
                    if b % 2:
                        ln_step(5, b // 2, lambda b: ve.wait_ge(free[dve], r_oc[b].count))
            norm_lo(5, NTs1)
            gates(1, r_g1[0], E1)
            for e in range(NX + 1):
                if e < NX:
                    for h in range(2):
                        slot = r_up1[e][2 * h + 1]
                        ve.wait_ge(free[act], r_up1[e][2 * h].count)
                        empty(slot, v.tensor_tensor(hx[:, e % 2, x_cols(h)], bank(slot)[:, 0:HT],
                                                    sg[:, e % 2, x_cols(h)], ALU.mult))
                    for h in range(2):
                        ve.wait_ge(s["hx_hi_ready"], 2 * e + h + 1)
                        v.tensor_tensor(hxs[1][:, e % 2, x_cols(h)], hx[:, e % 2, x_cols(h)],
                                        hxs[0][:, e % 2, x_cols(h)], ALU.subtract).then_inc(s["hx_lo_ready"], 1)
                if e:
                    f = e - 1
                    gated(r_dn1[f], r_dn1[f - 1] if f else [r_g1[0]] * 4,
                          lambda b: cw[:, b, f:f + 1] if f < E1 else 1.0)


_INS = ['x', 'ctx_1024', 'L0_attn_Wk', 'L0_attn_Wq', 'L0_attn_Wv', 'L0_ffn_Wr', 'L0_ffn_br', 'L0_ffn_W1',
        'L0_ffn_b1', 'L0_ffn_W2', 'L0_ffn_b2', 'L1_attn_wq', 'L1_attn_bq', 'L1_attn_wk', 'L1_attn_bk',
        'L1_attn_wv', 'L1_attn_bv', 'L1_attn_wo', 'L1_attn_bo', 'L1_attn_cos', 'L1_attn_sin',
        'L1_xattn_Wq', 'L1_xattn_bq', 'L1_xattn_Wk', 'L1_xattn_bk', 'L1_xattn_Wv', 'L1_xattn_bv',
        'L1_ffn_Wr', 'L1_ffn_Wg', 'L1_ffn_Wu', 'L1_ffn_Wd', 'L1_ffn_Sg', 'L1_ffn_Su', 'L1_ffn_Sd']


def kernel(**inputs):
    import numpy as _np
    import concourse.bacc as _bacc
    from concourse import mybir as _mybir
    from concourse.bass_utils import run_bass_kernel_spmd as _run

    nc = _bacc.Bacc("TRN2", target_bir_lowering=False, num_devices=1)
    arrays, args = {}, {}
    for name in _INS:
        a = _np.ascontiguousarray(inputs[name])
        arrays[f"in_{name}"] = a
        args[name] = nc.dram_tensor(f"in_{name}", a.shape, _mybir.dt.from_np(a.dtype), kind="ExternalInput").ap()
    shape = tuple(inputs["x"].shape)
    out = nc.dram_tensor("out_0", shape, _mybir.dt.from_np(_np.dtype("float32")), kind="ExternalOutput").ap()
    decoder_kernel(nc, args, out)
    r = _run(nc, [arrays], core_ids=[0])
    return r.results[0]["out_0"]
```
